# Optimizing a Trainium2 kernel written in Bass

```python
import numpy as np
import jax
import jax.numpy as jnp

def _softmax(x, axis=-1):
    return jax.nn.softmax(x, axis=axis)

def _gelu(x):
    return jax.nn.gelu(x, approximate=True)

def _silu(x):
    return jax.nn.silu(x)

def _sigmoid(x):
    return jax.nn.sigmoid(x)

def _layernorm(x, axis=-1, eps=1e-05):
    m = jnp.mean(x, axis=axis, keepdims=True)
    v = jnp.var(x, axis=axis, keepdims=True)
    return (x - m) / jnp.sqrt(v + eps)

def _scatter_add(tgt, idx, src, axis=0):
    return tgt.at[idx].add(src)

def _segment_sum(src, seg, n):
    return jax.ops.segment_sum(src, seg, n)
kernel_name = 'mk_prb_d1_jaxref_r8_bfec6f'

def setup_inputs(seed: int=0):
    np.random.seed(seed)
    _w = jnp.asarray

    def _L0_attn_setup():
        import jax, jax.numpy as jnp
        import numpy as np
        HEAD_NUM = 16
        NEG_BIG = 1000000.0
        key = jax.random.key(seed)
        ks = jax.random.split(key, 5)
        E = 128
        B, S = (1, 512)
        x = jax.random.normal(ks[0], (B, S, E), dtype=jnp.float32)
        W1 = jax.random.normal(ks[1], (E, 3 * E), dtype=jnp.float32) * (1.0 / np.sqrt(E))
        b1 = jax.random.normal(ks[2], (3 * E,), dtype=jnp.float32) * 0.02
        Wp = jax.random.normal(ks[3], (E, E), dtype=jnp.float32) * (1.0 / np.sqrt(E))
        bp = jax.random.normal(ks[4], (E,), dtype=jnp.float32) * 0.02
        return {'x': x, 'W1': W1, 'b1': b1, 'Wp': Wp, 'bp': bp}
    _L0_attn_in = _L0_attn_setup()

    def _L0_ffn_setup():
        import jax, jax.numpy as jnp
        import numpy as np
        TOP_K = 2

        def _ffn(x, gw, uw, dw):
            return jax.nn.silu(x @ gw.T) * (x @ uw.T) @ dw.T
        key = jax.random.key(seed)
        ks = jax.random.split(key, 8)
        w = lambda k, shape: jax.random.normal(k, shape, jnp.float32) * 0.02
        return dict(x=jax.random.normal(ks[0], (4, 256, 128), jnp.float32), gate_w=w(ks[1], (8, 128)), expert_gate=w(ks[2], (8, 352, 128)), expert_up=w(ks[3], (8, 352, 128)), expert_down=w(ks[4], (8, 128, 352)), shared_gate=w(ks[5], (352, 128)), shared_up=w(ks[6], (352, 128)), shared_down=w(ks[7], (128, 352)))
    _L0_ffn_in = _L0_ffn_setup()
    _d = {'L0_attn_x': _L0_attn_in['x'], 'L0_attn_W1': _L0_attn_in['W1'], 'L0_attn_b1': _L0_attn_in['b1'], 'L0_attn_Wp': _L0_attn_in['Wp'], 'L0_attn_bp': _L0_attn_in['bp'], 'L0_ffn_gate_w': _L0_ffn_in['gate_w'], 'L0_ffn_expert_gate': _L0_ffn_in['expert_gate'], 'L0_ffn_expert_up': _L0_ffn_in['expert_up'], 'L0_ffn_expert_down': _L0_ffn_in['expert_down'], 'L0_ffn_shared_gate': _L0_ffn_in['shared_gate'], 'L0_ffn_shared_up': _L0_ffn_in['shared_up'], 'L0_ffn_shared_down': _L0_ffn_in['shared_down']}
    _x0 = _d['L0_attn_x']
    _d['L0_attn_x'] = jax.random.normal(jax.random.fold_in(jax.random.key(seed), 1), (8, 512, 128), dtype=_x0.dtype)
    del _x0
    return _d

def reference(L0_attn_x, L0_attn_W1, L0_attn_b1, L0_attn_Wp, L0_attn_bp, L0_ffn_gate_w, L0_ffn_expert_gate, L0_ffn_expert_up, L0_ffn_expert_down, L0_ffn_shared_gate, L0_ffn_shared_up, L0_ffn_shared_down):

    def _L0_attn_ref(x, W1, b1, Wp, bp):
        import jax, jax.numpy as jnp
        import numpy as np
        HEAD_NUM = 16
        NEG_BIG = 1000000.0
        B, S, E = x.shape
        H = HEAD_NUM
        d = E // H
        dk = jnp.asarray(d, x.dtype) ** 0.5
        h = x @ W1 + b1
        h = jnp.swapaxes(h.reshape(B, S, H, 3 * d), 1, 2)
        q, k, v = (h[..., :d], h[..., d:2 * d], h[..., 2 * d:])
        w = jnp.einsum('bhqd,bhkd->bhqk', q, k) / dk
        mask = jnp.tril(jnp.ones((S, S), dtype=x.dtype))
        w = jax.nn.softmax(w * mask - (1.0 - mask) * NEG_BIG, axis=-1)
        a = jnp.einsum('bhqk,bhkd->bhqd', w, v)
        a = jnp.swapaxes(a, 1, 2).reshape(B, S, E)
        return a @ Wp + bp

    def _L0_ffn_ref(x, gate_w, expert_gate, expert_up, expert_down, shared_gate, shared_up, shared_down):
        import jax, jax.numpy as jnp
        import numpy as np
        TOP_K = 2

        def _ffn(x, gw, uw, dw):
            return jax.nn.silu(x @ gw.T) * (x @ uw.T) @ dw.T
        B, S, H = x.shape
        xf = x.reshape(-1, H)
        T = xf.shape[0]
        E = expert_gate.shape[0]
        shared = _ffn(xf, shared_gate, shared_up, shared_down)
        logits = xf @ gate_w.T
        probs = jax.nn.softmax(logits, axis=-1)
        topw, topi = jax.lax.top_k(probs, TOP_K)
        topw = topw / (topw.sum(-1, keepdims=True) + 1e-20)
        comb = jnp.zeros((T, E), xf.dtype).at[jnp.arange(T)[:, None], topi].add(topw)

        def body(acc, ws):
            gw, uw, dw, wcol = ws
            return (acc + _ffn(xf, gw, uw, dw) * wcol[:, None], None)
        routed, _ = jax.lax.scan(body, jnp.zeros_like(xf), (expert_gate, expert_up, expert_down, comb.T))
        return (shared + routed).reshape(B, S, H)
    x = L0_attn_x
    xn = _layernorm(x, axis=-1)
    x = x + _L0_attn_ref(xn, L0_attn_W1, L0_attn_b1, L0_attn_Wp, L0_attn_bp) + _L0_ffn_ref(xn, L0_ffn_gate_w, L0_ffn_expert_gate, L0_ffn_expert_up, L0_ffn_expert_down, L0_ffn_shared_gate, L0_ffn_shared_up, L0_ffn_shared_down)
    return x

_drawn_inputs = setup_inputs


def setup_inputs(seed=0):
    import zlib

    import numpy as np

    out = dict(_drawn_inputs(seed))
    spreads = {}
    factors = {'L0_attn_b1': 17.328,
     'L0_attn_bp': 15.961,
     'L0_ffn_gate_w': 8.0,
     'L0_ffn_expert_gate': 8.0,
     'L0_ffn_expert_up': 8.0,
     'L0_ffn_expert_down': 8.0,
     'L0_ffn_shared_gate': 5.959,
     'L0_ffn_shared_up': 5.908,
     'L0_ffn_shared_down': 5.937}
    for name, (base, spread) in spreads.items():
        noise = np.random.default_rng([zlib.crc32(name.encode()), seed]).standard_normal(out[name].shape)
        drawn = base * np.exp(spread * noise) if base else spread * noise
        out[name] = jnp.asarray(drawn.astype(out[name].dtype))
    for name, factor in factors.items():
        out[name] = (out[name] * factor).astype(out[name].dtype)
    return out
```

```python
from contextlib import ExitStack

import concourse.bass as bass
from concourse import mybir

F32 = mybir.dt.float32
F32R = mybir.dt.float32r
BF16 = mybir.dt.bfloat16
I32 = mybir.dt.int32
U32 = mybir.dt.uint32
ALU = mybir.AluOpType
ACT = mybir.ActivationFunctionType
AX = mybir.AxisListType

P = 128
E = 128
B, S = 8, 512
T = B * S
H = 16
D = E // H
NB = S // P
NT = T // P
HG = 4
NG = H // HG
NX = 8
F = 352
FC = 3
FR = F - 2 * P
NTILE = 2 * T // P + NX
SLOTS = NTILE * P
SCALE = float(D) ** -0.5
EPS = 1e-5
NEG = -1.0e30

NU = 11
ST_KB = [0, 0, 0, 0, 1, 1, 1, 1, 2, 2, 3]
ST_HEADS = [[0], [1], [2], [3], [0], [1], [2], [3], [0, 1], [2, 3], [0, 1, 2, 3]]
MX_QB = [0, 1, 1, 2, 2, 2, 2, 3, 3, 3, 3]
MX_HEADS = [[0, 1, 2, 3], [0, 1], [2, 3], [0], [1], [2], [3], [0], [1], [2], [3]]
UB = NG * NU
LAG = 6
AV_UNITS = [4, 8, 10, 11]
PRIME_EXP, PRIME_AV, PRIME_AO, PRIME_T, PRIME_F, PRIME_ATOUT = 2, 4, 2, 2, 1, 1


def attention_moe_kernel(nc, x, w_qkv, b_qkv, w_out, b_out, gate_w, e_gu, e_down, s_gu, s_down, out):
    x_tok = x.rearrange("b s e -> (b s) e")
    out_tok = out.rearrange("b s e -> (b s) e")

    q_rows = nc.dram_tensor("q_rows", [H, 3 * D, S], F32, kind="Internal").ap()
    k_rows = nc.dram_tensor("k_rows", [H, 3 * D, S], F32, kind="Internal").ap()
    sorted_x = nc.dram_tensor("sorted_x", [SLOTS, E], F32, kind="Internal").ap()
    sorted_y = nc.dram_tensor("sorted_y", [SLOTS, E], F32, kind="Internal").ap()
    att_T = nc.dram_tensor("att_T", [B, E, S], F32, kind="Internal").ap()

    with ExitStack() as ctx:
        def sb(name, shape, dt=F32, stack=ctx):
            return stack.enter_context(nc.sbuf_tensor(name, shape, dt))

        def ps(name, shape, stack=ctx):
            return stack.enter_context(nc.psum_tensor(name, shape, F32))

        def sem(name):
            return ctx.enter_context(nc.semaphore(name))

        ident = sb("ident", [P, P])
        ident_bf = sb("ident_bf", [P, P], BF16)
        mask_kq = sb("mask_kq", [P, HG, P], BF16)
        mask_qk = sb("mask_qk", [P, HG, P], BF16)
        before = sb("before", [P, P], BF16)
        ones_bf = sb("ones_bf", [P, P], BF16)
        expert_no = sb("expert_no", [P, NX])
        ones_f = sb("ones_f", [P, NX])
        tile_start = sb("tile_start", [1, NTILE])
        not_first = sb("not_first", [P, NX, NT])
        wqkv = sb("wqkv", [P, 3, E])
        bqkv = sb("bqkv", [P, 3])
        wout = sb("wout", [P, E])
        bout = sb("bout", [P, 1])
        gate = sb("gate", [P, NX])
        sgu = sb("sgu", [P, 2, F])
        sdn = sb("sdn", [P, FC, E])
        edn = sb("edn", [P, NX, FC, E])
        xnT = sb("xnT", [P, T])
        xn_rows = sb("xn_rows", [P, NT, E])
        slot_idx = sb("slot_idx", [P, 2, NT], U32)
        topw = sb("topw", [P, 2, NT])
        tile_expert = sb("tile_expert", [1, NTILE], I32)
        lg = sb("lg", [P, NT, NX])
        bn = sb("bn", [P, NT, 6])
        mv = sb("mv", [P, NT, 2])
        var = sb("var", [P, NT])
        std = sb("std", [P, NT])
        rstd = sb("rstd", [P, NT])
        newton = sb("newton", [P, NT])
        primed = sb("primed", [P, 10])

        attn = ExitStack()
        q_bd = [sb(f"q_bd{i}", [P, H, S], F32R, attn) for i in range(2)]
        k_st = [sb(f"k_st{i}", [P, NG, S], F32R, attn) for i in range(2)]
        v32 = [sb(f"v32_{i}", [P, NB, H, 32], F32, attn) for i in range(2)]
        q_hi = sb("q_hi", [P, S], F32R, attn)
        q_lo = sb("q_lo", [P, S], F32R, attn)
        k_hi = sb("k_hi", [P, S], F32R, attn)
        k_lo = sb("k_lo", [P, S], F32R, attn)
        vT = sb("vT", [P, S], F32, attn)
        av_sb = [sb(f"av_sb{i}", [P, S], F32, attn) for i in range(2)]
        a_tok = sb("a_tok", [P, NB, E], F32, attn)
        a_T = sb("a_T", [P, S], F32, attn)
        neg_max = sb("neg_max", [P, NG, NB, HG], F32, attn)
        m_row = [sb(f"m_row{g}", [HG, S], F32R, attn) for g in range(NG)]
        one_row = sb("one_row", [1, S], F32, attn)
        inv_sum = sb("inv_sum", [P, NB * HG], F32, attn)

        first = ExitStack()
        x_all = sb("x_all", [P, NT, E], F32, first)
        xn_blk = sb("xn_blk", [P, NB, E], F32, first)
        lgT = sb("lgT", [P, S], F32, first)
        first.close()
        route = ExitStack()
        logit = sb("logit", [P, NT, NX], F32, route)
        prob = sb("prob", [P, NT, NX], F32, route)
        cand = sb("cand", [P, NT, NX], F32, route)
        hot = [sb(f"hot{c}", [P, NT, NX], F32, route) for c in range(2)]
        hot_bf = sb("hot_bf", [P, NT, NX], BF16, route)
        total = sb("total", [P, NX, NT], F32, route)
        incl = sb("incl", [P, NX, NT], F32, route)
        slot = sb("slot", [P, NT, NX], F32, route)
        best = [sb(f"best{c}", [P, NT], F32, route) for c in range(2)]
        pick = sb("pick", [P, NT], F32, route)
        slot_f = sb("slot_f", [P, 2, NT], F32, route)
        rows_i = sb("rows_i", [P, NX], I32, route)
        rows_f = sb("rows_f", [P, NX], F32, route)
        end_row = sb("end_row", [P, NX], F32, route)
        base_row = sb("base_row", [P, NX], F32, route)
        past = sb("past", [1, NTILE, NX], F32, route)
        tile_f = sb("tile_f", [1, NTILE], F32, route)
        route.close()
        probs = sb("probs", [P, NU, S], F32, attn)
        attn.close()

        ffn = ExitStack()
        egu = sb("egu", [P, NX, 2, F], F32, ffn)
        sb("fill_q_bd0", [P, H * S - NX * 2 * F], F32, ffn)
        xg = [sb(f"xg{i}", [P, E], F32, ffn) for i in range(2)]
        xgT = [sb(f"xgT{i}", [P, P], F32, ffn) for i in range(2)]
        sg = [sb(f"sg{i}", [P, F], F32, ffn) for i in range(2)]
        hid = [sb(f"hid{i}", [P, F], F32, ffn) for i in range(2)]
        hidT = [sb(f"hidT{i}", [P, FC, P], F32, ffn) for i in range(2)]
        y_sb = [sb(f"y_sb{i}", [P, E], F32, ffn) for i in range(2)]
        s_sig = sb("s_sig", [P, FC, S], F32, ffn)
        s_hid = [sb(f"s_hid{i}", [P, FC, S], F32, ffn) for i in range(2)]
        a_in = [sb(f"a_in{i}", [P, S], F32, ffn) for i in range(2)]
        x_in = [sb(f"x_in{i}", [P, NB, E], F32, ffn) for i in range(2)]
        resT = sb("resT", [P, S], F32, ffn)
        picked = [sb(f"picked{i}", [P, 2, NB, E], F32, ffn) for i in range(2)]
        o_sb = [sb(f"o_sb{i}", [P, NB, E], F32, ffn) for i in range(2)]
        ffn.close()

        bank = [ps(f"bank{i}", [P, S]) for i in range(8)]
        st_bank, mx_bank, av_bank = bank[0:2], bank[2:4], bank[4:6]
        row_bank, proj_bank = bank[6], bank[7]

        x_ld = [sem(f"x_ld{i}") for i in range(4)]
        w_early, w_late, egu_ld = sem("w_early"), sem("w_late"), sem("egu_ld")
        consts, cleared, ones_set = sem("consts"), sem("cleared"), sem("ones_set")
        fill_done = sem("fill_done")
        stats, std_done = sem("stats"), sem("std_done")
        vec_p, stat1, o_half = sem("vec_p"), sem("stat1"), sem("o_half")
        xn_done, xn_kept, xT_done, xnT_done = sem("xn_done"), sem("xn_kept"), sem("xT_done"), sem("xnT_done")
        lgT_mm, lgT_done, lg_done = sem("lgT_mm"), sem("lgT_done"), sem("lg_done")
        lg_kept, lgT_clear = sem("lg_kept"), sem("lgT_clear")
        vec = sem("vec")
        z_ready, e_ready, hot_ready, count_done, routed = (sem(n) for n in ("z_ready", "e_ready", "hot_ready", "count_done", "routed"))
        scattered = sem("scattered")
        qk_proj, qk_hi, qk_split = sem("qk_proj"), sem("qk_hi"), sem("qk_split")
        q_wr, k_wr = sem("q_wr"), sem("k_wr")
        qk_ld = [sem(f"qk_ld{i}") for i in range(2)]
        v_proj, v_biased, v_tr, v_ready = sem("v_proj"), sem("v_biased"), sem("v_tr"), sem("v_ready")
        mx_done, red_done, m_tr, m_ready = sem("mx_done"), sem("red_done"), sem("m_tr"), sem("m_ready")
        m_ld = [sem(f"m_ld{g}") for g in range(NG)]
        st_done, exp_done, av_done, av_out, t_done = (sem(n) for n in ("st_done", "exp_done", "av_done", "av_out", "t_done"))
        inv_done, a_done, f_done, aT_ready, aT_st = (sem(n) for n in ("inv_done", "a_done", "f_done", "aT_ready", "aT_st"))
        xg_ld = [sem(f"xg_ld{i}") for i in range(2)]
        y_st = [sem(f"y_st{i}") for i in range(2)]
        xg_tr, xgT_done, gu_done, sg_done, hid_done, hid_tr, hidT_done, y_done, y_out = (
            sem(n) for n in ("xg_tr", "xgT_done", "gu_done", "sg_done", "hid_done", "hid_tr", "hidT_done", "y_done", "y_out"))
        sgu_done, ssig_done, shid_done, res_done, res_out, o_tr, o_base, o_sum = (
            sem(n) for n in ("sgu_done", "ssig_done", "shid_done", "res_done", "res_out", "o_tr", "o_base", "o_sum"))
        s_ld = [sem(f"s_ld{i}") for i in range(2)]
        got = [sem(f"got{i}") for i in range(2)]
        o_st = [sem(f"o_st{i}") for i in range(2)]

        block = ctx.enter_context(nc.Block())

        def half(b, par, n):
            if isinstance(b, int):
                return (b + n) // 2
            return b[1] + (par + n) // 2

        def at(b, par):
            return b if isinstance(b, int) else 2 * b[1] + par

        def loads_of(t):
            return t.rearrange("(g j) r t -> j r g t", j=HG)

        @block.sync
        def _(sp):
            for i in range(4):
                n = T // 4
                sp.dma_start(x_all[:, i * NT // 4:(i + 1) * NT // 4, :],
                             x_tok[i * n:(i + 1) * n, :].rearrange("(n p) e -> p n e", p=P)).then_inc(x_ld[i], 16)
                if i == 0:
                    sp.dma_start(gate[:], gate_w).then_inc(w_early, 16)
                    sp.dma_start(wqkv[:], w_qkv).then_inc(w_early, 16)
                    sp.dma_start(bqkv[:], b_qkv).then_inc(w_early, 16)
            sp.dma_start(wout[:], w_out).then_inc(w_late, 16)
            sp.dma_start(bout[:], b_out).then_inc(w_late, 16)
            sp.dma_start(sgu[:], s_gu).then_inc(w_late, 16)
            sp.dma_start(sdn[:, 0:2, :], s_down[0:2 * P, :].rearrange("(c f) e -> f c e", f=P)).then_inc(w_late, 16)
            sp.dma_start(sdn[0:FR, 2, :], s_down[2 * P:F, :]).then_inc(w_late, 16)
            for c in range(2):
                sp.dma_start(edn[:, :, c, :], e_down[:, c * P:(c + 1) * P, :].rearrange("x f e -> f x e")).then_inc(w_late, 16)
            sp.dma_start(edn[0:FR, :, 2, :], e_down[:, 2 * P:F, :].rearrange("x f e -> f x e")).then_inc(w_late, 16)

            sp.wait_ge(cleared, 3)
            sp.wait_ge(ones_set, 1)
            for par in range(2):
                for g in range(NG):
                    sp.dma_start(k_st[par][P - 1:P, g, :].bitcast(F32), one_row[:]).then_inc(w_late, 16)

            def split_rows_out(b, par):
                n = at(b, par)
                for c, (hi, lo, rows, done) in enumerate(((q_hi, q_lo, q_rows, q_wr), (k_hi, k_lo, k_rows, k_wr))):
                    sp.wait_ge(qk_split, sp.snap(2 * n + c + 1))
                    order = (hi, hi, lo) if c == 0 else (hi, lo, hi)
                    for r in range(3):
                        sp.dma_start(rows[:, r * D:(r + 1) * D, :], order[r][:].bitcast(F32)).then_inc(done, 16)

            def split_rows_in(b, par):
                n = at(b, par)
                sp.wait_ge(q_wr, sp.snap(48 * (n + 1)))
                sp.wait_ge(k_wr, sp.snap(48 * (n + 1)))
                for j in range(HG):
                    strip = slice(32 * j, 32 * j + 3 * D)
                    sp.dma_start(q_bd[par][strip, j:H:HG, :].bitcast(F32), loads_of(q_rows)[j]).then_inc(qk_ld[par], 16)
                    sp.dma_start(k_st[par][strip, :, :].bitcast(F32), loads_of(k_rows)[j]).then_inc(qk_ld[par], 16)

            def max_row_in(b, par, g):
                n = at(b, par)
                sp.wait_ge(m_ready, sp.snap(NG * n + g + 1))
                sp.dma_start(q_bd[par][P - 1:P, HG * g:HG * (g + 1), :].bitcast(F32), m_row[g][:].bitcast(F32)).then_inc(m_ld[g], 16)

            split_rows_out(0, 0)
            split_rows_in(0, 0)
            half_rows = SLOTS // P // 2 * E
            for i in range(2):
                sp.dma_start(sorted_x.rearrange("(p k) e -> p (k e)", p=P)[:, i * half_rows:(i + 1) * half_rows],
                             q_bd[1][:, 0:half_rows // S, :].bitcast(F32).rearrange("p h s -> p (h s)")).then_inc(fill_done, 16)
            sp.wait_ge(qk_ld[0], 16 * 2 * HG)
            split_rows_out(1, 1)
            sp.wait_ge(fill_done, 32)
            split_rows_in(1, 1)
            for g in range(NG):
                max_row_in(0, 0, g)

            def attention(b, par, more, more2):
                n = at(b, par)
                nxt = (b + 1) if isinstance(b, int) else ("r", b[1] + (par + 1) // 2)
                nxt2 = (b + 2) if isinstance(b, int) else ("r", b[1] + 1)
                if more:
                    max_row_in(nxt, 1 - par, 0)
                if more2:
                    sp.wait_ge(qk_ld[1 - par], sp.snap(16 * 2 * HG * (half(b, par, 1) + 1)))
                    split_rows_out(nxt2, par)
                if more:
                    max_row_in(nxt, 1 - par, 1)
                    max_row_in(nxt, 1 - par, 2)
                if more2:
                    sp.wait_ge(st_done, sp.snap(UB * (n + 1)))
                    split_rows_in(nxt2, par)
                if more:
                    max_row_in(nxt, 1 - par, 3)
                dst = sp.snap(n * E) if not isinstance(n, int) else n * E
                sp.wait_ge(aT_ready, sp.snap(n + 1 + PRIME_ATOUT))
                sp.dma_start(att_T.rearrange("b e s -> (b e) s")[bass.ds(dst, E), :], a_T[:]).then_inc(aT_st, 16)

            with sp.Fori(0, B // 2 - 1) as i:
                for par in range(2):
                    attention(("r", i), par, True, True)
            attention(B - 2, 0, True, False)
            sp.wait_ge(st_done, UB * (B - 1))
            sp.dma_start(egu[:], e_gu).then_inc(egu_ld, 16)
            attention(B - 1, 1, False, False)

            sp.wait_ge(scattered, 16 * 2 * NT)
            sp.wait_ge(f_done, B + PRIME_F)
            sp.wait_ge(aT_st, 16 * (B + 1))

            for t in range(2):
                sp.dma_start(xg[t][:], sorted_x[t * P:(t + 1) * P, :]).then_inc(xg_ld[t], 16)

            def expert_tile(t, par, first, load):
                n = at(t, par)
                src = sp.snap((n + 2) * P) if not isinstance(n, int) else (n + 2) * P
                if load:
                    sp.wait_ge(xg_tr, sp.snap(n + 1))
                    sp.dma_start(xg[par][:], sorted_x[bass.ds(src, P), :]).then_inc(xg_ld[par], 16)
                if not first:
                    dst = sp.snap((n - 2) * P) if not isinstance(n, int) else (n - 2) * P
                    sp.wait_ge(y_out, sp.snap(n - 1))
                    sp.dma_start(sorted_y[bass.ds(dst, P), :], y_sb[par][:]).then_inc(y_st[par], 16)

            for t in range(2):
                expert_tile(t, t, True, True)
            with sp.Fori(1, NTILE // 2 - 1) as i:
                for par in range(2):
                    expert_tile(("r", i), par, False, True)
            for t in range(NTILE - 2, NTILE + 2):
                expert_tile(t, t % 2, False, False)

            def last_in(b, par):
                n = at(b, par)
                src = n * E if isinstance(n, int) else sp.snap(n * E)
                tok = n * S if isinstance(n, int) else sp.snap(n * S)
                sp.dma_start(a_in[par][:], att_T.rearrange("b e s -> (b e) s")[bass.ds(src, E), :]).then_inc(s_ld[par], 16)
                sp.dma_start(x_in[par][:], x_tok[bass.ds(tok, S), :].rearrange("(n p) e -> p n e", p=P)).then_inc(s_ld[par], 16)

            def last_out(b, par):
                n = at(b, par)
                tok = n * S if isinstance(n, int) else sp.snap(n * S)
                sp.wait_ge(o_sum, sp.snap(n + 1))
                sp.dma_start(out_tok[bass.ds(tok, S), :].rearrange("(n p) e -> p n e", p=P), o_sb[par][:]).then_inc(o_st[par], 16)

            for b in range(2):
                last_in(b, b)
            with sp.Fori(0, B // 2 - 1) as i:
                for par in range(2):
                    last_out(("r", i), par)
                    last_in(("r", i + 1), par)
            for par in range(2):
                last_out(B - 2 + par, par)
            for par in range(2):
                sp.wait_ge(o_st[par], 16 * (B // 2))
                sp.wait_ge(y_st[par], 16 * (NTILE // 2))

        @block.gpsimd
        def _(pool):
            pool.memset(ident[:], 0.0).then_inc(vec_p, 1)
            pool.wait_ge(vec_p, 1)
            pool.affine_select(out=ident[:], in_=ident[:], compare_op=ALU.not_equal, fill=1.0, base=0,
                               pattern=[[-1, P]], channel_multiplier=1).then_inc(consts, 1)
            pool.wait_ge(consts, 1)
            pool.tensor_copy(ident_bf[:], ident[:]).then_inc(consts, 1)
            for i in range(2):
                pool.memset(q_bd[i][:].bitcast(F32), 0.0).then_inc(cleared, 1)
                if i == 0:
                    for k in range(2):
                        ins = pool.memset(k_st[k][:].bitcast(F32), 0.0)
                    ins.then_inc(cleared, 1)
            pool.memset(mask_kq[:], 0.0)
            pool.memset(mask_qk[:], 0.0)
            pool.memset(before[:], 1.0)
            for i in range(2):
                pool.memset(v32[i][:], 0.0)
            pool.memset(not_first[:], 1.0)
            pool.memset(ones_f[:], 1.0)
            pool.memset(ones_bf[:], 1.0).then_inc(vec_p, 1)
            pool.wait_ge(vec_p, 2)
            pool.affine_select(out=mask_kq[:], in_=mask_kq[:], compare_op=ALU.is_ge, fill=NEG, base=0,
                               pattern=[[0, HG], [1, P]], channel_multiplier=-1)
            pool.affine_select(out=mask_qk[:], in_=mask_qk[:], compare_op=ALU.is_ge, fill=NEG, base=0,
                               pattern=[[0, HG], [-1, P]], channel_multiplier=1)
            pool.affine_select(out=before[:], in_=before[:], compare_op=ALU.is_ge, fill=0.0, base=-1,
                               pattern=[[1, P]], channel_multiplier=-1)
            for i in range(2):
                pool.memset(v32[i][:, :, :, D:D + 1], 1.0)
            pool.memset(not_first[:, :, 0:1], 0.0)
            pool.iota(expert_no[:], pattern=[[1, NX]], base=0, channel_multiplier=0, allow_small_or_imprecise_dtypes=True)
            pool.iota(tile_start[:], pattern=[[P, NTILE]], base=0, channel_multiplier=0,
                      allow_small_or_imprecise_dtypes=True).then_inc(consts, 1)
            with pool.Fori(0, B) as b:
                pool.wait_ge(xn_done, b + 1)
                pool.tensor_copy(xn_rows[:, bass.ds(b * NB, NB), :], xn_blk[:]).then_inc(xn_kept, 1)
            pool.wait_ge(routed, 1)
            pool.wait_ge(fill_done, 32)
            for n in range(NT):
                for c in range(2):
                    pool.indirect_dma_start(sorted_x, bass.IndirectOffsetOnAxis(ap=slot_idx[:, c, n:n + 1], axis=0),
                                            xn_rows[:, n, :], None).then_inc(scattered, 16)
            for par in range(2):
                pool.wait_ge(y_st[par], 16 * (NTILE // 2))
            for b in range(B):
                par = b % 2
                if b >= 2:
                    pool.wait_ge(o_sum, b - 1)
                for n in range(NB):
                    for c in range(2):
                        pool.indirect_dma_start(picked[par][:, c, n, :], None, sorted_y,
                                                bass.IndirectOffsetOnAxis(ap=slot_idx[:, c, b * NB + n:b * NB + n + 1], axis=0)
                                                ).then_inc(got[par], 16)

        @block.tensor
        def _(pe):
            pe.wait_ge(consts, 3)
            pe.wait_ge(w_early, 48)
            with pe.Fori(0, B) as b:
                pe.wait_ge(xn_done, b + 1)
                pe.wait_ge(xnT_done, b + 1)
                for n in range(NB):
                    ins = pe.transpose(bank[0][:, n * P:(n + 1) * P], xn_blk[:, n, :], ident[:])
                ins.then_inc(xT_done, 1)
                pe.wait_ge(xnT_done, b + 2)
                pe.matmul(bank[1][0:NX, :], gate[:], xnT[:, bass.ds(b * S, S)], start=True, stop=True).then_inc(lgT_mm, 1)
                pe.wait_ge(lgT_done, b + 1)
                for n in range(NB):
                    ins = pe.transpose(bank[2][:, n * P:(n + 1) * P], lgT[:, n * P:(n + 1) * P], ident[:])
                ins.then_inc(lg_done, 1)

            def project(n, c, done):
                pe.matmul(proj_bank[:], wqkv[:, c, :], xnT[:, bass.ds(n * S, S)], start=True, stop=True).then_inc(done, 1)

            def v_transposes(n):
                pe.wait_ge(v_biased, n + 1)
                for k in range(NB):
                    ins = pe.transpose(proj_bank[:, k * P:(k + 1) * P], vT[:, k * P:(k + 1) * P], ident[:])
                ins.then_inc(v_tr, 1)

            def max_unit(n, par, u):
                g, k = divmod(u, NU)
                qb, heads = MX_QB[k], MX_HEADS[k]
                w = (qb + 1) * P
                dst = mx_bank[u % 2]
                if not (isinstance(n, int) and n * UB + u < 2):
                    pe.wait_ge(red_done, n * UB + u - 1)
                for i, j in enumerate(heads):
                    pe.matmul(dst[:, i * w:(i + 1) * w], q_bd[par][0:P - 1, HG * g + j, qb * P:(qb + 1) * P],
                              k_st[par][0:P - 1, g, 0:w], start=(i == 0), stop=False, skip_group_check=True)
                nh = len(heads)
                diag = dst[:, 0:nh * w].rearrange("p (h w) -> p h w", h=nh)[:, :, qb * P:w]
                pe.matmul(diag, ident_bf[:], mask_qk[:, 0:nh, :], start=False, stop=True, skip_group_check=True).then_inc(mx_done, 1)

            def max_transposes(n, g):
                pe.wait_ge(red_done, n * UB + NU * (g + 1))
                for qb in range(NB):
                    ins = pe.transpose(row_bank[0:HG, qb * P:(qb + 1) * P], neg_max[:, g, qb, :], ident[:])
                ins.then_inc(m_tr, 1)

            def score_unit(n, par, g, u):
                kb, heads = ST_KB[u], ST_HEADS[u]
                w = S - kb * P
                dst = st_bank[(g * NU + u) % 2]
                nh = len(heads)
                pe.wait_ge(exp_done, n * UB + g * NU + u - 1 + PRIME_EXP)
                h0 = HG * g + heads[0]
                pe.matmul(dst[:, 0:nh * w], k_st[par][:, g, kb * P:(kb + 1) * P], q_bd[par][:, h0:h0 + nh, kb * P:S],
                          start=True, stop=False, skip_group_check=True)
                diag = dst[:, 0:nh * w].rearrange("p (h w) -> p h w", h=nh)[:, :, 0:P]
                pe.matmul(diag, ident_bf[:], mask_kq[:, 0:nh, :], start=False, stop=True, skip_group_check=True).then_inc(st_done, 1)

            def value_bundle(n, par, g, kb):
                pe.wait_ge(exp_done, n * UB + g * NU + AV_UNITS[kb] + PRIME_EXP)
                dst = av_bank[g % 2]
                if kb == 0:
                    pe.wait_ge(av_out, n * NG + g - 1 + PRIME_AO)
                for j in range(HG):
                    u, lo = [(j, 0), (4 + j, 0), (8 + j // 2, j % 2 * 2 * P), (10, j * P)][kb]
                    w = S - kb * P
                    ins = pe.matmul(dst[32 * j:32 * j + 32, kb * P:S], v32[par][:, kb, HG * g + j, :], probs[:, u, lo:lo + w],
                                    start=(kb == 0), stop=(kb == NB - 1), skip_group_check=True)
                ins.then_inc(av_done, 1)

            def to_tokens(n, g, more):
                pe.wait_ge(av_out, n * NG + g + 1 + PRIME_AO)
                if g == 0:
                    pe.wait_ge(aT_ready, n + PRIME_ATOUT)
                elif more:
                    pe.wait_ge(m_ready, (n + 1) * NG + g)
                else:
                    pe.wait_ge(a_done, n * NG + g)
                for k in range(NB):
                    ins = pe.transpose(row_bank[:, k * P:(k + 1) * P], av_sb[g % 2][:, k * P:(k + 1) * P], ident[:])
                ins.then_inc(t_done, 1)

            def to_features(n, more):
                pe.wait_ge(a_done, (n + 1) * NG)
                if more:
                    pe.wait_ge(m_ready, (n + 2) * NG)
                for k in range(NB):
                    ins = pe.transpose(row_bank[:, k * P:(k + 1) * P], a_tok[:, k, :], ident[:])
                ins.then_inc(f_done, 1)

            for n in range(2):
                for c in range(2):
                    if n or c:
                        pe.wait_ge(qk_split, 2 * n + c)
                    project(n, c, qk_proj)
            pe.wait_ge(qk_split, 4)
            project(0, 2, v_proj)
            v_transposes(0)
            pe.wait_ge(hot_ready, 1)
            flat = hot_bf[:].rearrange("p n x -> p (n x)")
            pe.matmul(bank[0][:, 0:NT * NX], before[:], flat, start=True, stop=True, skip_group_check=True)
            pe.matmul(bank[0][:, NT * NX:2 * NT * NX], ones_bf[:], flat, start=False, stop=True, skip_group_check=True).then_inc(count_done, 1)
            pe.wait_ge(qk_ld[0], 16 * 2 * HG)
            pe.wait_ge(lg_kept, B)
            for u in range(UB):
                max_unit(0, 0, u)
                if u % NU == NU - 1:
                    g = u // NU
                    if g:
                        pe.wait_ge(m_ready, g)
                    max_transposes(0, g)

            def attention(b, par, more, more2):
                n = at(b, par)
                for g in range(NG):
                    for u in range(NU):
                        s = g * NU + u
                        if u == 0:
                            pe.wait_ge(m_ld[g], 16 * (n + 1))
                            if g == 0:
                                pe.wait_ge(v_ready, n + 1)
                        score_unit(n, par, g, u)
                        if more and s >= LAG:
                            if s == LAG:
                                pe.wait_ge(qk_ld[1 - par], 16 * 2 * HG * (half(b, par, 1) + 1))
                            max_unit(n + 1, 1 - par, s - LAG)
                        if u == 6:
                            value_bundle(n, par, g, 0)
                        if u == 10:
                            value_bundle(n, par, g, 1)
                        if g and u == 1:
                            value_bundle(n, par, g - 1, 2)
                        if g and u == 2:
                            value_bundle(n, par, g - 1, 3)
                        if g and u == 5:
                            to_tokens(n, g - 1, more)
                        if g and u == 7 and more:
                            pe.wait_ge(a_done, n * NG + g)
                            max_transposes(n + 1, g - 1)
                        if more and s == 8:
                            pe.wait_ge(qk_split, 2 * (n + 2))
                            project(n + 1, 2, v_proj)
                        if more and s == 11:
                            v_transposes(n + 1)
                        if more2 and s == 15:
                            pe.wait_ge(v_ready, n + 2)
                            project(n + 2, 0, qk_proj)
                        if more2 and s == 20:
                            pe.wait_ge(qk_split, 2 * (n + 2) + 1)
                            project(n + 2, 1, qk_proj)
                tail = list(range(UB - LAG, UB))
                for u in tail[:3]:
                    if more:
                        max_unit(n + 1, 1 - par, u)
                value_bundle(n, par, NG - 1, 2)
                value_bundle(n, par, NG - 1, 3)
                for u in tail[3:]:
                    if more:
                        max_unit(n + 1, 1 - par, u)
                to_tokens(n, NG - 1, more)
                if more:
                    pe.wait_ge(a_done, (n + 1) * NG)
                    max_transposes(n + 1, NG - 1)
                to_features(n, more)

            with pe.Fori(0, B // 2 - 1) as i:
                for par in range(2):
                    attention(("r", i), par, True, True)
            attention(B - 2, 0, True, False)
            attention(B - 1, 1, False, False)

            g_bank, u_bank = bank[0:2], bank[2:4]
            xgT_bank, hidT_bank, y_bank = bank[4], bank[5], bank[6]
            pe.wait_ge(aT_ready, B + PRIME_ATOUT)
            pe.wait_ge(exp_done, B * UB + PRIME_EXP)
            pe.wait_ge(egu_ld, 16)
            pe.wait_ge(w_late, 16 * 16)

            def gate_up(t, par):
                n = at(t, par)
                ex = pe.value_load(tile_expert[0:1, bass.ds(n, 1)], min_val=0, max_val=NX - 1)
                pe.wait_ge(xgT_done, n + 1)
                if not (isinstance(n, int) and n < 2):
                    pe.wait_ge(hid_done, n - 1)
                w = egu[:].rearrange("p x a f -> p (x a f)")
                pe.matmul(g_bank[par][:, 0:F], xgT[par][:], w[:, bass.ds(ex * (2 * F), F)], start=True, stop=True)
                pe.matmul(u_bank[par][:, 0:F], xgT[par][:], w[:, bass.ds(ex * (2 * F) + F, F)], start=True, stop=True).then_inc(gu_done, 1)

            def hid_transposes(t, par):
                n = at(t, par)
                pe.wait_ge(hid_done, n + 1)
                if not (isinstance(n, int) and n == 0):
                    pe.wait_ge(hidT_done, n)
                for c in range(FC):
                    m = min(P, F - c * P)
                    ins = pe.transpose(hidT_bank[0:m, c * P:(c + 1) * P], hid[par][:, c * P:c * P + m], ident[:])
                ins.then_inc(hid_tr, 1)

            def down(t, par):
                n = at(t, par)
                ex = pe.value_load(tile_expert[0:1, bass.ds(n, 1)], min_val=0, max_val=NX - 1)
                pe.wait_ge(hidT_done, n + 1)
                if not (isinstance(n, int) and n == 0):
                    pe.wait_ge(y_out, n)
                w = edn[:].rearrange("p x c e -> p (x c e)")
                for c in range(FC):
                    m = min(P, F - c * P)
                    ins = pe.matmul(y_bank[:, 0:E], hidT[par][0:m, c, :], w[0:m, bass.ds(ex * (FC * E) + c * E, E)],
                                    start=(c == 0), stop=(c == FC - 1))
                ins.then_inc(y_done, 1)

            def x_step(t, par):
                n = at(t, par)
                pe.wait_ge(xg_ld[par], 16 * (half(t, par, 0) + 1))
                if not (isinstance(n, int) and n == 0):
                    pe.wait_ge(xgT_done, n)
                pe.transpose(xgT_bank[:, 0:P], xg[par][:], ident[:]).then_inc(xg_tr, 1)

            def shift(t, par, d):
                if isinstance(t, int):
                    return t + d, (t + d) % 2
                return ("r", t[1] + (par + d) // 2), (par + d) % 2

            def expert_step(t, par, has_t, has_1, has_2, has_x):
                if has_t:
                    gate_up(t, par)
                if has_1:
                    hid_transposes(*shift(t, par, -1))
                if has_x:
                    x_step(*shift(t, par, 1))
                if has_2:
                    down(*shift(t, par, -2))

            x_step(0, 0)
            for t in range(2):
                expert_step(t, t, True, t >= 1, False, True)
            with pe.Fori(1, NTILE // 2 - 1) as i:
                for par in range(2):
                    expert_step(("r", i), par, True, True, True, True)
            for t in range(NTILE - 2, NTILE + 2):
                expert_step(t, t % 2, t < NTILE, t <= NTILE, True, t + 1 < NTILE)

            res_bank, tok_bank = bank[6], bank[7]
            pe.wait_ge(y_out, NTILE)

            def shared_up(t, par):
                n = at(t, par)
                for c in range(FC):
                    m = min(P, F - c * P)
                    if not (isinstance(n, int) and n == 0):
                        pe.wait_ge(shid_done, FC * (n - 1) + c + 1)
                    for a in range(2):
                        ins = pe.matmul(bank[2 * c + a][0:m, :], sgu[:, a, c * P:c * P + m], xnT[:, bass.ds(n * S, S)], start=True, stop=True)
                    ins.then_inc(sgu_done, 1)

            def shared_down(t, par):
                n = at(t, par)
                pe.wait_ge(s_ld[par], 32 * (half(t, par, 0) + 1))
                if not (isinstance(n, int) and n == 0):
                    pe.wait_ge(res_out, n)
                pe.matmul(res_bank[:], wout[:], a_in[par][:], start=True, stop=False)
                for c in range(FC):
                    m = min(P, F - c * P)
                    pe.wait_ge(shid_done, FC * n + c + 1)
                    ins = pe.matmul(res_bank[:], sdn[0:m, c, :], s_hid[par][0:m, c, :], start=False, stop=(c == FC - 1))
                ins.then_inc(res_done, 1)

            def back_to_tokens(t, par):
                n = at(t, par)
                pe.wait_ge(res_out, n + 1)
                if not (isinstance(n, int) and n == 0):
                    pe.wait_ge(o_base, n)
                for k in range(NB):
                    ins = pe.transpose(tok_bank[:, k * P:(k + 1) * P], resT[:, k * P:(k + 1) * P], ident[:])
                ins.then_inc(o_tr, 1)

            shared_up(0, 0)
            shared_up(1, 1)
            shared_down(0, 0)
            with pe.Fori(1, B // 2) as i:
                for par in range(2):
                    shared_up(("r", i), par)
                    back_to_tokens(*shift(("r", i), par, -2))
                    shared_down(*shift(("r", i), par, -1))
            back_to_tokens(B - 2, 0)
            shared_down(B - 1, 1)
            back_to_tokens(B - 1, 1)

        @block.scalar
        def _(act):
            act.wait_ge(stats, 1)
            act.wait_ge(lgT_clear, 1)
            act.activation(std[:], var[:], ACT.Sqrt).then_inc(std_done, 1)
            with act.Fori(0, B) as b:
                act.wait_ge(xT_done, b + 2)
                act.activation(xnT[:, bass.ds(b * S, S)], bank[0][:], ACT.Copy).then_inc(xnT_done, 1)
                act.wait_ge(lgT_mm, b + 1)
                act.activation(lgT[0:NX, :], bank[1][0:NX, :], ACT.Copy).then_inc(lgT_done, 1)
                act.wait_ge(lg_done, b + 1)
                act.activation(lg[:, bass.ds(b * NB, NB), :], bank[2][:].rearrange("p (n c) -> p n c", c=P)[:, :, 0:NX],
                               ACT.Copy).then_inc(lg_kept, 1)

            def split_high(n, c):
                dst, wr = ((q_hi, q_wr), (k_hi, k_wr))[c]
                act.wait_ge(qk_proj, 2 * n + c + 1)
                if not (isinstance(n, int) and n == 0):
                    act.wait_ge(wr, 48 * n)
                act.activation(dst[:], proj_bank[:], ACT.Identity, bias=bqkv[:, c:c + 1]).then_inc(qk_hi, 1)

            act.wait_ge(w_early, 48)
            for n in range(2):
                for c in range(2):
                    split_high(n, c)
            act.wait_ge(z_ready, 1)
            act.activation(prob[:], logit[:], ACT.Exp).then_inc(e_ready, 1)
            act.wait_ge(routed, 1)

            def exp_unit(n, g, u):
                w = (S - ST_KB[u] * P) * len(ST_HEADS[u])
                act.wait_ge(st_done, n * UB + g * NU + u + 1)
                if u in (0, 4, 8, 10):
                    k = (0, 4, 8, 10).index(u)
                    act.wait_ge(av_done, (n * NG + g - 1) * NB + k + 1 + PRIME_AV)
                act.activation(probs[:, u, 0:w], st_bank[(g * NU + u) % 2][:, 0:w], ACT.Exp, scale=SCALE).then_inc(exp_done, 1)

            def values_out(n, g):
                act.wait_ge(av_done, (n * NG + g + 1) * NB + PRIME_AV)
                act.wait_ge(t_done, n * NG + g - 1 + PRIME_T)
                act.activation(av_sb[g % 2][:], av_bank[g % 2][:], ACT.Copy).then_inc(av_out, 1)

            def attention(b, par, more, more2):
                n = at(b, par)
                for g in range(NG):
                    for u in range(NU):
                        s = g * NU + u
                        exp_unit(n, g, u)
                        if g and u == 3:
                            values_out(n, g - 1)
                        if more2 and s == 17:
                            split_high(n + 2, 0)
                        if more2 and s == 22:
                            split_high(n + 2, 1)
                values_out(n, NG - 1)

            with act.Fori(0, B // 2 - 1) as i:
                for par in range(2):
                    attention(("r", i), par, True, True)
            attention(B - 2, 0, True, False)
            attention(B - 1, 1, False, False)

            g_bank, xgT_bank = bank[0:2], bank[4]

            def x_out(t, par):
                n = at(t, par)
                act.wait_ge(xg_tr, n + 1)
                if not (isinstance(n, int) and n < 2):
                    act.wait_ge(gu_done, n - 1)
                act.activation(xgT[par][:], xgT_bank[:, 0:P], ACT.Copy).then_inc(xgT_done, 1)

            def sigmoid_part(t, par):
                n = at(t, par)
                act.wait_ge(gu_done, n + 1)
                if not (isinstance(n, int) and n < 2):
                    act.wait_ge(hid_done, n - 1)
                act.activation(sg[par][:], g_bank[par][:, 0:F], ACT.Silu).then_inc(sg_done, 1)

            def expert_step(t, par, has_x):
                if has_x:
                    if isinstance(t, int):
                        x_out(t + 1, (t + 1) % 2)
                    else:
                        x_out(("r", t[1] + (par + 1) // 2), 1 - par)
                sigmoid_part(t, par)

            act.wait_ge(f_done, B + PRIME_F)
            act.wait_ge(aT_st, 16 * (B + 1))
            x_out(0, 0)
            for t in range(2):
                expert_step(t, t, True)
            with act.Fori(1, NTILE // 2 - 1) as i:
                for par in range(2):
                    expert_step(("r", i), par, True)
            for t in range(NTILE - 2, NTILE):
                expert_step(t, t % 2, t + 1 < NTILE)

            def shared_sigmoid(t, par):
                n = at(t, par)
                for c in range(FC):
                    m = min(P, F - c * P)
                    act.wait_ge(sgu_done, FC * n + c + 1)
                    if not (isinstance(n, int) and n == 0):
                        act.wait_ge(shid_done, FC * (n - 1) + c + 1)
                    act.activation(s_sig[0:m, c, :], bank[2 * c][0:m, :], ACT.Silu).then_inc(ssig_done, 1)

            def result_out(t, par):
                n = at(t, par)
                act.wait_ge(res_done, n + 1)
                if not (isinstance(n, int) and n == 0):
                    act.wait_ge(o_tr, n)
                act.activation(resT[:], bank[6][:], ACT.Identity, bias=bout[:, 0:1]).then_inc(res_out, 1)

            shared_sigmoid(0, 0)
            with act.Fori(0, B // 2 - 1) as i:
                for par in range(2):
                    shared_sigmoid(("r", i + (par + 1) // 2), 1 - par)
                    result_out(("r", i), par)
            shared_sigmoid(B - 1, 1)
            result_out(B - 2, 0)
            result_out(B - 1, 1)

        @block.vector
        def _(dve):
            chain = [0]

            def link(ins):
                chain[0] += 1
                ins.then_inc(vec, 1)
                dve.wait_ge(vec, chain[0])

            dve.memset(one_row[:], 1.0).then_inc(ones_set, 1)
            dve.memset(lgT[:], 0.0).then_inc(lgT_clear, 1)
            for i, (s_, n_) in enumerate(((xnT_done, 1), (xT_done, 1), (xn_kept, 1), (exp_done, PRIME_EXP), (av_done, PRIME_AV), (av_out, PRIME_AO),
                           (t_done, PRIME_T), (f_done, PRIME_F), (aT_ready, PRIME_ATOUT), (aT_st, 16))):
                dve.memset(primed[:, i:i + 1], 0.0).then_inc(s_, n_)

            for i in range(4):
                dve.wait_ge(x_ld[i], 16)
                with dve.Fori(i * NT // 4, (i + 1) * NT // 4) as n:
                    dve.bn_stats(bn[:, bass.ds(n, 1), :], x_all[:, bass.ds(n, 1), :]).then_inc(stat1, 1)
            dve.wait_ge(stat1, NT)
            for n in range(NT):
                dve.bn_aggr(mv[:, n, :], bn[:, n, :]).then_inc(stat1, 1)
            dve.wait_ge(stat1, 2 * NT)
            dve.tensor_scalar(var[:], mv[:, :, 1], EPS, None, ALU.add).then_inc(stats, 1)
            dve.wait_ge(std_done, 1)
            link(dve.reciprocal(rstd[:], std[:]))
            link(dve.tensor_tensor(newton[:], rstd[:], rstd[:], ALU.mult))
            link(dve.tensor_tensor(newton[:], newton[:], var[:], ALU.mult))
            link(dve.tensor_scalar(newton[:], newton[:], -0.5, 1.5, ALU.mult, ALU.add))
            link(dve.tensor_tensor(rstd[:], rstd[:], newton[:], ALU.mult))
            with dve.Fori(0, B) as b:
                dve.wait_ge(xT_done, b + 1)
                dve.wait_ge(xn_kept, b + 1)
                for k in range(NB):
                    n = b * NB + k
                    ins = dve.tensor_scalar(xn_blk[:, k, :], x_all[:, bass.ds(n, 1), :].rearrange("p a e -> p (a e)"),
                                            mv[:, bass.ds(n, 1), 0:1].rearrange("p a e -> p (a e)"), rstd[:, bass.ds(n, 1)],
                                            ALU.subtract, ALU.mult)
                ins.then_inc(xn_done, 1)

            def split_low(n, c):
                hi, lo, wr = ((q_hi, q_lo, q_wr), (k_hi, k_lo, k_wr))[c]
                dve.wait_ge(qk_hi, 2 * n + c + 1)
                if not (isinstance(n, int) and n == 0):
                    dve.wait_ge(wr, 48 * n)
                dve.scalar_tensor_tensor(out=lo[:], in0=proj_bank[:], scalar=bqkv[:, c:c + 1], in1=hi[:].bitcast(F32),
                                         op0=ALU.add, op1=ALU.subtract).then_inc(qk_split, 1)

            def value_bias(n):
                dve.wait_ge(v_proj, n + 1)
                if not (isinstance(n, int) and n == 0):
                    dve.wait_ge(v_tr, n)
                dve.tensor_scalar(vT[:], proj_bank[:], bqkv[:, 2:3], None, ALU.add).then_inc(v_biased, 1)

            def value_rows(n, par):
                dve.wait_ge(v_tr, n + 1)
                if not (isinstance(n, int) and n < 2):
                    dve.wait_ge(av_done, (n - 1) * NG * NB + PRIME_AV)
                dve.tensor_copy(v32[par][:].rearrange("p n h c -> p (n h) c")[:, :, 0:D],
                                proj_bank[:].rearrange("p (n d) -> p n d", d=D)).then_inc(v_ready, 1)

            dve.wait_ge(w_early, 48)
            for n in range(2):
                for c in range(2):
                    split_low(n, c)
            value_bias(0)
            dve.wait_ge(consts, 3)
            value_rows(0, 0)

            each = [P, NT, NX]
            dve.wait_ge(lg_kept, B)
            dve.wait_ge(xn_kept, B + 1)
            link(dve.tensor_reduce(pick[:], lg[:], AX.X, ALU.max))
            dve.tensor_tensor(logit[:], lg[:], pick[:, :, None].broadcast_to(each), ALU.subtract).then_inc(z_ready, 1)
            dve.wait_ge(e_ready, 1)
            link(dve.tensor_reduce(pick[:], prob[:], AX.X, ALU.add))
            link(dve.reciprocal(pick[:], pick[:]))
            link(dve.tensor_tensor(prob[:], prob[:], pick[:, :, None].broadcast_to(each), ALU.mult))
            for c in range(2):
                link(dve.tensor_reduce(best[c][:], prob[:], AX.X, ALU.max))
                link(dve.tensor_tensor(cand[:], prob[:], best[c][:, :, None].broadcast_to(each), ALU.is_equal))
                link(dve.scalar_tensor_tensor(out=cand[:], in0=cand[:], scalar=-float(NX * NX),
                                              in1=expert_no[:, None, :].broadcast_to(each), op0=ALU.mult, op1=ALU.add))
                link(dve.tensor_reduce(pick[:], cand[:], AX.X, ALU.min))
                link(dve.tensor_tensor(hot[c][:], cand[:], pick[:, :, None].broadcast_to(each), ALU.is_equal))
                if c == 0:
                    link(dve.scalar_tensor_tensor(out=prob[:], in0=hot[0][:], scalar=-4.0, in1=prob[:], op0=ALU.mult, op1=ALU.add))
            dve.tensor_tensor(hot_bf[:], hot[0][:], hot[1][:], ALU.add).then_inc(hot_ready, 1)
            link(dve.scalar_tensor_tensor(out=pick[:], in0=best[0][:], scalar=1e-20, in1=best[1][:], op0=ALU.add, op1=ALU.add))
            link(dve.reciprocal(pick[:], pick[:]))
            for c in range(2):
                link(dve.tensor_tensor(topw[:, c, :], best[c][:], pick[:], ALU.mult))
            dve.wait_ge(count_done, 1)
            link(dve.tensor_copy(total[:], bank[0][:, NT * NX:2 * NT * NX].rearrange("p (n x) -> p x n", x=NX)))
            flat = [t[:].rearrange("p x n -> p (x n)") for t in (incl, not_first, total)]
            link(dve.tensor_tensor_scan(flat[0], flat[1], flat[2], 0.0, ALU.mult, ALU.add))
            link(dve.tensor_scalar(rows_i[:], incl[:, :, NT - 1], float(P - 1), None, ALU.add))
            link(dve.tensor_scalar(rows_i[:], rows_i[:], -P, None, ALU.bitwise_and))
            link(dve.tensor_copy(rows_f[:], rows_i[:]))
            link(dve.tensor_tensor_scan(end_row[:], ones_f[:], rows_f[:], 0.0, ALU.mult, ALU.add))
            link(dve.tensor_tensor(base_row[:], end_row[:], rows_f[:], ALU.subtract))
            link(dve.tensor_tensor(incl[:], incl[:], total[:], ALU.subtract))
            link(dve.tensor_tensor(incl[:], incl[:], base_row[:, :, None].broadcast_to([P, NX, NT]), ALU.add))
            link(dve.tensor_tensor(slot[:], bank[0][:, 0:NT * NX].rearrange("p (n x) -> p n x", x=NX),
                                   incl[:].rearrange("p x n -> p n x"), ALU.add))
            for c in range(2):
                link(dve.tensor_tensor(hot[c][:], hot[c][:], slot[:], ALU.mult))
                link(dve.tensor_reduce(slot_f[:, c, :], hot[c][:], AX.X, ALU.add))
            link(dve.tensor_copy(slot_idx[:], slot_f[:]))
            tiles = [1, NTILE, NX]
            link(dve.tensor_tensor(past[:], end_row[0:1, None, :].broadcast_to(tiles), tile_start[:, :, None].broadcast_to(tiles), ALU.is_le))
            link(dve.tensor_reduce(tile_f[:], past[:], AX.X, ALU.add))
            dve.tensor_scalar(tile_expert[:], tile_f[:], float(NX - 1), None, ALU.min).then_inc(routed, 1)

            def reduce_unit(n, u):
                g, k = divmod(u, NU)
                qb, heads = MX_QB[k], MX_HEADS[k]
                w, nh = (qb + 1) * P, len(heads)
                dve.wait_ge(mx_done, n * UB + u + 1)
                dve.tensor_reduce(neg_max[:, g, qb, heads[0]:heads[0] + nh],
                                  mx_bank[u % 2][:, 0:nh * w].rearrange("p (h w) -> p h w", h=nh), AX.X, ALU.max,
                                  negate=True).then_inc(red_done, 1)

            def max_rows(n, g):
                dve.wait_ge(m_tr, n * NG + g + 1)
                if not (isinstance(n, int) and n == 0):
                    dve.wait_ge(m_ld[g], 16 * n)
                dve.tensor_copy(m_row[g][:], row_bank[0:HG, :]).then_inc(m_ready, 1)

            def normalise(n, g):
                dve.wait_ge(t_done, n * NG + g + 1 + PRIME_T)
                o = row_bank[:].rearrange("p (n c) -> p n c", c=32)
                dve.reciprocal(inv_sum[:], o[:, :, D]).then_inc(inv_done, 1)
                dve.wait_ge(inv_done, n * NG + g + 1)
                if g == 0:
                    dve.wait_ge(f_done, n + PRIME_F)
                dve.tensor_tensor(a_tok[:, :, g * HG * D:(g + 1) * HG * D].rearrange("p n (h d) -> p n h d", d=D),
                                  row_bank[:].rearrange("p (n h c) -> p n h c", h=HG, c=32)[:, :, :, 0:D],
                                  inv_sum[:].rearrange("p (n h) -> p n h", h=HG)[:, :, :, None].broadcast_to([P, NB, HG, D]),
                                  ALU.mult).then_inc(a_done, 1)

            for u in range(UB):
                reduce_unit(0, u)
                if u % NU == NU - 1:
                    max_rows(0, u // NU)

            def attention(b, par, more, more2):
                n = at(b, par)
                for g in range(NG):
                    for u in range(NU):
                        s = g * NU + u
                        if more and s >= LAG:
                            reduce_unit(n + 1, s - LAG)
                        if g and u == 5:
                            normalise(n, g - 1)
                        if g and u == 7 and more:
                            max_rows(n + 1, g - 1)
                        if more and s == 8:
                            value_bias(n + 1)
                        if more and s == 11:
                            value_rows(n + 1, 1 - par)
                        if more2 and s == 17:
                            split_low(n + 2, 0)
                        if more2 and s == 22:
                            split_low(n + 2, 1)
                for u in range(UB - LAG, UB):
                    if more:
                        reduce_unit(n + 1, u)
                normalise(n, NG - 1)
                if more:
                    max_rows(n + 1, NG - 1)
                dve.wait_ge(f_done, n + 1 + PRIME_F)
                dve.wait_ge(aT_st, 16 * (n + 1))
                dve.tensor_copy(a_T[:], row_bank[:]).then_inc(aT_ready, 1)

            with dve.Fori(0, B // 2 - 1) as i:
                for par in range(2):
                    attention(("r", i), par, True, True)
            attention(B - 2, 0, True, False)
            attention(B - 1, 1, False, False)

            u_bank, hidT_bank, y_bank = bank[2:4], bank[5], bank[6]

            def hidden(t, par):
                n = at(t, par)
                dve.wait_ge(sg_done, n + 1)
                if not (isinstance(n, int) and n < 2):
                    dve.wait_ge(hid_tr, n - 1)
                dve.tensor_tensor(hid[par][:], sg[par][:], u_bank[par][:, 0:F], ALU.mult).then_inc(hid_done, 1)

            def hiddenT_out(t, par):
                n = at(t, par)
                dve.wait_ge(hid_tr, n + 1)
                if not (isinstance(n, int) and n < 2):
                    dve.wait_ge(y_done, n - 1)
                src = hidT_bank[:, 0:FC * P].rearrange("p (c m) -> p c m", c=FC)
                dve.tensor_copy(hidT[par][:, 0:2, :], src[:, 0:2, :])
                dve.tensor_copy(hidT[par][0:FR, 2, :], src[0:FR, 2, :]).then_inc(hidT_done, 1)

            def result(t, par):
                n = at(t, par)
                dve.wait_ge(y_done, n + 1)
                if not (isinstance(n, int) and n < 2):
                    dve.wait_ge(y_st[par], 16 * half(t, par, 0))
                dve.tensor_copy(y_sb[par][:], y_bank[:, 0:E]).then_inc(y_out, 1)

            def shift(t, par, d):
                if isinstance(t, int):
                    return t + d, (t + d) % 2
                return ("r", t[1] + (par + d) // 2), (par + d) % 2

            def expert_step(t, par, has_t, has_1, has_2):
                if has_1:
                    hiddenT_out(*shift(t, par, -1))
                if has_2:
                    result(*shift(t, par, -2))
                if has_t:
                    hidden(t, par)

            dve.wait_ge(aT_st, 16 * (B + 1))
            for t in range(2):
                expert_step(t, t, True, t >= 1, False)
            with dve.Fori(1, NTILE // 2 - 1) as i:
                for par in range(2):
                    expert_step(("r", i), par, True, True, True)
            for t in range(NTILE - 2, NTILE + 2):
                expert_step(t, t % 2, t < NTILE, t <= NTILE, True)

            def shared_hidden(t, par):
                n = at(t, par)
                for c in range(FC):
                    m = min(P, F - c * P)
                    dve.wait_ge(ssig_done, FC * n + c + 1)
                    if c == 0 and not (isinstance(n, int) and n < 2):
                        dve.wait_ge(res_done, n - 1)
                    dve.tensor_tensor(s_hid[par][0:m, c, :], s_sig[0:m, c, :], bank[2 * c + 1][0:m, :], ALU.mult).then_inc(shid_done, 1)

            def add_up(t, par):
                n = at(t, par)
                dve.wait_ge(o_tr, n + 1)
                dve.wait_ge(s_ld[par], 32 * (half(t, par, 0) + 1))
                if not (isinstance(n, int) and n < 2):
                    dve.wait_ge(o_st[par], 16 * half(t, par, 0))
                dve.tensor_tensor(o_sb[par][:], x_in[par][:], bank[7][:].rearrange("p (n e) -> p n e", e=E), ALU.add).then_inc(o_base, 1)
                dve.wait_ge(got[par], 16 * 2 * NB * (half(t, par, 0) + 1))
                dve.wait_ge(o_base, n + 1)
                for c in range(2):
                    for k in range(NB):
                        o = o_sb[par][:, k, :]
                        ins = dve.scalar_tensor_tensor(out=o, in0=picked[par][:, c, k, :], scalar=topw[:, c, bass.ds(n * NB + k, 1)],
                                                       in1=o, op0=ALU.mult, op1=ALU.add)
                        if k == NB - 1:
                            if c == 0:
                                ins.then_inc(o_half, 1)
                                dve.wait_ge(o_half, n + 1)
                            else:
                                ins.then_inc(o_sum, 1)

            shared_hidden(0, 0)
            shared_hidden(1, 1)
            with dve.Fori(1, B // 2) as i:
                for par in range(2):
                    shared_hidden(("r", i), par)
                    add_up(*shift(("r", i), par, -2))
            add_up(B - 2, 0)
            add_up(B - 1, 1)


_OUTS = [((B, S, E), "float32")]


def kernel(L0_attn_x, L0_attn_W1, L0_attn_b1, L0_attn_Wp, L0_attn_bp, L0_ffn_gate_w, L0_ffn_expert_gate,
           L0_ffn_expert_up, L0_ffn_expert_down, L0_ffn_shared_gate, L0_ffn_shared_up, L0_ffn_shared_down):
    import numpy as np
    import concourse.bacc as bacc
    from concourse.bass_utils import run_bass_kernel_spmd

    w1 = np.asarray(L0_attn_W1).reshape(E, H, 3, D).transpose(0, 2, 1, 3).reshape(E, 3, E)
    b1 = np.asarray(L0_attn_b1).reshape(H, 3, D).transpose(0, 2, 1).reshape(E, 3)
    e_gu = np.stack([np.asarray(L0_ffn_expert_gate), np.asarray(L0_ffn_expert_up)], axis=1).transpose(3, 0, 1, 2)
    s_gu = np.stack([np.asarray(L0_ffn_shared_gate), np.asarray(L0_ffn_shared_up)], axis=0).transpose(2, 0, 1)
    laid_out = {
        "x": np.asarray(L0_attn_x), "w_qkv": w1, "b_qkv": b1, "w_out": np.asarray(L0_attn_Wp),
        "b_out": np.asarray(L0_attn_bp).reshape(E, 1), "gate_w": np.asarray(L0_ffn_gate_w).transpose(1, 0),
        "e_gu": e_gu, "e_down": np.asarray(L0_ffn_expert_down).transpose(0, 2, 1),
        "s_gu": s_gu, "s_down": np.asarray(L0_ffn_shared_down).transpose(1, 0),
    }
    nc = bacc.Bacc("TRN2", target_bir_lowering=False, num_devices=1)
    arrays, args = {}, {}
    for name, a in laid_out.items():
        a = np.ascontiguousarray(a)
        arrays[f"in_{name}"] = a
        args[name] = nc.dram_tensor(f"in_{name}", a.shape, mybir.dt.from_np(a.dtype), kind="ExternalInput").ap()
    (shape, dtype), = _OUTS
    out = nc.dram_tensor("out_0", shape, mybir.dt.from_np(np.dtype(dtype)), kind="ExternalOutput").ap()
    nc.disable_value_cache = True
    attention_moe_kernel(nc, **args, out=out)
    return run_bass_kernel_spmd(nc, [arrays], core_ids=[0]).results[0]["out_0"]
```

```python
from contextlib import ExitStack

import concourse.bass as bass
from concourse import mybir

F32 = mybir.dt.float32
F32R = mybir.dt.float32r
BF16 = mybir.dt.bfloat16
I32 = mybir.dt.int32
U32 = mybir.dt.uint32
ALU = mybir.AluOpType
ACT = mybir.ActivationFunctionType
AX = mybir.AxisListType

P = 128
E = 128
B, S = 8, 512
T = B * S
H = 16
D = E // H
NB = S // P
NT = T // P
HG = 4
NG = H // HG
NX = 8
F = 352
FC = 3
FR = F - 2 * P
NTILE = 2 * T // P + NX
SLOTS = NTILE * P
NPAIR = NTILE // 2
PR = 2 * P
SCALE = float(D) ** -0.5
EPS = 1e-5
NEG = -1.0e30

NU = 11
ST_KB = [0, 0, 0, 0, 1, 1, 1, 1, 2, 2, 3]
ST_HEADS = [[0], [1], [2], [3], [0], [1], [2], [3], [0, 1], [2, 3], [0, 1, 2, 3]]
MX_QB = [0, 1, 1, 2, 2, 2, 2, 3, 3, 3, 3]
MX_HEADS = [[0, 1, 2, 3], [0, 1], [2, 3], [0], [1], [2], [3], [0], [1], [2], [3]]
UB = NG * NU
AHEAD = NU + 6
AV_UNITS = [4, 8, 10, 11]
PRIME_AO, PRIME_T, PRIME_F, PRIME_ATOUT = 2, 2, 1, 1


def attention_moe_kernel(nc, x, w_qkv, b_qkv, w_out, b_out, gate_w, e_gu, e_down, s_gu, s_down, out):
    x_tok = x.rearrange("b s e -> (b s) e")
    out_tok = out.rearrange("b s e -> (b s) e")

    q_rows = nc.dram_tensor("q_rows", [H, 3 * D, S], F32, kind="Internal").ap()
    k_rows = nc.dram_tensor("k_rows", [H, 3 * D, S], F32, kind="Internal").ap()
    sorted_x = nc.dram_tensor("sorted_x", [SLOTS, E], F32, kind="Internal").ap()
    sorted_y = nc.dram_tensor("sorted_y", [SLOTS, E], F32, kind="Internal").ap()
    att_T = nc.dram_tensor("att_T", [B, E, S], F32, kind="Internal").ap()

    with ExitStack() as ctx:
        def sb(name, shape, dt=F32, stack=ctx):
            return stack.enter_context(nc.sbuf_tensor(name, shape, dt))

        def ps(name, shape, stack=ctx):
            return stack.enter_context(nc.psum_tensor(name, shape, F32))

        def sem(name):
            return ctx.enter_context(nc.semaphore(name))

        ident = sb("ident", [P, P])
        ident_bf = sb("ident_bf", [P, P], BF16)
        mask_kq = sb("mask_kq", [P, HG, P], BF16)
        mask_qk = sb("mask_qk", [P, HG, P], BF16)
        before = sb("before", [P, P], BF16)
        ones_bf = sb("ones_bf", [P, P], BF16)
        expert_no = sb("expert_no", [P, NX])
        ones_f = sb("ones_f", [P, NX])
        tile_start = sb("tile_start", [1, NTILE])
        not_first = sb("not_first", [P, NX, NT])
        wqkv = sb("wqkv", [P, 3, E])
        bqkv = sb("bqkv", [P, 3])
        wout = sb("wout", [P, E])
        bout = sb("bout", [P, 1])
        gate = sb("gate", [P, NX])
        sgu = sb("sgu", [P, 2, F])
        sdn = sb("sdn", [P, FC, E])
        xnT = sb("xnT", [P, T])
        xn_rows = sb("xn_rows", [P, NT, E])
        slot_idx = sb("slot_idx", [P, 2, NT], U32)
        topw = sb("topw", [P, 2, NT])
        columns = sb("columns", [1, NPAIR + 2, 4], I32)
        lg = sb("lg", [P, NT, NX])
        bn = sb("bn", [P, NT, 6])
        mv = sb("mv", [P, NT, 2])
        var = sb("var", [P, NT])
        std = sb("std", [P, NT])
        rstd = sb("rstd", [P, NT])
        newton = sb("newton", [P, NT])
        primed = sb("primed", [P, 6])

        attn = ExitStack()
        q_bd, k_st = [], []
        for i in range(2):
            q_bd.append(sb(f"q_bd{i}", [P, H, S], F32R, attn))
            k_st.append(sb(f"k_st{i}", [P, NG, S], F32R, attn))
        v32 = [sb(f"v32_{i}", [P, NB, H, 32], F32, attn) for i in range(2)]
        q_hi = sb("q_hi", [P, S], F32R, attn)
        q_lo = sb("q_lo", [P, S], F32R, attn)
        k_hi = sb("k_hi", [P, S], F32R, attn)
        k_lo = sb("k_lo", [P, S], F32R, attn)
        vT = sb("vT", [P, S], F32, attn)
        av_sb = [sb(f"av_sb{i}", [P, S], F32, attn) for i in range(2)]
        a_tok = sb("a_tok", [P, NB, E], F32, attn)
        a_T = sb("a_T", [P, S], F32, attn)
        neg_max = sb("neg_max", [P, NG, NB, HG], F32, attn)
        m_row = [sb(f"m_row{g}", [HG, S], F32R, attn) for g in range(NG)]
        one_row = sb("one_row", [1, S], F32, attn)
        inv_sum = sb("inv_sum", [P, NB * HG], F32, attn)

        logit = sb("logit", [P, NT, NX], F32, attn)
        prob = sb("prob", [P, NT, NX], F32, attn)
        cand = sb("cand", [P, NT, NX], F32, attn)
        hot = [sb(f"hot{c}", [P, NT, NX], F32, attn) for c in range(2)]
        hot_bf = sb("hot_bf", [P, NT, NX], BF16, attn)
        rank = sb("rank", [P, NT, NX], F32, attn)
        total = sb("total", [P, NX, NT], F32, attn)
        incl = sb("incl", [P, NX, NT], F32, attn)
        slot = sb("slot", [P, NT, NX], F32, attn)
        best = [sb(f"best{c}", [P, NT], F32, attn) for c in range(2)]
        pick = sb("pick", [P, NT], F32, attn)
        slot_f = sb("slot_f", [P, 2, NT], F32, attn)
        rows_i = sb("rows_i", [P, NX], I32, attn)
        rows_f = sb("rows_f", [P, NX], F32, attn)
        end_row = sb("end_row", [P, NX], F32, attn)
        base_row = sb("base_row", [P, NX], F32, attn)
        past = sb("past", [1, NTILE, NX], F32, attn)
        tile_f = sb("tile_f", [1, NTILE], F32, attn)
        first = ExitStack()
        x_all = sb("x_all", [P, NT, E], F32, first)
        first.close()
        probs = sb("probs", [P, NU, S], F32, attn)
        attn.close()

        ffn = ExitStack()
        egu = sb("egu", [P, NX, 2, F], F32, ffn)
        edn = sb("edn", [P, NX, FC, E], F32, ffn)
        sb("rest_of_batch_buffers", [P, (H + NG) * S - NX * (2 * F + FC * E)], F32, ffn)
        xg = [sb(f"xg{i}", [P, 2, E], F32, ffn) for i in range(2)]
        xgT = [sb(f"xgT{i}", [P, 2, P], F32, ffn) for i in range(2)]
        sg = sb("sg", [P, 2, F], F32, ffn)
        hid = sb("hid", [P, 2, F], F32, ffn)
        hidT = [sb(f"hidT{i}", [P, FC, 2, P], F32, ffn) for i in range(2)]
        y_sb = [sb(f"y_sb{i}", [P, 2, E], F32, ffn) for i in range(2)]
        s_sig = sb("s_sig", [P, FC, S], F32, ffn)
        s_hid = [sb(f"s_hid{i}", [P, FC, S], F32, ffn) for i in range(2)]
        a_in = [sb(f"a_in{i}", [P, S], F32, ffn) for i in range(2)]
        x_in = [sb(f"x_in{i}", [P, NB, E], F32, ffn) for i in range(2)]
        resT = sb("resT", [P, S], F32, ffn)
        picked = [sb(f"picked{i}", [P, 2, NB, E], F32, ffn) for i in range(2)]
        o_sb = [sb(f"o_sb{i}", [P, NB, E], F32, ffn) for i in range(2)]
        ffn.close()

        bank = [ps(f"bank{i}", [P, S]) for i in range(8)]
        st_bank, mx_bank, av_bank = bank[0:2], bank[2:4], bank[4:6]
        row_bank, proj_bank = bank[6], bank[7]

        x_ld = [sem(f"x_ld{i}") for i in range(4)]
        w_early, w_late, egu_ld = sem("w_early"), sem("w_late"), sem("egu_ld")
        consts, cleared, ones_set = sem("consts"), sem("cleared"), sem("ones_set")
        fill_done = sem("fill_done")
        stats, std_done = sem("stats"), sem("std_done")
        vec_p, stat1, o_half = sem("vec_p"), sem("stat1"), sem("o_half")
        xn_done, xT_done, xnT_done = sem("xn_done"), sem("xT_done"), sem("xnT_done")
        lg_done, lg_kept = sem("lg_done"), sem("lg_kept")
        vec = sem("vec")
        z_ready, e_ready, hot_ready, count_done, counts_kept, routed = (
            sem(n) for n in ("z_ready", "e_ready", "hot_ready", "count_done", "counts_kept", "routed"))
        scattered = sem("scattered")
        qk_proj, qk_hi, qk_split = sem("qk_proj"), sem("qk_hi"), sem("qk_split")
        q_wr, k_wr = sem("q_wr"), sem("k_wr")
        qk_ld = [sem(f"qk_ld{i}") for i in range(2)]
        v_proj, v_biased, v_tr, v_ready = sem("v_proj"), sem("v_biased"), sem("v_tr"), sem("v_ready")
        mx_done, red_done, m_tr, m_ready = sem("mx_done"), sem("red_done"), sem("m_tr"), sem("m_ready")
        m_ld = [sem(f"m_ld{g}") for g in range(NG)]
        st_done, exp_done, av_done, av_out, t_done = (sem(n) for n in ("st_done", "exp_done", "av_done", "av_out", "t_done"))
        inv_done, a_done, f_done, aT_ready, aT_st = (sem(n) for n in ("inv_done", "a_done", "f_done", "aT_ready", "aT_st"))
        xg_ld = [sem(f"xg_ld{i}") for i in range(2)]
        y_st = [sem(f"y_st{i}") for i in range(2)]
        xg_tr, xgT_done, gu_done, sg_done, hid_done, hid_tr, hidT_done, y_done, y_out = (
            sem(n) for n in ("xg_tr", "xgT_done", "gu_done", "sg_done", "hid_done", "hid_tr", "hidT_done", "y_done", "y_out"))
        sgu_done, ssig_done, shid_done, res_done, res_out, o_tr, o_base, o_sum = (
            sem(n) for n in ("sgu_done", "ssig_done", "shid_done", "res_done", "res_out", "o_tr", "o_base", "o_sum"))
        s_ld = [sem(f"s_ld{i}") for i in range(2)]
        got = [sem(f"got{i}") for i in range(2)]
        o_st = [sem(f"o_st{i}") for i in range(2)]

        block = ctx.enter_context(nc.Block())

        def half(b, par, n):
            if isinstance(b, int):
                return (b + n) // 2
            return b[1] + (par + n) // 2

        def at(b, par):
            return b if isinstance(b, int) else 2 * b[1] + par

        def shift(t, par, d):
            if isinstance(t, int):
                return t + d, (t + d) % 2
            return ("r", t[1] + (par + d) // 2), (par + d) % 2

        def loads_of(t):
            return t.rearrange("(g j) r t -> j r g t", j=HG)

        @block.sync
        def _(sp):
            for i in range(4):
                n = T // 4
                sp.dma_start(x_all[:, i * NT // 4:(i + 1) * NT // 4, :],
                             x_tok[i * n:(i + 1) * n, :].rearrange("(n p) e -> p n e", p=P)).then_inc(x_ld[i], 16)
                if i == 0:
                    sp.dma_start(gate[:], gate_w).then_inc(w_early, 16)
                    sp.dma_start(wqkv[:], w_qkv).then_inc(w_early, 16)
                    sp.dma_start(bqkv[:], b_qkv).then_inc(w_early, 16)
            sp.wait_ge(cleared, 3)
            sp.wait_ge(ones_set, 1)
            for par in range(2):
                for g in range(NG):
                    sp.dma_start(k_st[par][P - 1:P, g, :].bitcast(F32), one_row[:]).then_inc(w_late, 16)

            def split_rows_out(b, par):
                n = at(b, par)
                for c, (hi, lo, rows, done) in enumerate(((q_hi, q_lo, q_rows, q_wr), (k_hi, k_lo, k_rows, k_wr))):
                    sp.wait_ge(qk_split, sp.snap(2 * n + c + 1))
                    order = (hi, hi, lo) if c == 0 else (hi, lo, hi)
                    for r in range(3):
                        sp.dma_start(rows[:, r * D:(r + 1) * D, :], order[r][:].bitcast(F32)).then_inc(done, 16)

            def split_rows_in(b, par):
                n = at(b, par)
                sp.wait_ge(q_wr, sp.snap(48 * (n + 1)))
                sp.wait_ge(k_wr, sp.snap(48 * (n + 1)))
                for j in range(HG):
                    strip = slice(32 * j, 32 * j + 3 * D)
                    sp.dma_start(q_bd[par][strip, j:H:HG, :].bitcast(F32), loads_of(q_rows)[j]).then_inc(qk_ld[par], 16)
                    sp.dma_start(k_st[par][strip, :, :].bitcast(F32), loads_of(k_rows)[j]).then_inc(qk_ld[par], 16)

            def max_row_in(b, par, g):
                n = at(b, par)
                sp.wait_ge(m_ready, sp.snap(NG * n + g + 1))
                sp.dma_start(q_bd[par][P - 1:P, HG * g:HG * (g + 1), :].bitcast(F32), m_row[g][:].bitcast(F32)).then_inc(m_ld[g], 16)

            split_rows_out(0, 0)
            split_rows_in(0, 0)
            half_rows = SLOTS // P // 2 * E
            for i in range(2):
                sp.dma_start(sorted_x.rearrange("(p k) e -> p (k e)", p=P)[:, i * half_rows:(i + 1) * half_rows],
                             q_bd[1][:, 0:half_rows // S, :].bitcast(F32).rearrange("p h s -> p (h s)")).then_inc(fill_done, 16)
            sp.wait_ge(qk_ld[0], 16 * 2 * HG)
            split_rows_out(1, 1)
            sp.wait_ge(fill_done, 32)
            for g in range(NG - 1):
                max_row_in(0, 0, g)
                if g == 0:
                    split_rows_in(1, 1)
            sp.dma_start(wout[:], w_out).then_inc(w_late, 16)
            sp.dma_start(bout[:], b_out).then_inc(w_late, 16)
            sp.dma_start(sgu[:], s_gu).then_inc(w_late, 16)
            sp.dma_start(sdn[:, 0:2, :], s_down[0:2 * P, :].rearrange("(c f) e -> f c e", f=P)).then_inc(w_late, 16)
            sp.dma_start(sdn[0:FR, 2, :], s_down[2 * P:F, :]).then_inc(w_late, 16)

            def attention(b, par, more, more2):
                n = at(b, par)
                nxt, _ = shift(b, par, 1)
                nxt2, _ = shift(b, par, 2)
                max_row_in(b, par, NG - 1)
                if more:
                    max_row_in(nxt, 1 - par, 0)
                if more2:
                    sp.wait_ge(qk_ld[1 - par], sp.snap(16 * 2 * HG * (half(b, par, 1) + 1)))
                    split_rows_out(nxt2, par)
                if more:
                    max_row_in(nxt, 1 - par, 1)
                if more2:
                    sp.wait_ge(st_done, sp.snap(UB * (n + 1)))
                    split_rows_in(nxt2, par)
                if more:
                    max_row_in(nxt, 1 - par, 2)
                dst = sp.snap(n * E) if not isinstance(n, int) else n * E
                sp.wait_ge(aT_ready, sp.snap(n + 1 + PRIME_ATOUT))
                sp.dma_start(att_T.rearrange("b e s -> (b e) s")[bass.ds(dst, E), :], a_T[:]).then_inc(aT_st, 16)

            with sp.Fori(0, B // 2 - 1) as i:
                for par in range(2):
                    attention(("r", i), par, True, True)
            attention(B - 2, 0, True, False)
            sp.wait_ge(st_done, UB * (B - 1))
            sp.dma_start(egu[:], e_gu).then_inc(egu_ld, 16)
            for c in range(2):
                sp.dma_start(edn[:, :, c, :], e_down[:, c * P:(c + 1) * P, :].rearrange("x f e -> f x e")).then_inc(egu_ld, 16)
            sp.dma_start(edn[0:FR, :, 2, :], e_down[:, 2 * P:F, :].rearrange("x f e -> f x e")).then_inc(egu_ld, 16)
            attention(B - 1, 1, False, False)

            sp.wait_ge(scattered, 16 * 2 * NT)
            sp.wait_ge(f_done, B + PRIME_F)
            sp.wait_ge(aT_st, 16 * (B + 1))

            def pair_rows(t, n):
                start = sp.snap(n * PR) if not isinstance(n, int) else n * PR
                return t[bass.ds(start, PR), :].rearrange("(k p) e -> p k e", p=P)

            for t in range(2):
                sp.dma_start(xg[t][:], pair_rows(sorted_x, t)).then_inc(xg_ld[t], 16)

            def expert_pair(t, par, load, store):
                n = at(t, par)
                if load:
                    sp.wait_ge(xg_tr, sp.snap(n + 1))
                    sp.dma_start(xg[par][:], pair_rows(sorted_x, n + 2)).then_inc(xg_ld[par], 16)
                if store:
                    sp.wait_ge(y_out, sp.snap(n - 1))
                    sp.dma_start(pair_rows(sorted_y, n - 2), y_sb[par][:]).then_inc(y_st[par], 16)

            for t in range(2):
                expert_pair(t, t, True, False)
            with sp.Fori(1, NPAIR // 2 - 1) as i:
                for par in range(2):
                    expert_pair(("r", i), par, True, True)
            for t in range(NPAIR - 2, NPAIR + 2):
                expert_pair(t, t % 2, False, True)

            def last_in(b, par):
                n = at(b, par)
                src = n * E if isinstance(n, int) else sp.snap(n * E)
                tok = n * S if isinstance(n, int) else sp.snap(n * S)
                sp.dma_start(a_in[par][:], att_T.rearrange("b e s -> (b e) s")[bass.ds(src, E), :]).then_inc(s_ld[par], 16)
                sp.dma_start(x_in[par][:], x_tok[bass.ds(tok, S), :].rearrange("(n p) e -> p n e", p=P)).then_inc(s_ld[par], 16)

            def last_out(b, par):
                n = at(b, par)
                tok = n * S if isinstance(n, int) else sp.snap(n * S)
                sp.wait_ge(o_sum, sp.snap(n + 1))
                sp.dma_start(out_tok[bass.ds(tok, S), :].rearrange("(n p) e -> p n e", p=P), o_sb[par][:]).then_inc(o_st[par], 16)

            for b in range(2):
                last_in(b, b)
            with sp.Fori(0, B // 2 - 1) as i:
                for par in range(2):
                    last_out(("r", i), par)
                    last_in(("r", i + 1), par)
            for par in range(2):
                last_out(B - 2 + par, par)
            for par in range(2):
                sp.wait_ge(o_st[par], 16 * (B // 2))
                sp.wait_ge(y_st[par], 16 * (NPAIR // 2))

        @block.gpsimd
        def _(pool):
            pool.memset(ident[:], 0.0).then_inc(vec_p, 1)
            pool.wait_ge(vec_p, 1)
            pool.affine_select(out=ident[:], in_=ident[:], compare_op=ALU.not_equal, fill=1.0, base=0,
                               pattern=[[-1, P]], channel_multiplier=1).then_inc(consts, 1)
            pool.wait_ge(consts, 1)
            pool.tensor_copy(ident_bf[:], ident[:]).then_inc(consts, 1)
            for i in range(2):
                pool.memset(q_bd[i][:].bitcast(F32), 0.0).then_inc(cleared, 1)
                if i == 0:
                    for k in range(2):
                        ins = pool.memset(k_st[k][:].bitcast(F32), 0.0)
                    ins.then_inc(cleared, 1)
            pool.memset(mask_kq[:], 0.0)
            pool.memset(mask_qk[:], 0.0)
            pool.memset(before[:], 1.0)
            for i in range(2):
                pool.memset(v32[i][:], 0.0)
            pool.memset(not_first[:], 1.0)
            pool.memset(ones_f[:], 1.0)
            pool.memset(ones_bf[:], 1.0).then_inc(vec_p, 1)
            pool.wait_ge(vec_p, 2)
            pool.affine_select(out=mask_kq[:], in_=mask_kq[:], compare_op=ALU.is_ge, fill=NEG, base=0,
                               pattern=[[0, HG], [1, P]], channel_multiplier=-1)
            pool.affine_select(out=mask_qk[:], in_=mask_qk[:], compare_op=ALU.is_ge, fill=NEG, base=0,
                               pattern=[[0, HG], [-1, P]], channel_multiplier=1)
            pool.affine_select(out=before[:], in_=before[:], compare_op=ALU.is_ge, fill=0.0, base=-1,
                               pattern=[[1, P]], channel_multiplier=-1)
            for i in range(2):
                pool.memset(v32[i][:, :, :, D:D + 1], 1.0)
            pool.memset(not_first[:, :, 0:1], 0.0)
            pool.iota(expert_no[:], pattern=[[1, NX]], base=0, channel_multiplier=0, allow_small_or_imprecise_dtypes=True)
            pool.iota(tile_start[:], pattern=[[P, NTILE]], base=0, channel_multiplier=0,
                      allow_small_or_imprecise_dtypes=True).then_inc(consts, 1)
            pool.wait_ge(routed, 2)
            pool.wait_ge(fill_done, 32)
            for n in range(NT):
                for c in range(2):
                    pool.indirect_dma_start(sorted_x, bass.IndirectOffsetOnAxis(ap=slot_idx[:, c, n:n + 1], axis=0),
                                            xn_rows[:, n, :], None).then_inc(scattered, 16)
            for par in range(2):
                pool.wait_ge(y_st[par], 16 * (NPAIR // 2))
            for b in range(B):
                par = b % 2
                if b >= 2:
                    pool.wait_ge(o_sum, b - 1)
                for n in range(NB):
                    for c in range(2):
                        pool.indirect_dma_start(picked[par][:, c, n, :], None, sorted_y,
                                                bass.IndirectOffsetOnAxis(ap=slot_idx[:, c, b * NB + n:b * NB + n + 1], axis=0)
                                                ).then_inc(got[par], 16)

        @block.tensor
        def _(pe):
            def project(n, c, done):
                pe.matmul(proj_bank[:], wqkv[:, c, :], xnT[:, bass.ds(n * S, S)], start=True, stop=True).then_inc(done, 1)

            def v_transposes(n):
                pe.wait_ge(v_biased, n + 1)
                for k in range(NB):
                    ins = pe.transpose(proj_bank[:, k * P:(k + 1) * P], vT[:, k * P:(k + 1) * P], ident[:])
                ins.then_inc(v_tr, 1)

            def max_unit(n, par, u):
                g, k = divmod(u, NU)
                qb, heads = MX_QB[k], MX_HEADS[k]
                w = (qb + 1) * P
                dst = mx_bank[u % 2]
                if isinstance(n, int) and n == 0:
                    dst = first_mx_bank[u % 3]
                    if u >= 3:
                        pe.wait_ge(red_done, u - 2)
                else:
                    pe.wait_ge(red_done, n * UB + u - 1)
                for i, j in enumerate(heads):
                    pe.matmul(dst[:, i * w:(i + 1) * w], q_bd[par][0:P - 1, HG * g + j, qb * P:(qb + 1) * P],
                              k_st[par][0:P - 1, g, 0:w], start=(i == 0), stop=False, skip_group_check=True)
                nh = len(heads)
                diag = dst[:, 0:nh * w].rearrange("p (h w) -> p h w", h=nh)[:, :, qb * P:w]
                pe.matmul(diag, ident_bf[:], mask_qk[:, 0:nh, :], start=False, stop=True, skip_group_check=True).then_inc(mx_done, 1)

            def max_transposes(n, g):
                pe.wait_ge(red_done, n * UB + NU * (g + 1))
                for qb in range(NB):
                    ins = pe.transpose(row_bank[0:HG, qb * P:(qb + 1) * P], neg_max[:, g, qb, :], ident[:])
                ins.then_inc(m_tr, 1)

            def score_unit(n, par, g, u):
                kb, heads = ST_KB[u], ST_HEADS[u]
                w = S - kb * P
                dst = st_bank[(g * NU + u) % 2]
                nh = len(heads)
                if not (isinstance(n, int) and n * UB + g * NU + u < 2):
                    pe.wait_ge(exp_done, n * UB + g * NU + u - 1)
                h0 = HG * g + heads[0]
                pe.matmul(dst[:, 0:nh * w], k_st[par][:, g, kb * P:(kb + 1) * P], q_bd[par][:, h0:h0 + nh, kb * P:S],
                          start=True, stop=False, skip_group_check=True)
                diag = dst[:, 0:nh * w].rearrange("p (h w) -> p h w", h=nh)[:, :, 0:P]
                pe.matmul(diag, ident_bf[:], mask_kq[:, 0:nh, :], start=False, stop=True, skip_group_check=True).then_inc(st_done, 1)

            def value_bundle(n, par, g, kb):
                pe.wait_ge(exp_done, n * UB + g * NU + AV_UNITS[kb])
                dst = av_bank[g % 2]
                if kb == 0:
                    pe.wait_ge(av_out, n * NG + g - 1 + PRIME_AO)
                for j in range(HG):
                    u, lo = [(j, 0), (4 + j, 0), (8 + j // 2, j % 2 * 2 * P), (10, j * P)][kb]
                    w = S - kb * P
                    ins = pe.matmul(dst[32 * j:32 * j + 32, kb * P:S], v32[par][:, kb, HG * g + j, :], probs[:, u, lo:lo + w],
                                    start=(kb == 0), stop=(kb == NB - 1), skip_group_check=True)
                ins.then_inc(av_done, 1)

            def to_tokens(n, g, more):
                pe.wait_ge(av_out, n * NG + g + 1 + PRIME_AO)
                if more or g == 0:
                    pe.wait_ge(m_ready, (n + 1) * NG + g)
                else:
                    pe.wait_ge(a_done, n * NG + g)
                for k in range(NB):
                    ins = pe.transpose(row_bank[:, k * P:(k + 1) * P], av_sb[g % 2][:, k * P:(k + 1) * P], ident[:])
                ins.then_inc(t_done, 1)

            def to_features(n):
                pe.wait_ge(a_done, (n + 1) * NG)
                for k in range(NB):
                    ins = pe.transpose(row_bank[:, k * P:(k + 1) * P], a_tok[:, k, :], ident[:])
                ins.then_inc(f_done, 1)

            def x_transposes(b):
                pe.wait_ge(xn_done, b + 1)
                if b >= 2:
                    pe.wait_ge(xnT_done, b - 1)
                for n in range(NB):
                    ins = pe.transpose(bank[b % 2][:, n * P:(n + 1) * P], xn_rows[:, b * NB + n, :], ident[:])
                ins.then_inc(xT_done, 1)

            def router(b):
                pe.wait_ge(xnT_done, b + 1)
                for n in range(b * NB, (b + 1) * NB):
                    ins = pe.matmul(lg_bank[:, n * NX:(n + 1) * NX], xnT[:, n * P:(n + 1) * P], gate[:],
                                    start=(n == 0), stop=True, skip_group_check=True)
                ins.then_inc(lg_done, 1)

            def first_project(n, c):
                if n or c:
                    pe.wait_ge(qk_split, 2 * n + c)
                pe.wait_ge(xnT_done, n + 1)
                project(n, c, v_proj if c == 2 else qk_proj)

            lg_bank = bank[5]
            first_mx_bank = [bank[2], bank[3], bank[5]]
            pe.wait_ge(consts, 3)
            pe.wait_ge(w_early, 48)
            x_transposes(0)
            first_project(0, 0)
            x_transposes(1)
            x_transposes(2)
            first_project(0, 1)
            x_transposes(3)
            for b in range(3):
                router(b)
            for b in range(4, 6):
                x_transposes(b)
                router(b - 1)
            first_project(1, 0)
            for b in range(6, 8):
                x_transposes(b)
                router(b - 1)
            first_project(1, 1)
            router(B - 1)
            pe.wait_ge(qk_split, 4)
            project(0, 2, v_proj)
            v_transposes(0)
            pe.wait_ge(hot_ready, 1)
            flat = hot_bf[:].rearrange("p n x -> p (n x)")
            pe.matmul(bank[0][:, 0:NT * NX], before[:], flat, start=True, stop=True, skip_group_check=True)
            pe.matmul(bank[0][:, NT * NX:2 * NT * NX], ones_bf[:], flat, start=False, stop=True, skip_group_check=True).then_inc(count_done, 1)

            pe.wait_ge(qk_ld[0], 16 * 2 * HG)
            pe.wait_ge(w_late, 16 * NG)
            pe.wait_ge(lg_kept, 1)
            for u in range(NU):
                max_unit(0, 0, u)
            max_transposes(0, 0)
            for u in range(NU, AHEAD):
                max_unit(0, 0, u)
            pe.wait_ge(m_ld[0], 16)
            pe.wait_ge(v_ready, 1)
            pe.wait_ge(counts_kept, 2)
            for u in range(NU):
                score_unit(0, 0, 0, u)
                for v in range(AHEAD + 3 * u, min(AHEAD + 3 * u + 3, UB)):
                    max_unit(0, 0, v)
                if u == 3:
                    pe.wait_ge(m_ready, 1)
                    max_transposes(0, 1)
                if u == 6:
                    value_bundle(0, 0, 0, 0)
                if u == 7:
                    pe.wait_ge(m_ready, 2)
                    max_transposes(0, 2)
                if u == 10:
                    value_bundle(0, 0, 0, 1)
            pe.wait_ge(m_ready, 3)

            def attention(b, par, more, more2):
                n = at(b, par)
                for k in range(NG):
                    g = (k + 1) % NG
                    sn, spar = (n, par) if g else (n + 1, 1 - par)
                    for u in range(NU):
                        if g or more:
                            if u == 0:
                                pe.wait_ge(m_ld[g], 16 * (sn + 1))
                                if g == 0:
                                    pe.wait_ge(v_ready, sn + 1)
                            score_unit(sn, spar, g, u)
                        if more:
                            if k == 0 and u == 0:
                                pe.wait_ge(qk_ld[1 - par], 16 * 2 * HG * (half(b, par, 1) + 1))
                            max_unit(n + 1, 1 - par, k * NU + u)
                        if u == 1:
                            value_bundle(n, par, k, 2)
                        if u == 2:
                            value_bundle(n, par, k, 3)
                        if u == 3 and k == 0:
                            pe.wait_ge(aT_ready, n + PRIME_ATOUT)
                            max_transposes(n, NG - 1)
                        if u == 3 and k and more:
                            pe.wait_ge(a_done, n * NG + k)
                            max_transposes(n + 1, k - 1)
                        if u == 5:
                            to_tokens(n, k, more)
                        if u == 6 and (g or more):
                            value_bundle(sn, spar, g, 0)
                        if u == 8 and k == NG - 1:
                            to_features(n)
                        if u == 10 and (g or more):
                            value_bundle(sn, spar, g, 1)
                        s = k * NU + u
                        if more and s == 4:
                            pe.wait_ge(qk_split, 2 * (n + 2))
                            project(n + 1, 2, v_proj)
                        if more and s == 8:
                            v_transposes(n + 1)
                        if more2 and s == 13:
                            pe.wait_ge(v_ready, n + 2)
                            project(n + 2, 0, qk_proj)
                        if more2 and s == 18:
                            pe.wait_ge(qk_split, 2 * (n + 2) + 1)
                            project(n + 2, 1, qk_proj)

            with pe.Fori(0, B // 2 - 1) as i:
                for par in range(2):
                    attention(("r", i), par, True, True)
            attention(B - 2, 0, True, False)
            attention(B - 1, 1, False, False)

            g_bank, u_bank = bank[0:2], bank[2:4]
            xgT_bank, hidT_bank, y_bank = bank[4], bank[5:7], bank[7]
            pe.wait_ge(aT_ready, B + PRIME_ATOUT)
            pe.wait_ge(exp_done, B * UB)
            pe.wait_ge(egu_ld, 16 * 4)
            pe.wait_ge(w_late, 16 * (2 * NG + 5))

            def load_columns(step):
                clamped = "DVE clamps the expert before it multiplies"
                _, cols = nc.values_load_multi_w_load_instructions(
                    columns[0:1, bass.ds(step, 1), :].rearrange("o s c -> o (s c)"), engines=[mybir.EngineType.PE], min_val=0,
                    max_val=(NX - 1) * 2 * F, skip_runtime_bounds_check_because=clamped)
                return [c if k < 2 else nc.s_assert_within(c, 0, (NX - 1) * FC * E, skip_runtime_bounds_check_because=clamped)
                        for k, c in enumerate(cols)]

            def x_step(t, par):
                n = at(t, par)
                pe.wait_ge(xg_ld[par], 16 * (half(t, par, 0) + 1))
                for k in range(2):
                    ins = pe.transpose(xgT_bank[:, k * P:(k + 1) * P], xg[par][:, k, :], ident[:])
                ins.then_inc(xg_tr, 1)

            def gate_up(t, par, cols):
                pe.wait_ge(xgT_done, at(t, par) + 1)
                w = egu[:].rearrange("p x a f -> p (x a f)")
                for k in range(2):
                    pe.matmul(g_bank[k][:, 0:F], xgT[par][:, k, :], w[:, bass.ds(cols[k], F)], start=True, stop=True)
                    pe.matmul(u_bank[k][:, 0:F], xgT[par][:, k, :], w[:, bass.ds(cols[k] + F, F)], start=True, stop=True).then_inc(gu_done, 1)

            def down(t, par, cols):
                n = at(t, par)
                pe.wait_ge(hidT_done, n + 1)
                if not (isinstance(n, int) and n == 0):
                    pe.wait_ge(y_out, n)
                w = edn[:].rearrange("p x c e -> p (x c e)")
                for k in range(2):
                    for c in range(FC):
                        m = min(P, F - c * P)
                        ins = pe.matmul(y_bank[:, k * E:(k + 1) * E], hidT[par][0:m, c, k, :], w[0:m, bass.ds(cols[2 + k] + c * E, E)],
                                        start=(c == 0), stop=(c == FC - 1))
                ins.then_inc(y_done, 1)

            def hid_transposes(t, par):
                pe.wait_ge(hid_done, 2 * at(t, par) + 2)
                for k in range(2):
                    for c in range(FC):
                        m = min(P, F - c * P)
                        col = (c % 2 * 2 + k) * P
                        ins = pe.transpose(hidT_bank[c // 2][0:m, col:col + P], hid[:, k, c * P:c * P + m], ident[:])
                ins.then_inc(hid_tr, 1)

            def after_gate_up(t, par, has_next, has_t, has_1):
                if has_next or has_1:
                    cols = load_columns(at(t, par) + 1)
                if has_next:
                    x_step(*shift(t, par, 1))
                if has_1:
                    down(*shift(t, par, -1), cols)
                if has_t:
                    hid_transposes(t, par)
                if has_next:
                    gate_up(*shift(t, par, 1), cols)

            x_step(0, 0)
            gate_up(0, 0, load_columns(0))
            after_gate_up(0, 0, True, True, False)
            after_gate_up(1, 1, True, True, True)
            with pe.Fori(1, NPAIR // 2 - 1) as i:
                for par in range(2):
                    after_gate_up(("r", i), par, True, True, True)
            for t in range(NPAIR - 2, NPAIR + 1):
                after_gate_up(t, t % 2, t + 1 < NPAIR, t < NPAIR, True)

            res_bank, tok_bank = bank[6], bank[7]
            pe.wait_ge(y_out, NPAIR)

            def shared_up(t, par):
                n = at(t, par)
                for c in range(FC):
                    m = min(P, F - c * P)
                    if not (isinstance(n, int) and n == 0):
                        pe.wait_ge(shid_done, FC * (n - 1) + c + 1)
                    for a in range(2):
                        ins = pe.matmul(bank[2 * c + a][0:m, :], sgu[:, a, c * P:c * P + m], xnT[:, bass.ds(n * S, S)], start=True, stop=True)
                    ins.then_inc(sgu_done, 1)

            def shared_down(t, par):
                n = at(t, par)
                pe.wait_ge(s_ld[par], 32 * (half(t, par, 0) + 1))
                if not (isinstance(n, int) and n == 0):
                    pe.wait_ge(res_out, n)
                pe.matmul(res_bank[:], wout[:], a_in[par][:], start=True, stop=False)
                for c in range(FC):
                    m = min(P, F - c * P)
                    pe.wait_ge(shid_done, FC * n + c + 1)
                    ins = pe.matmul(res_bank[:], sdn[0:m, c, :], s_hid[par][0:m, c, :], start=False, stop=(c == FC - 1))
                ins.then_inc(res_done, 1)

            def back_to_tokens(t, par):
                n = at(t, par)
                pe.wait_ge(res_out, n + 1)
                if not (isinstance(n, int) and n == 0):
                    pe.wait_ge(o_base, n)
                for k in range(NB):
                    ins = pe.transpose(tok_bank[:, k * P:(k + 1) * P], resT[:, k * P:(k + 1) * P], ident[:])
                ins.then_inc(o_tr, 1)

            shared_up(0, 0)
            shared_up(1, 1)
            shared_down(0, 0)
            with pe.Fori(1, B // 2) as i:
                for par in range(2):
                    shared_up(("r", i), par)
                    back_to_tokens(*shift(("r", i), par, -2))
                    shared_down(*shift(("r", i), par, -1))
            back_to_tokens(B - 2, 0)
            shared_down(B - 1, 1)
            back_to_tokens(B - 1, 1)

        @block.scalar
        def _(act):
            def split_high(n, c):
                dst, wr = ((q_hi, q_wr), (k_hi, k_wr))[c]
                act.wait_ge(qk_proj, 2 * n + c + 1)
                if not (isinstance(n, int) and n == 0):
                    act.wait_ge(wr, 48 * n)
                act.activation(dst[:], proj_bank[:], ACT.Identity, bias=bqkv[:, c:c + 1]).then_inc(qk_hi, 1)

            def first_std(i):
                act.wait_ge(stats, i + 1)
                q = slice(i * NT // 4, (i + 1) * NT // 4)
                act.activation(std[:, q], var[:, q], ACT.Sqrt).then_inc(std_done, 1)

            def xT_out(b):
                act.wait_ge(xT_done, b + 1)
                act.activation(xnT[:, b * S:(b + 1) * S], bank[b % 2][:], ACT.Copy).then_inc(xnT_done, 1)

            act.wait_ge(w_early, 48)
            first_std(0)
            xT_out(0)
            first_std(1)
            split_high(0, 0)
            xT_out(1)
            first_std(2)
            xT_out(2)
            xT_out(3)
            split_high(0, 1)
            xT_out(4)
            first_std(3)
            for b in range(5, 8):
                xT_out(b)
            split_high(1, 0)
            split_high(1, 1)
            act.wait_ge(lg_done, B)
            act.activation(lg[:].rearrange("p n x -> p (n x)"), bank[5][:, 0:NT * NX], ACT.Copy).then_inc(lg_kept, 1)
            act.wait_ge(z_ready, 1)
            act.activation(prob[:], logit[:], ACT.Exp).then_inc(e_ready, 1)
            act.wait_ge(count_done, 1)
            both = bank[0][:].rearrange("p (a n x) -> p a n x", a=2, x=NX)
            act.activation(rank[:], both[:, 0], ACT.Copy).then_inc(counts_kept, 1)
            act.activation(total[:].rearrange("p x n -> p n x"), both[:, 1], ACT.Copy).then_inc(counts_kept, 1)

            def exp_unit(n, g, u):
                w = (S - ST_KB[u] * P) * len(ST_HEADS[u])
                act.wait_ge(st_done, n * UB + g * NU + u + 1)
                if u in (0, 4, 8, 10) and not (isinstance(n, int) and n + g == 0):
                    k = (0, 4, 8, 10).index(u)
                    act.wait_ge(av_done, (n * NG + g - 1) * NB + k + 1)
                act.activation(probs[:, u, 0:w], st_bank[(g * NU + u) % 2][:, 0:w], ACT.Exp, scale=SCALE).then_inc(exp_done, 1)

            def values_out(n, g):
                act.wait_ge(av_done, (n * NG + g + 1) * NB)
                act.wait_ge(t_done, n * NG + g - 1 + PRIME_T)
                act.activation(av_sb[g % 2][:], av_bank[g % 2][:], ACT.Copy).then_inc(av_out, 1)

            def attention(b, par, more, more2):
                n = at(b, par)
                for k in range(NG):
                    g = (k + 1) % NG
                    for u in range(NU):
                        if g or more:
                            exp_unit(n if g else n + 1, g, u)
                        if u == 3:
                            values_out(n, k)
                        s = k * NU + u
                        if more2 and s == 13:
                            split_high(n + 2, 0)
                        if more2 and s == 18:
                            split_high(n + 2, 1)

            for u in range(NU):
                exp_unit(0, 0, u)
            with act.Fori(0, B // 2 - 1) as i:
                for par in range(2):
                    attention(("r", i), par, True, True)
            attention(B - 2, 0, True, False)
            attention(B - 1, 1, False, False)

            g_bank, xgT_bank, y_bank = bank[0:2], bank[4], bank[7]

            def x_out(t, par):
                n = at(t, par)
                act.wait_ge(xg_tr, n + 1)
                if not (isinstance(n, int) and n < 2):
                    act.wait_ge(gu_done, 2 * n - 2)
                act.activation(xgT[par][:].rearrange("p k m -> p (k m)"), xgT_bank[:, 0:PR], ACT.Copy).then_inc(xgT_done, 1)

            def sigmoid_part(t, par):
                n = at(t, par)
                for k in range(2):
                    act.wait_ge(gu_done, 2 * n + k + 1)
                    if not (isinstance(n, int) and n < 1):
                        act.wait_ge(hid_done, 2 * n + k - 1)
                    act.activation(sg[:, k, :], g_bank[k][:, 0:F], ACT.Silu).then_inc(sg_done, 1)

            def result(t, par):
                n = at(t, par)
                act.wait_ge(y_done, n + 1)
                if not (isinstance(n, int) and n < 2):
                    act.wait_ge(y_st[par], 16 * half(t, par, 0))
                act.activation(y_sb[par][:].rearrange("p k e -> p (k e)"), y_bank[:, 0:2 * E], ACT.Copy).then_inc(y_out, 1)

            def expert_step(t, par, has_t, has_next, has_1):
                if has_t:
                    sigmoid_part(t, par)
                if has_next:
                    x_out(*shift(t, par, 1))
                if has_1:
                    result(*shift(t, par, -1))

            act.wait_ge(f_done, B + PRIME_F)
            act.wait_ge(aT_st, 16 * (B + 1))
            x_out(0, 0)
            expert_step(0, 0, True, True, False)
            expert_step(1, 1, True, True, True)
            with act.Fori(1, NPAIR // 2 - 1) as i:
                for par in range(2):
                    expert_step(("r", i), par, True, True, True)
            for t in range(NPAIR - 2, NPAIR + 1):
                expert_step(t, t % 2, t < NPAIR, t + 1 < NPAIR, True)

            def shared_sigmoid(t, par):
                n = at(t, par)
                for c in range(FC):
                    m = min(P, F - c * P)
                    act.wait_ge(sgu_done, FC * n + c + 1)
                    if not (isinstance(n, int) and n == 0):
                        act.wait_ge(shid_done, FC * (n - 1) + c + 1)
                    act.activation(s_sig[0:m, c, :], bank[2 * c][0:m, :], ACT.Silu).then_inc(ssig_done, 1)

            def result_out(t, par):
                n = at(t, par)
                act.wait_ge(res_done, n + 1)
                if not (isinstance(n, int) and n == 0):
                    act.wait_ge(o_tr, n)
                act.activation(resT[:], bank[6][:], ACT.Identity, bias=bout[:, 0:1]).then_inc(res_out, 1)

            shared_sigmoid(0, 0)
            with act.Fori(0, B // 2 - 1) as i:
                for par in range(2):
                    shared_sigmoid(("r", i + (par + 1) // 2), 1 - par)
                    result_out(("r", i), par)
            shared_sigmoid(B - 1, 1)
            result_out(B - 2, 0)
            result_out(B - 1, 1)

        @block.vector
        def _(dve):
            chain = [0]

            def link(ins):
                chain[0] += 1
                ins.then_inc(vec, 1)
                dve.wait_ge(vec, chain[0])

            dve.memset(one_row[:], 1.0).then_inc(ones_set, 1)
            link(dve.memset(columns[:], 0))
            for i, (s_, n_) in enumerate(((av_out, PRIME_AO), (t_done, PRIME_T), (f_done, PRIME_F), (aT_ready, PRIME_ATOUT), (aT_st, 16))):
                dve.memset(primed[:, i:i + 1], 0.0).then_inc(s_, n_)

            QT = NT // 4

            def block_stats(i):
                dve.wait_ge(x_ld[i], 16)
                for n in range(i * QT, (i + 1) * QT):
                    ins = dve.bn_stats(bn[:, n, :], x_all[:, n, :])
                ins.then_inc(stat1, 1)

            def variance(i):
                q = slice(i * QT, (i + 1) * QT)
                dve.wait_ge(stat1, i + 1)
                for n in range(i * QT, (i + 1) * QT):
                    ins = dve.bn_aggr(mv[:, n, :], bn[:, n, :])
                link(ins)
                dve.tensor_scalar(var[:, q], mv[:, q, 1], EPS, None, ALU.add).then_inc(stats, 1)

            def normal_rows(i):
                q = slice(i * QT, (i + 1) * QT)
                dve.wait_ge(std_done, i + 1)
                link(dve.reciprocal(rstd[:, q], std[:, q]))
                link(dve.scalar_tensor_tensor(out=newton[:, q], in0=rstd[:, q], scalar=-0.5, in1=rstd[:, q], op0=ALU.mult, op1=ALU.mult))
                link(dve.tensor_tensor(newton[:, q], newton[:, q], var[:, q], ALU.mult))
                link(dve.scalar_tensor_tensor(out=rstd[:, q], in0=newton[:, q], scalar=1.5, in1=rstd[:, q], op0=ALU.add, op1=ALU.mult))
                for n in range(i * QT, (i + 1) * QT):
                    ins = dve.tensor_scalar(xn_rows[:, n, :], x_all[:, n, :], mv[:, n, 0:1], rstd[:, n:n + 1], ALU.subtract, ALU.mult)
                    if n % NB == NB - 1:
                        ins.then_inc(xn_done, 1)

            def split_low(n, c):
                hi, lo, wr = ((q_hi, q_lo, q_wr), (k_hi, k_lo, k_wr))[c]
                dve.wait_ge(qk_hi, 2 * n + c + 1)
                if not (isinstance(n, int) and n == 0):
                    dve.wait_ge(wr, 48 * n)
                dve.scalar_tensor_tensor(out=lo[:], in0=proj_bank[:], scalar=bqkv[:, c:c + 1], in1=hi[:].bitcast(F32),
                                         op0=ALU.add, op1=ALU.subtract).then_inc(qk_split, 1)

            def value_bias(n):
                dve.wait_ge(v_proj, n + 1)
                if not (isinstance(n, int) and n == 0):
                    dve.wait_ge(v_tr, n)
                dve.tensor_scalar(vT[:], proj_bank[:], bqkv[:, 2:3], None, ALU.add).then_inc(v_biased, 1)

            def value_rows(n, par):
                dve.wait_ge(v_tr, n + 1)
                if not (isinstance(n, int) and n < 2):
                    dve.wait_ge(av_done, (n - 1) * NG * NB)
                dve.tensor_copy(v32[par][:].rearrange("p n h c -> p (n h) c")[:, :, 0:D],
                                proj_bank[:].rearrange("p (n d) -> p n d", d=D)).then_inc(v_ready, 1)

            dve.wait_ge(w_early, 48)
            block_stats(0)
            variance(0)
            block_stats(1)
            normal_rows(0)
            variance(1)
            block_stats(2)
            normal_rows(1)
            split_low(0, 0)
            variance(2)
            block_stats(3)
            normal_rows(2)
            split_low(0, 1)
            variance(3)
            normal_rows(3)
            split_low(1, 0)
            split_low(1, 1)
            value_bias(0)
            dve.wait_ge(consts, 3)
            value_rows(0, 0)

            each = [P, NT, NX]
            dve.wait_ge(lg_kept, 1)
            link(dve.tensor_reduce(pick[:], lg[:], AX.X, ALU.max))
            dve.tensor_tensor(logit[:], lg[:], pick[:, :, None].broadcast_to(each), ALU.subtract).then_inc(z_ready, 1)
            dve.wait_ge(e_ready, 1)
            link(dve.tensor_reduce(pick[:], prob[:], AX.X, ALU.add))
            link(dve.reciprocal(pick[:], pick[:]))
            link(dve.tensor_tensor(prob[:], prob[:], pick[:, :, None].broadcast_to(each), ALU.mult))
            for c in range(2):
                link(dve.tensor_reduce(best[c][:], prob[:], AX.X, ALU.max))
                link(dve.tensor_tensor(cand[:], prob[:], best[c][:, :, None].broadcast_to(each), ALU.is_equal))
                link(dve.scalar_tensor_tensor(out=cand[:], in0=cand[:], scalar=-float(NX * NX),
                                              in1=expert_no[:, None, :].broadcast_to(each), op0=ALU.mult, op1=ALU.add))
                link(dve.tensor_reduce(pick[:], cand[:], AX.X, ALU.min))
                link(dve.tensor_tensor(hot[c][:], cand[:], pick[:, :, None].broadcast_to(each), ALU.is_equal))
                if c == 0:
                    link(dve.scalar_tensor_tensor(out=prob[:], in0=hot[0][:], scalar=-4.0, in1=prob[:], op0=ALU.mult, op1=ALU.add))
            dve.tensor_tensor(hot_bf[:], hot[0][:], hot[1][:], ALU.add).then_inc(hot_ready, 1)
            link(dve.scalar_tensor_tensor(out=pick[:], in0=best[0][:], scalar=1e-20, in1=best[1][:], op0=ALU.add, op1=ALU.add))
            link(dve.reciprocal(pick[:], pick[:]))
            for c in range(2):
                link(dve.tensor_tensor(topw[:, c, :], best[c][:], pick[:], ALU.mult))
            def reduce_unit(n, u):
                g, k = divmod(u, NU)
                qb, heads = MX_QB[k], MX_HEADS[k]
                w, nh = (qb + 1) * P, len(heads)
                src = [bank[2], bank[3], bank[5]][u % 3] if isinstance(n, int) and n == 0 else mx_bank[u % 2]
                dve.wait_ge(mx_done, n * UB + u + 1)
                dve.tensor_reduce(neg_max[:, g, qb, heads[0]:heads[0] + nh],
                                  src[:, 0:nh * w].rearrange("p (h w) -> p h w", h=nh), AX.X, ALU.max,
                                  negate=True).then_inc(red_done, 1)

            def max_rows(n, g):
                dve.wait_ge(m_tr, n * NG + g + 1)
                if not (isinstance(n, int) and n == 0):
                    dve.wait_ge(m_ld[g], 16 * n)
                dve.tensor_copy(m_row[g][:], row_bank[0:HG, :]).then_inc(m_ready, 1)

            def normalise(n, g):
                dve.wait_ge(t_done, n * NG + g + 1 + PRIME_T)
                o = row_bank[:].rearrange("p (n c) -> p n c", c=32)
                dve.reciprocal(inv_sum[:], o[:, :, D]).then_inc(inv_done, 1)
                dve.wait_ge(inv_done, n * NG + g + 1)
                if g == 0:
                    dve.wait_ge(f_done, n + PRIME_F)
                dve.tensor_tensor(a_tok[:, :, g * HG * D:(g + 1) * HG * D].rearrange("p n (h d) -> p n h d", d=D),
                                  row_bank[:].rearrange("p (n h c) -> p n h c", h=HG, c=32)[:, :, :, 0:D],
                                  inv_sum[:].rearrange("p (n h) -> p n h", h=HG)[:, :, :, None].broadcast_to([P, NB, HG, D]),
                                  ALU.mult).then_inc(a_done, 1)

            for u in range(UB):
                reduce_unit(0, u)
                if u == NU - 1:
                    max_rows(0, 0)
                if u == AHEAD + 12:
                    max_rows(0, 1)
            max_rows(0, 2)

            dve.wait_ge(counts_kept, 2)
            flat = [t[:].rearrange("p x n -> p (x n)") for t in (incl, not_first, total)]
            link(dve.tensor_tensor_scan(flat[0], flat[1], flat[2], 0.0, ALU.mult, ALU.add))
            link(dve.tensor_scalar(rows_i[:], incl[:, :, NT - 1], float(P - 1), None, ALU.add))
            link(dve.tensor_scalar(rows_i[:], rows_i[:], -P, None, ALU.bitwise_and))
            link(dve.tensor_copy(rows_f[:], rows_i[:]))
            link(dve.tensor_tensor_scan(end_row[:], ones_f[:], rows_f[:], 0.0, ALU.mult, ALU.add))
            link(dve.tensor_tensor(base_row[:], end_row[:], rows_f[:], ALU.subtract))
            link(dve.tensor_tensor(incl[:], incl[:], total[:], ALU.subtract))
            link(dve.tensor_tensor(incl[:], incl[:], base_row[:, :, None].broadcast_to([P, NX, NT]), ALU.add))
            link(dve.tensor_tensor(slot[:], rank[:],
                                   incl[:].rearrange("p x n -> p n x"), ALU.add))
            for c in range(2):
                link(dve.tensor_tensor(hot[c][:], hot[c][:], slot[:], ALU.mult))
                link(dve.tensor_reduce(slot_f[:, c, :], hot[c][:], AX.X, ALU.add))
            link(dve.tensor_copy(slot_idx[:], slot_f[:]))
            tiles = [1, NTILE, NX]
            link(dve.tensor_tensor(past[:], end_row[0:1, None, :].broadcast_to(tiles), tile_start[:, :, None].broadcast_to(tiles), ALU.is_le))
            link(dve.tensor_reduce(tile_f[:], past[:], AX.X, ALU.add))
            pairs = tile_f[:].rearrange("o (p k) -> o p k", k=2)
            dve.tensor_scalar(columns[:, 0:NPAIR, 0:2], pairs, float(NX - 1), float(2 * F), ALU.min, ALU.mult).then_inc(routed, 1)
            dve.tensor_scalar(columns[:, 2:NPAIR + 2, 2:4], pairs, float(NX - 1), float(FC * E), ALU.min, ALU.mult).then_inc(routed, 1)

            def attention(b, par, more, more2):
                n = at(b, par)
                for k in range(NG):
                    for u in range(NU):
                        s = k * NU + u
                        if more:
                            reduce_unit(n + 1, s)
                        if u == 3 and k == 0:
                            max_rows(n, NG - 1)
                        if u == 3 and k and more:
                            max_rows(n + 1, k - 1)
                        if u == 6:
                            normalise(n, k)
                        if more and s == 4:
                            value_bias(n + 1)
                        if more and s == 8:
                            value_rows(n + 1, 1 - par)
                        if more2 and s == 13:
                            split_low(n + 2, 0)
                        if more2 and s == 18:
                            split_low(n + 2, 1)
                        if u == 9 and k == NG - 1:
                            dve.wait_ge(f_done, n + 1 + PRIME_F)
                            dve.wait_ge(aT_st, 16 * (n + 1))
                            dve.tensor_copy(a_T[:], row_bank[:]).then_inc(aT_ready, 1)

            with dve.Fori(0, B // 2 - 1) as i:
                for par in range(2):
                    attention(("r", i), par, True, True)
            attention(B - 2, 0, True, False)
            attention(B - 1, 1, False, False)

            u_bank, hidT_bank = bank[2:4], bank[5:7]

            def hidden(t, par):
                n = at(t, par)
                if not (isinstance(n, int) and n < 1):
                    dve.wait_ge(hid_tr, n)
                for k in range(2):
                    dve.wait_ge(sg_done, 2 * n + k + 1)
                    dve.tensor_tensor(hid[:, k, :], sg[:, k, :], u_bank[k][:, 0:F], ALU.mult).then_inc(hid_done, 1)

            def hiddenT_out(t, par):
                n = at(t, par)
                dve.wait_ge(hid_tr, n + 1)
                if not (isinstance(n, int) and n < 2):
                    dve.wait_ge(y_done, n - 1)
                dve.tensor_copy(hidT[par][:, 0:2].rearrange("p c k m -> p (c k m)"), hidT_bank[0][:])
                dve.tensor_copy(hidT[par][0:FR, 2].rearrange("p k m -> p (k m)"), hidT_bank[1][0:FR, 0:PR]).then_inc(hidT_done, 1)

            dve.wait_ge(aT_st, 16 * (B + 1))
            for t in range(2):
                hidden(t, t)
                hiddenT_out(t, t)
            with dve.Fori(1, NPAIR // 2) as i:
                for par in range(2):
                    hidden(("r", i), par)
                    hiddenT_out(("r", i), par)

            def shared_hidden(t, par):
                n = at(t, par)
                for c in range(FC):
                    m = min(P, F - c * P)
                    dve.wait_ge(ssig_done, FC * n + c + 1)
                    if c == 0 and not (isinstance(n, int) and n < 2):
                        dve.wait_ge(res_done, n - 1)
                    dve.tensor_tensor(s_hid[par][0:m, c, :], s_sig[0:m, c, :], bank[2 * c + 1][0:m, :], ALU.mult).then_inc(shid_done, 1)

            def add_up(t, par):
                n = at(t, par)
                dve.wait_ge(o_tr, n + 1)
                dve.wait_ge(s_ld[par], 32 * (half(t, par, 0) + 1))
                if not (isinstance(n, int) and n < 2):
                    dve.wait_ge(o_st[par], 16 * half(t, par, 0))
                dve.tensor_tensor(o_sb[par][:], x_in[par][:], bank[7][:].rearrange("p (n e) -> p n e", e=E), ALU.add).then_inc(o_base, 1)
                dve.wait_ge(got[par], 16 * 2 * NB * (half(t, par, 0) + 1))
                dve.wait_ge(o_base, n + 1)
                for c in range(2):
                    for k in range(NB):
                        o = o_sb[par][:, k, :]
                        ins = dve.scalar_tensor_tensor(out=o, in0=picked[par][:, c, k, :], scalar=topw[:, c, bass.ds(n * NB + k, 1)],
                                                       in1=o, op0=ALU.mult, op1=ALU.add)
                        if k == NB - 1:
                            if c == 0:
                                ins.then_inc(o_half, 1)
                                dve.wait_ge(o_half, n + 1)
                            else:
                                ins.then_inc(o_sum, 1)

            shared_hidden(0, 0)
            shared_hidden(1, 1)
            with dve.Fori(1, B // 2) as i:
                for par in range(2):
                    shared_hidden(("r", i), par)
                    add_up(*shift(("r", i), par, -2))
            add_up(B - 2, 0)
            add_up(B - 1, 1)


_OUTS = [((B, S, E), "float32")]


def kernel(L0_attn_x, L0_attn_W1, L0_attn_b1, L0_attn_Wp, L0_attn_bp, L0_ffn_gate_w, L0_ffn_expert_gate,
           L0_ffn_expert_up, L0_ffn_expert_down, L0_ffn_shared_gate, L0_ffn_shared_up, L0_ffn_shared_down):
    import numpy as np
    import concourse.bacc as bacc
    from concourse.bass_utils import run_bass_kernel_spmd

    w1 = np.asarray(L0_attn_W1).reshape(E, H, 3, D).transpose(0, 2, 1, 3).reshape(E, 3, E)
    b1 = np.asarray(L0_attn_b1).reshape(H, 3, D).transpose(0, 2, 1).reshape(E, 3)
    e_gu = np.stack([np.asarray(L0_ffn_expert_gate), np.asarray(L0_ffn_expert_up)], axis=1).transpose(3, 0, 1, 2)
    s_gu = np.stack([np.asarray(L0_ffn_shared_gate), np.asarray(L0_ffn_shared_up)], axis=0).transpose(2, 0, 1)
    laid_out = {
        "x": np.asarray(L0_attn_x), "w_qkv": w1, "b_qkv": b1, "w_out": np.asarray(L0_attn_Wp),
        "b_out": np.asarray(L0_attn_bp).reshape(E, 1), "gate_w": np.asarray(L0_ffn_gate_w).transpose(1, 0),
        "e_gu": e_gu, "e_down": np.asarray(L0_ffn_expert_down).transpose(0, 2, 1),
        "s_gu": s_gu, "s_down": np.asarray(L0_ffn_shared_down).transpose(1, 0),
    }
    nc = bacc.Bacc("TRN2", target_bir_lowering=False, num_devices=1)
    arrays, args = {}, {}
    for name, a in laid_out.items():
        a = np.ascontiguousarray(a)
        arrays[f"in_{name}"] = a
        args[name] = nc.dram_tensor(f"in_{name}", a.shape, mybir.dt.from_np(a.dtype), kind="ExternalInput").ap()
    (shape, dtype), = _OUTS
    out = nc.dram_tensor("out_0", shape, mybir.dt.from_np(np.dtype(dtype)), kind="ExternalOutput").ap()
    nc.disable_value_cache = True
    attention_moe_kernel(nc, **args, out=out)
    return run_bass_kernel_spmd(nc, [arrays], core_ids=[0]).results[0]["out_0"]
```

```python
from contextlib import ExitStack

import concourse.bass as bass
from concourse import mybir

F32 = mybir.dt.float32
F32R = mybir.dt.float32r
BF16 = mybir.dt.bfloat16
I32 = mybir.dt.int32
U32 = mybir.dt.uint32
ALU = mybir.AluOpType
ACT = mybir.ActivationFunctionType
AX = mybir.AxisListType

P = 128
E = 128
B, S = 8, 512
T = B * S
H = 16
D = E // H
NB = S // P
NT = T // P
HG = 4
NG = H // HG
NX = 8
F = 352
FC = 3
FR = F - 2 * P
NTILE = 2 * T // P + NX
SLOTS = NTILE * P
ER = E + 1
NPAIR = NTILE // 2
PR = 2 * P
FILLS = 8
NOWHERE = 4
SCALE = float(D) ** -0.5
EPS = 1e-5
NEG = -1.0e30

NU = 11
ST_KB = [0, 0, 0, 0, 1, 1, 1, 1, 2, 2, 3]
ST_HEADS = [[0], [1], [2], [3], [0], [1], [2], [3], [0, 1], [2, 3], [0, 1, 2, 3]]
MX_QB = [0, 1, 1, 2, 2, 2, 2, 3, 3, 3, 3]
MX_HEADS = [[0, 1, 2, 3], [0, 1], [2, 3], [0], [1], [2], [3], [0], [1], [2], [3]]
UB = NG * NU
AHEAD = NU + 8
AV_UNITS = [4, 8, 10, 11]
PRIME_AO, PRIME_T, PRIME_F, PRIME_ATOUT, PRIME_A = 1, 2, 1, 1, 1
PRIME_HID, PRIME_HIDT, PRIME_Y = 1, 2, 3


def attention_moe_kernel(nc, x, w_qkv, b_qkv, w_out, b_out, gate_w, e_gu, e_down, s_gu, s_down, out):
    x_tok = x.rearrange("b s e -> (b s) e")
    out_tok = out.rearrange("b s e -> (b s) e")

    q_rows = nc.dram_tensor("q_rows", [H, 3 * D, S], F32, kind="Internal").ap()
    k_rows = nc.dram_tensor("k_rows", [H, 3 * D, S], F32, kind="Internal").ap()
    sorted_x = nc.dram_tensor("sorted_x", [SLOTS, ER], F32, kind="Internal").ap()
    y_tok = nc.dram_tensor("y_tok", [NOWHERE + 2 * T, E], F32, kind="Internal").ap()
    att_T = nc.dram_tensor("att_T", [B, E, S], F32, kind="Internal").ap()

    with ExitStack() as ctx:
        def sb(name, shape, dt=F32, stack=ctx):
            return stack.enter_context(nc.sbuf_tensor(name, shape, dt))

        def ps(name, shape, stack=ctx):
            return stack.enter_context(nc.psum_tensor(name, shape, F32))

        def sem(name):
            return ctx.enter_context(nc.semaphore(name))

        ident = sb("ident", [P, P])
        ident_bf = sb("ident_bf", [P, P], BF16)
        mask_qk = sb("mask_qk", [P, HG, P], BF16)
        before = sb("before", [P, P], BF16)
        ones_bf = sb("ones_bf", [P, P], BF16)
        expert_no = sb("expert_no", [P, NX])
        ones_f = sb("ones_f", [P, NT])
        tile_start = sb("tile_start", [1, NTILE])
        wqkv = sb("wqkv", [P, 3, E])
        bqkv = sb("bqkv", [P, 3])
        wout = sb("wout", [P, E])
        bout = sb("bout", [P, 1])
        gate = sb("gate", [P, NX])
        sgu = sb("sgu", [P, 2, F])
        sdn = sb("sdn", [P, FC, E])
        xnT = sb("xnT", [P, T])
        xn_rows = sb("xn_rows", [P, NT, ER])
        slot_idx = sb("slot_idx", [P, 2, NT], U32)
        topw = sb("topw", [P, 2, NT])
        columns = sb("columns", [1, NPAIR + 2, 4], I32)
        lg = sb("lg", [P, NT, NX])
        bn = sb("bn", [P, NT, 6])
        mv = sb("mv", [P, NT, 2])
        var = sb("var", [P, NT])
        std = sb("std", [P, NT])
        rstd = sb("rstd", [P, NT])
        newton = sb("newton", [P, NT])
        nowhere = sb("nowhere", [P, 2, 2])
        y_rows = sb("y_rows", [P, NPAIR, 2], U32)
        primed = sb("primed", [P, 9])

        attn = ExitStack()
        q_bd, k_st, v32 = [None, None], [None, None], [None, None]

        def batch_buffers(i):
            q_bd[i] = sb(f"q_bd{i}", [P, H, S], F32R, attn)
            k_st[i] = sb(f"k_st{i}", [P, NG, S], F32R, attn)
            v32[i] = sb(f"v32_{i}", [P, NB, H, 32], F32, attn)

        batch_buffers(0)
        q_hi = sb("q_hi", [P, S], F32R, attn)
        q_lo = sb("q_lo", [P, S], F32R, attn)
        k_hi = sb("k_hi", [P, S], F32R, attn)
        k_lo = sb("k_lo", [P, S], F32R, attn)
        vT = sb("vT", [P, S], F32, attn)
        logit = sb("logit", [P, NT, NX], F32, attn)
        prob = sb("prob", [P, NT, NX], F32, attn)
        cand = sb("cand", [P, NT, NX], F32, attn)
        hot = [sb(f"hot{c}", [P, NT, NX], F32, attn) for c in range(2)]
        hot_bf = sb("hot_bf", [P, NT, NX], BF16, attn)
        counts = sb("counts", [P, 2, NT, NX], F32, attn)
        upto = sb("upto", [P, NT, NX], F32, attn)
        four = sb("four", [P, NT, NX // 2], F32, attn)
        two = sb("two", [P, NT, NX // 4], F32, attn)
        slot = sb("slot", [P, NT, NX], F32, attn)
        best = [sb(f"best{c}", [P, NT], F32, attn) for c in range(2)]
        pick = sb("pick", [P, NT], F32, attn)
        slot_f = sb("slot_f", [P, 2, NT], F32, attn)
        rows_i = sb("rows_i", [P, NX], I32, attn)
        rows_f = sb("rows_f", [P, NX], F32, attn)
        end_row = sb("end_row", [P, NX], F32, attn)
        base_row = sb("base_row", [P, NX], F32, attn)
        past = sb("past", [1, NTILE, NX], F32, attn)
        tile_f = sb("tile_f", [1, NTILE], F32, attn)
        batch_buffers(1)
        av_sb = [sb(f"av_sb{i}", [P, S], F32, attn) for i in range(2)]
        a_tok = sb("a_tok", [P, NB, E], F32, attn)
        a_T = sb("a_T", [P, S], F32, attn)
        neg_max = sb("neg_max", [P, NG, HG, NB], F32, attn)
        m_row = [sb(f"m_row{g}", [HG * NB, P], F32R, attn) for g in range(NG)]
        one_row = sb("one_row", [1, S], F32, attn)
        zeros = sb("zeros", [P, SLOTS // P * ER // FILLS], F32, attn)
        inv_sum = sb("inv_sum", [P, NB * HG], F32, attn)
        first = ExitStack()
        x_all = sb("x_all", [P, NT, E], F32, first)
        first.close()
        probs = sb("probs", [P, NU, S], F32, attn)
        attn.close()

        last = ExitStack()
        s_hid_hi = [sb(f"s_hid_hi{i}", [P, FC, S], F32R, last) for i in range(2)]
        a_hi = [sb(f"a_hi{i}", [P, S], F32R, last) for i in range(2)]
        s_hid = sb("s_hid", [P, FC, S], F32, last)
        a_lo = [sb(f"a_lo{i}", [P, S], F32R, last) for i in range(2)]
        o_last = sb("o_last", [P, NB, E], F32, last)
        last.close()
        ffn = ExitStack()
        egu_lo = sb("egu_lo", [P, NX, 2, F], F32R, ffn)
        edn = sb("edn", [P, NX, FC, E], F32, ffn)
        egu_hi = sb("egu_hi", [P, NX, 2, F], F32R, ffn)
        xg = [sb(f"xg{i}", [P, 2, ER], F32, ffn) for i in range(2)]
        xgT_hi = [sb(f"xgT_hi{i}", [P, 2, P], F32R, ffn) for i in range(2)]
        xgT_lo = [sb(f"xgT_lo{i}", [P, 2, P], F32R, ffn) for i in range(2)]
        used, free = NX * (4 * F + FC * E) + 4 * ER + 8 * P, (H + NG) * S + NB * H * 32 + 5 * S + 5 * NT * NX
        sb("rest_before_odd_batches", [P, free - used], F32, ffn)
        sg = sb("sg", [P, 2, F], F32, ffn)
        hid = sb("hid", [P, 2, F], F32, ffn)
        hidT = [sb(f"hidT{i}", [P, FC, 2, P], F32, ffn) for i in range(2)]
        y_sb = [sb(f"y_sb{i}", [P, 2, E], F32, ffn) for i in range(2)]
        xn_hi = sb("xn_hi", [P, T], F32R, ffn)
        xn_lo = sb("xn_lo", [P, T], F32R, ffn)
        sgu_hi = sb("sgu_hi", [P, 2, F], F32R, ffn)
        sgu_lo = sb("sgu_lo", [P, 2, F], F32R, ffn)
        wout_hi = sb("wout_hi", [P, E], F32R, ffn)
        wout_lo = sb("wout_lo", [P, E], F32R, ffn)
        sdn_hi = sb("sdn_hi", [P, FC, E], F32R, ffn)
        sdn_lo = sb("sdn_lo", [P, FC, E], F32R, ffn)
        s_sig = sb("s_sig", [P, FC, S], F32, ffn)
        s_hid_lo = [sb(f"s_hid_lo{i}", [P, FC, S], F32R, ffn) for i in range(2)]
        a_in = [sb(f"a_in{i}", [P, S], F32, ffn) for i in range(2)]
        x_in = [sb(f"x_in{i}", [P, NB, E], F32, ffn) for i in range(2)]
        resT = sb("resT", [P, S], F32, ffn)
        picked = [sb(f"picked{i}", [P, 2, NB, E], F32, ffn) for i in range(2)]
        o_sb = [sb(f"o_sb{i}", [P, NB, E], F32, ffn) for i in range(2)]
        ffn.close()

        bank = [ps(f"bank{i}", [P, S]) for i in range(8)]
        st_bank, mx_bank, av_bank = [bank[0], bank[1], bank[4]], bank[2:4], bank[5]
        first_mx_bank = [bank[2], bank[3], bank[4]]
        row_bank, proj_bank = bank[6], bank[7]

        x_ld = [sem(f"x_ld{i}") for i in range(4)]
        ones_ld = [sem(f"ones_ld{i}") for i in range(2)]
        egu_ld = [sem(f"egu_ld{i}") for i in range(2)]
        edn_ld, egu_high, egu_split, xg_split, shared_high, shared_split = (
            sem(n) for n in ("edn_ld", "egu_high", "egu_split", "xg_split", "shared_high", "shared_split"))
        w_early, w_late = sem("w_early"), sem("w_late")
        consts, cleared, ones_set = sem("consts"), sem("cleared"), sem("ones_set")
        fill_done = sem("fill_done")
        stats, std_done = sem("stats"), sem("std_done")
        vec_p, stat1, o_half = sem("vec_p"), sem("stat1"), sem("o_half")
        xn_done, xT_done, xnT_done = sem("xn_done"), sem("xT_done"), sem("xnT_done")
        lg_done, lg_kept = sem("lg_done"), sem("lg_kept")
        vec = sem("vec")
        z_ready, e_ready, hot_ready, count_done, counts_kept, base_ready, routed = (
            sem(n) for n in ("z_ready", "e_ready", "hot_ready", "count_done", "counts_kept", "base_ready", "routed"))
        scattered, columns_set, vec_r, rows_numbered, y_rows_kept = (
            sem(n) for n in ("scattered", "columns_set", "vec_r", "rows_numbered", "y_rows_kept"))
        qk_proj, qk_hi, qk_split = sem("qk_proj"), sem("qk_hi"), sem("qk_split")
        q_wr, k_wr = sem("q_wr"), sem("k_wr")
        qk_ld = [sem(f"qk_ld{i}") for i in range(2)]
        v_proj, v_biased, v_tr, v_ready = sem("v_proj"), sem("v_biased"), sem("v_tr"), sem("v_ready")
        mx_done, red_done, st_done, exp_done = ([sem(f"{n}{u}") for u in range(NU)] for n in ("mx_done", "red_done", "st_done", "exp_done"))
        masked, av_done = ([sem(f"{n}{kb}") for kb in range(NB)] for n in ("masked", "av_done"))
        m_tr, m_ready = sem("m_tr"), sem("m_ready")
        m_ld = [sem(f"m_ld{g}") for g in range(NG)]
        av_out, t_done = sem("av_out"), sem("t_done")
        inv_done, a_done, f_done, aT_ready, aT_st = (sem(n) for n in ("inv_done", "a_done", "f_done", "aT_ready", "aT_st"))
        xg_ld = [sem(f"xg_ld{i}") for i in range(2)]
        y_st = [sem(f"y_st{i}") for i in range(2)]
        xg_tr, xgT_done, gu_done, sg_done, hid_done, hid_tr, hidT_done, y_done, y_out = (
            sem(n) for n in ("xg_tr", "xgT_done", "gu_done", "sg_done", "hid_done", "hid_tr", "hidT_done", "y_done", "y_out"))
        shid_high, shid_split, a_high, a_split = (sem(n) for n in ("shid_high", "shid_split", "a_high", "a_split"))
        sgu_done, ssig_done, shid_done, res_done, res_out, o_tr, o_sum = (
            sem(n) for n in ("sgu_done", "ssig_done", "shid_done", "res_done", "res_out", "o_tr", "o_sum"))
        a_ld, r_ld = ([sem(f"{n}{i}") for i in range(2)] for n in ("a_ld", "r_ld"))
        got = [sem(f"got{i}") for i in range(2)]
        o_st = [sem(f"o_st{i}") for i in range(2)]

        block = ctx.enter_context(nc.Block())

        def half(b, par, n):
            if isinstance(b, int):
                return (b + n) // 2
            return b[1] + (par + n) // 2

        def at(b, par):
            return b if isinstance(b, int) else 2 * b[1] + par

        def shift(t, par, d):
            if isinstance(t, int):
                return t + d, (t + d) % 2
            return ("r", t[1] + (par + d) // 2), (par + d) % 2

        def qkv_bank(b, c):
            return row_bank if isinstance(b, int) and b == 0 and c == 1 else proj_bank

        def sums_of(b, par):
            return o_last if isinstance(b, int) and b == B - 1 else o_sb[par]

        def res_bank_of(b):
            return bank[0] if isinstance(b, int) and b == B - 1 else bank[6]

        def held(engine, value):
            return value if isinstance(value, int) else engine.snap(value)

        def loads_of(t):
            return t.rearrange("(g j) r t -> j r g t", j=HG)

        @block.sync
        def _(sp):
            for i in range(4):
                n = T // 4
                sp.dma_start(x_all[:, i * NT // 4:(i + 1) * NT // 4, :],
                             x_tok[i * n:(i + 1) * n, :].rearrange("(n p) e -> p n e", p=P)).then_inc(x_ld[i], 16)
                if i == 0:
                    sp.dma_start(gate[:], gate_w).then_inc(w_early, 16)
                    sp.dma_start(wqkv[:], w_qkv).then_inc(w_early, 16)
                    sp.dma_start(bqkv[:], b_qkv).then_inc(w_early, 16)
            def constant_rows(par):
                for g in range(NG):
                    sp.dma_start(k_st[par][P - 1:P, g, :].bitcast(F32), one_row[:]).then_inc(ones_ld[par], 16)

            sp.wait_ge(ones_set, 1)
            sp.wait_ge(cleared, 1)
            constant_rows(0)

            def split_rows_out(b, par):
                n = at(b, par)
                for c, (hi, lo, rows, done) in enumerate(((q_hi, q_lo, q_rows, q_wr), (k_hi, k_lo, k_rows, k_wr))):
                    sp.wait_ge(qk_split, sp.snap(2 * n + c + 1))
                    order = (hi, hi, lo) if c == 0 else (hi, lo, hi)
                    for r in range(3):
                        sp.dma_start(rows[:, r * D:(r + 1) * D, :], order[r][:].bitcast(F32)).then_inc(done, 16)

            def split_rows_in(b, par):
                n = at(b, par)
                sp.wait_ge(q_wr, sp.snap(48 * (n + 1)))
                sp.wait_ge(k_wr, sp.snap(48 * (n + 1)))
                for j in range(HG):
                    strip = slice(32 * j, 32 * j + 3 * D)
                    sp.dma_start(q_bd[par][strip, j:H:HG, :].bitcast(F32), loads_of(q_rows)[j]).then_inc(qk_ld[par], 16)
                    sp.dma_start(k_st[par][strip, :, :].bitcast(F32), loads_of(k_rows)[j]).then_inc(qk_ld[par], 16)

            def max_row_in(b, par, g):
                n = at(b, par)
                sp.wait_ge(m_ready, sp.snap(NG * n + g + 1))
                sp.dma_start(q_bd[par][P - 1:P, HG * g:HG * (g + 1), :].bitcast(F32), m_row[g][:].bitcast(F32)).then_inc(m_ld[g], 16)

            split_rows_out(0, 0)
            sp.wait_ge(cleared, 2)
            split_rows_in(0, 0)
            sp.wait_ge(qk_ld[0], 16 * 2 * HG)
            max_row_in(0, 0, 0)
            split_rows_out(1, 1)
            sp.wait_ge(cleared, 3)
            split_rows_in(1, 1)
            constant_rows(1)
            for g in range(1, NG - 1):
                max_row_in(0, 0, g)
            sp.dma_start(wout[:], w_out).then_inc(w_late, 16)
            sp.dma_start(bout[:], b_out).then_inc(w_late, 16)
            sp.dma_start(sgu[:], s_gu).then_inc(w_late, 16)
            sp.dma_start(sdn[:, 0:2, :], s_down[0:2 * P, :].rearrange("(c f) e -> f c e", f=P)).then_inc(w_late, 16)
            sp.dma_start(sdn[0:FR, 2, :], s_down[2 * P:F, :]).then_inc(w_late, 16)

            def expert_weights():
                sp.wait_ge(st_done[NU - 1], NG * (B - 1))
                for i in range(2):
                    part = slice(i * NX // 2, (i + 1) * NX // 2)
                    sp.dma_start(egu_lo[:, part].bitcast(F32), e_gu[:, part]).then_inc(egu_ld[i], 16)
                for c in range(2):
                    sp.dma_start(edn[:, :, c, :], e_down[:, c * P:(c + 1) * P, :].rearrange("x f e -> f x e")).then_inc(edn_ld, 16)
                sp.dma_start(edn[0:FR, :, 2, :], e_down[:, 2 * P:F, :].rearrange("x f e -> f x e")).then_inc(edn_ld, 16)

            def attention(b, par, more, more2):
                n = at(b, par)
                nxt, _ = shift(b, par, 1)
                nxt2, _ = shift(b, par, 2)
                max_row_in(b, par, NG - 1)
                if more:
                    max_row_in(nxt, 1 - par, 0)
                if more2:
                    sp.wait_ge(qk_ld[1 - par], sp.snap(16 * 2 * HG * (half(b, par, 1) + 1)))
                    split_rows_out(nxt2, par)
                if more:
                    max_row_in(nxt, 1 - par, 1)
                if more2:
                    sp.wait_ge(st_done[NU - 1], sp.snap(NG * (n + 1)))
                    split_rows_in(nxt2, par)
                elif more:
                    expert_weights()
                if more:
                    max_row_in(nxt, 1 - par, 2)
                dst = sp.snap(n * E) if not isinstance(n, int) else n * E
                sp.wait_ge(aT_ready, sp.snap(n + 1 + PRIME_ATOUT))
                sp.dma_start(att_T.rearrange("b e s -> (b e) s")[bass.ds(dst, E), :], a_T[:]).then_inc(aT_st, 16)

            attention(0, 0, True, True)
            fill = SLOTS // P * ER // FILLS
            for i in range(FILLS):
                sp.dma_start(sorted_x.rearrange("(p k) e -> p (k e)", p=P)[:, i * fill:(i + 1) * fill], zeros[:]).then_inc(fill_done, 16)
            attention(1, 1, True, True)
            with sp.Fori(1, B // 2 - 1) as i:
                for par in range(2):
                    attention(("r", i), par, True, True)
            attention(B - 2, 0, True, False)
            def pair_rows(t, n):
                start = sp.snap(n * PR) if not isinstance(n, int) else n * PR
                return t[bass.ds(start, PR), :].rearrange("(k p) e -> p k e", p=P)

            sp.wait_ge(scattered, 16 * 2 * NT)
            for t in range(2):
                sp.dma_start(xg[t][:], pair_rows(sorted_x, t)).then_inc(xg_ld[t], 16)
            attention(B - 1, 1, False, False)

            def expert_pair(t, par):
                n = at(t, par)
                sp.wait_ge(xg_tr, sp.snap(n + 1))
                sp.wait_ge(y_rows_kept, sp.snap(n + 1))
                sp.dma_start(xg[par][:], pair_rows(sorted_x, n + 2)).then_inc(xg_ld[par], 16)

            with sp.Fori(0, NPAIR // 2 - 1) as i:
                for par in range(2):
                    expert_pair(("r", i), par)

            def attention_in(b, par):
                n = at(b, par)
                src = n * E if isinstance(n, int) else sp.snap(n * E)
                sp.dma_start(a_in[par][:], att_T.rearrange("b e s -> (b e) s")[bass.ds(src, E), :]).then_inc(a_ld[par], 16)

            def residual_in(b, par):
                n = at(b, par)
                tok = n * S if isinstance(n, int) else sp.snap(n * S)
                sp.dma_start(x_in[par][:], x_tok[bass.ds(tok, S), :].rearrange("(n p) e -> p n e", p=P)).then_inc(r_ld[par], 16)

            def results_in(b, par):
                n = at(b, par)
                for c in range(2):
                    row = NOWHERE + c * T + n * S
                    row = row if isinstance(n, int) else sp.snap(row)
                    sp.dma_start(picked[par][:, c], y_tok[bass.ds(row, S), :].rearrange("(n p) e -> p n e", p=P)).then_inc(got[par], 16)

            def last_out(b, par):
                n = at(b, par)
                tok = n * S if isinstance(n, int) else sp.snap(n * S)
                sp.wait_ge(o_sum, sp.snap(n + 1))
                sp.dma_start(out_tok[bass.ds(tok, S), :].rearrange("(n p) e -> p n e", p=P), sums_of(b, par)[:]).then_inc(o_st[par], 16)

            for b in range(2):
                attention_in(b, b)
                residual_in(b, b)
            for par in range(2):
                sp.wait_ge(y_st[par], 16 * NPAIR)
            for b in range(2):
                results_in(b, b)
            with sp.Fori(0, B // 2 - 1) as i:
                for par in range(2):
                    sp.wait_ge(res_done, sp.snap(at(("r", i), par) + 1))
                    attention_in(("r", i + 1), par)
                    sp.wait_ge(o_half, sp.snap(2 * at(("r", i), par) + 2))
                    residual_in(("r", i + 1), par)
                    results_in(("r", i + 1), par)
                    last_out(("r", i), par)
            for par in range(2):
                last_out(B - 2 + par, par)
            for par in range(2):
                sp.wait_ge(o_st[par], 16 * (B // 2))

        @block.gpsimd
        def _(pool):
            pool.memset(ident[:], 0.0).then_inc(vec_p, 1)
            pool.wait_ge(vec_p, 1)
            pool.affine_select(out=ident[:], in_=ident[:], compare_op=ALU.not_equal, fill=1.0, base=0,
                               pattern=[[-1, P]], channel_multiplier=1).then_inc(consts, 1)
            pool.wait_ge(consts, 1)
            pool.tensor_copy(ident_bf[:], ident[:]).then_inc(consts, 1)
            for k in range(2):
                ins = pool.memset(k_st[k][:].bitcast(F32), 0.0)
            ins.then_inc(cleared, 1)
            pool.memset(q_bd[0][:].bitcast(F32), 0.0).then_inc(cleared, 1)
            pool.memset(mask_qk[:], 0.0)
            pool.memset(before[:], 1.0)
            for i in range(2):
                pool.memset(v32[i][:], 0.0)
            pool.memset(ones_f[:], 1.0)
            pool.memset(ones_bf[:], 1.0).then_inc(vec_p, 1)
            pool.wait_ge(vec_p, 2)
            pool.affine_select(out=mask_qk[:], in_=mask_qk[:], compare_op=ALU.is_ge, fill=NEG, base=0,
                               pattern=[[0, HG], [-1, P]], channel_multiplier=1)
            pool.affine_select(out=before[:], in_=before[:], compare_op=ALU.is_ge, fill=0.0, base=-1,
                               pattern=[[1, P]], channel_multiplier=-1)
            for i in range(2):
                pool.memset(v32[i][:, :, :, D:D + 1], 1.0)
            pool.iota(expert_no[:], pattern=[[1, NX]], base=0, channel_multiplier=0, allow_small_or_imprecise_dtypes=True)
            pool.iota(nowhere[:], pattern=[[2, 2], [1, 2]], base=0, channel_multiplier=0, allow_small_or_imprecise_dtypes=True)
            pool.iota(tile_start[:], pattern=[[P, NTILE]], base=0, channel_multiplier=0,
                      allow_small_or_imprecise_dtypes=True).then_inc(consts, 1)
            pool.memset(zeros[:], 0.0)
            pool.memset(q_bd[1][:].bitcast(F32), 0.0).then_inc(cleared, 1)
            each = [P, NT, NX]
            chain = [0]

            def link(ins):
                chain[0] += 1
                ins.then_inc(vec_r, 1)
                pool.wait_ge(vec_r, chain[0])

            def over_experts(out, t, op):
                link(pool.tensor_tensor(four[:], t[:, :, 0:4], t[:, :, 4:8], op))
                link(pool.tensor_tensor(two[:], four[:, :, 0:2], four[:, :, 2:4], op))
                link(pool.tensor_tensor(out, two[:, :, 0], two[:, :, 1], op))

            def mask_block(n, g, kb):
                first = ([0] + AV_UNITS)[kb]
                for u in range(first, AV_UNITS[kb]):
                    pool.wait_ge(exp_done[u], n * NG + g + 1)
                heads = len(ST_HEADS[first])
                w = S - kb * P
                diag = probs[:, first:AV_UNITS[kb], 0:heads * w].rearrange("p u (h w) -> p u h w", h=heads)[:, :, :, 0:P]
                pool.affine_select(out=diag, in_=diag, compare_op=ALU.is_ge, fill=0.0, base=0,
                                   pattern=[[0, HG // heads], [0, heads], [1, P]], channel_multiplier=-1).then_inc(masked[kb], 1)

            for kb in range(NB):
                mask_block(0, 0, kb)

            def sum_rows():
                pool.wait_ge(base_ready, 1)
                link(pool.tensor_tensor(slot[:], counts[:, 0], base_row[:, None, :].broadcast_to(each), ALU.add))
                link(pool.tensor_tensor(slot[:], slot[:], upto[:], ALU.add))
                link(pool.tensor_tensor(slot[:], slot[:], counts[:, 1], ALU.subtract))

            def choose_rows(c):
                link(pool.tensor_tensor(hot[c][:], hot[c][:], slot[:], ALU.mult))
                over_experts(slot_f[:, c, :], hot[c], ALU.add)

            def keep_slots():
                pool.tensor_copy(slot_idx[:], slot_f[:]).then_inc(routed, 1)
                pool.wait_ge(routed, 1)
                pool.wait_ge(fill_done, 16 * FILLS)

            def number_rows(c):
                pool.iota(xn_rows[:, :, E], pattern=[[P, NT]], base=NOWHERE + c * T, channel_multiplier=1,
                          allow_small_or_imprecise_dtypes=True).then_inc(rows_numbered, 1)
                pool.wait_ge(rows_numbered, c + 1)

            def scatter(i):
                c, n = divmod(i, NT)
                if i == NT:
                    pool.wait_ge(scattered, 16 * NT)
                    number_rows(1)
                pool.indirect_dma_start(sorted_x, bass.IndirectOffsetOnAxis(ap=slot_idx[:, c, n:n + 1], axis=0),
                                        xn_rows[:, n, :], None).then_inc(scattered, 16)

            number_rows(0)
            for b in range(B):
                for k in range(NG):
                    g = (k + 1) % NG
                    n = b if g else b + 1
                    for kb in range(NB):
                        if n < B:
                            mask_block(n, g, kb)
                        if b == 1 and kb == 1 and k > 0:
                            if k == 1:
                                sum_rows()
                            else:
                                choose_rows(k - 2)
                        if b == 1 and kb == 2 and k == NG - 1:
                            keep_slots()
                        if 2 <= b < 2 + 2 * NT // (4 * NG) and kb % 2 == 1:
                            for i in range(2):
                                scatter((b - 2) * 4 * NG + 4 * k + kb - 1 + i)
            x_chunks = [(xn_hi[:, i * S:(i + 1) * S], xn_lo[:, i * S:(i + 1) * S], xnT[:, i * S:(i + 1) * S]) for i in range(B)]
            splits = x_chunks + [(sgu_hi[:, a], sgu_lo[:, a], sgu[:, a]) for a in range(2)] + [
                (wout_hi[:], wout_lo[:], wout[:]), (sdn_hi[:, 0:2], sdn_lo[:, 0:2], sdn[:, 0:2]),
                (sdn_hi[0:FR, 2], sdn_lo[0:FR, 2], sdn[0:FR, 2])]
            every = NPAIR // (len(splits) + 1)

            for t in range(NPAIR):
                pool.wait_ge(y_rows_kept, t + 1)
                pool.wait_ge(y_out, t + 1 + PRIME_Y)
                for k in range(2):
                    pool.indirect_dma_start(y_tok, bass.IndirectOffsetOnAxis(ap=y_rows[:, t, k:k + 1], axis=0),
                                            y_sb[t % 2][:, k, :], None).then_inc(y_st[t % 2], 16)
                if t == 0:
                    pool.wait_ge(f_done, B + PRIME_F)
                    pool.wait_ge(aT_st, 16 * (B + 1))
                    pool.wait_ge(w_late, 16 * 5)
                if t % every == 0 and t // every < len(splits):
                    hi, lo, whole = splits[t // every]
                    pool.tensor_copy(hi, whole).then_inc(shared_high, 1)
                    pool.wait_ge(shared_high, t // every + 1)
                    pool.tensor_tensor(lo, whole, hi.bitcast(F32), ALU.subtract).then_inc(shared_split, 1)

            def low_parts(b, par):
                n = at(b, par)
                for c in range(FC):
                    m = min(P, F - c * P)
                    pool.wait_ge(shid_high, FC * n + c + 1)
                    pool.tensor_tensor(s_hid_lo[par][0:m, c, :], s_hid[0:m, c, :], s_hid_hi[par][0:m, c, :].bitcast(F32),
                                       ALU.subtract).then_inc(shid_split, 1)
                pool.wait_ge(a_high, n + 1)
                pool.tensor_tensor(a_lo[par][:], a_in[par][:], a_hi[par][:].bitcast(F32), ALU.subtract).then_inc(a_split, 1)

            with pool.Fori(0, B // 2) as i:
                for par in range(2):
                    low_parts(("r", i), par)

        @block.tensor
        def _(pe):
            def project(n, c, done):
                pe.matmul(qkv_bank(n, c)[:], wqkv[:, c, :], xnT[:, bass.ds(n * S, S)], start=True, stop=True).then_inc(done, 1)

            def v_transposes(n):
                pe.wait_ge(v_biased, n + 1)
                for k in range(NB):
                    ins = pe.transpose(proj_bank[:, k * P:(k + 1) * P], vT[:, k * P:(k + 1) * P], ident[:])
                ins.then_inc(v_tr, 1)

            def max_unit(par, g, u, dst):
                qb, heads = MX_QB[u], MX_HEADS[u]
                w = (qb + 1) * P
                for i, j in enumerate(heads):
                    pe.matmul(dst[:, i * w:(i + 1) * w], q_bd[par][0:P - 1, HG * g + j, qb * P:(qb + 1) * P],
                              k_st[par][0:P - 1, g, 0:w], start=(i == 0), stop=False, skip_group_check=True)
                nh = len(heads)
                diag = dst[:, 0:nh * w].rearrange("p (h w) -> p h w", h=nh)[:, :, qb * P:w]
                pe.matmul(diag, ident_bf[:], mask_qk[:, 0:nh, :], start=False, stop=True, skip_group_check=True).then_inc(mx_done[u], 1)

            def max_transposes(g, groups):
                pe.wait_ge(red_done[NU - 1], groups)
                pe.transpose(row_bank[0:HG * NB, 0:P], neg_max[:, g].rearrange("p h n -> p (h n)"), ident[:]).then_inc(m_tr, 1)

            def score_unit(par, g, u, dst):
                kb, heads = ST_KB[u], ST_HEADS[u]
                w = S - kb * P
                nh = len(heads)
                h0 = HG * g + heads[0]
                pe.matmul(dst[:, 0:nh * w], k_st[par][:, g, kb * P:(kb + 1) * P], q_bd[par][:, h0:h0 + nh, kb * P:S],
                          start=True, stop=True).then_inc(st_done[u], 1)

            def value_bundle(par, g, kb, groups):
                pe.wait_ge(masked[kb], groups)
                for j in range(HG):
                    u, lo = [(j, 0), (4 + j, 0), (8 + j // 2, j % 2 * 2 * P), (10, j * P)][kb]
                    w = S - kb * P
                    ins = pe.matmul(av_bank[32 * j:32 * j + 32, kb * P:S], v32[par][:, kb, HG * g + j, :], probs[:, u, lo:lo + w],
                                    start=(kb == 0), stop=(kb == NB - 1), skip_group_check=True)
                ins.then_inc(av_done[kb], 1)

            def to_tokens(g):
                for k in range(NB):
                    ins = pe.transpose(row_bank[:, k * P:(k + 1) * P], av_sb[g % 2][:, k * P:(k + 1) * P], ident[:])
                ins.then_inc(t_done, 1)

            def to_features():
                for k in range(NB):
                    ins = pe.transpose(row_bank[:, k * P:(k + 1) * P], a_tok[:, k, :], ident[:])
                ins.then_inc(f_done, 1)

            def x_transposes(b):
                pe.wait_ge(xn_done, b + 1)
                if b >= 2:
                    pe.wait_ge(xnT_done, b - 1)
                for n in range(NB):
                    ins = pe.transpose(bank[b % 2][:, n * P:(n + 1) * P], xn_rows[:, b * NB + n, 0:E], ident[:])
                ins.then_inc(xT_done, 1)

            def router_block(n):
                ins = pe.matmul(lg_bank[:, n * NX:(n + 1) * NX], xnT[:, n * P:(n + 1) * P], gate[:],
                                start=(n == 0), stop=True, skip_group_check=True)
                if n == NT - 1:
                    ins.then_inc(lg_done, 1)

            def router(b):
                pe.wait_ge(xnT_done, b + 1)
                for n in range(b * NB, (b + 1) * NB):
                    router_block(n)

            def first_project(n, c):
                if n:
                    pe.wait_ge(qk_split, 2 * n + c)
                pe.wait_ge(xnT_done, n + 1)
                project(n, c, v_proj if c == 2 else qk_proj)

            lg_bank = bank[5]
            pe.wait_ge(consts, 1)
            pe.wait_ge(w_early, 48)
            x_transposes(0)
            first_project(0, 0)
            first_project(0, 1)
            x_transposes(1)
            x_transposes(2)
            x_transposes(3)
            for b in range(3):
                router(b)
            x_transposes(4)
            router(3)
            x_transposes(5)
            router(4)
            x_transposes(6)
            x_transposes(7)

            def count_tokens():
                pe.wait_ge(hot_ready, 1)
                pe.wait_ge(qk_split, 2 * 3)
                n = NT * NX
                chosen = hot_bf[:].rearrange("p n x -> p (n x)")
                pe.matmul(proj_bank[:, 0:n], before[:], chosen, start=True, stop=True, skip_group_check=True)
                pe.matmul(proj_bank[:, n:2 * n], ones_bf[:], chosen, start=False, stop=True, skip_group_check=True).then_inc(count_done, 1)

            pe.wait_ge(consts, 3)
            pe.wait_ge(qk_ld[0], 16 * 2 * HG)
            pe.wait_ge(ones_ld[0], 16 * NG)
            def first_max_unit(v):
                g, u = divmod(v, NU)
                if v >= 3:
                    pe.wait_ge(red_done[(v - 3) % NU], (v - 3) // NU + 1)
                max_unit(0, g, u, first_mx_bank[v % 3])

            for v in range(NU):
                first_max_unit(v)
            max_transposes(0, 1)
            for v in range(NU, AHEAD):
                first_max_unit(v)
            first_project(1, 0)
            pe.wait_ge(xnT_done, B)
            pe.wait_ge(m_ld[0], 16)
            for u in range(NU):
                if u >= 2:
                    pe.wait_ge(exp_done[u - 2], 1)
                score_unit(0, 0, u, st_bank[(u + 1) % 2])
                for v in range(AHEAD + 3 * u, min(AHEAD + 3 * u + 3, UB)):
                    first_max_unit(v)
                if 1 <= u < 7:
                    for n in range(5 * NB + 2 * (u - 1), 5 * NB + 2 * u):
                        router_block(n)
                if u == 3:
                    pe.wait_ge(m_ready, 1)
                    max_transposes(1, 2)
                if u == 0:
                    first_project(1, 1)
                if u == 3:
                    pe.wait_ge(qk_split, 4)
                    project(0, 2, v_proj)
                if u == 5:
                    v_transposes(0)
                if u == 7:
                    pe.wait_ge(m_ready, 2)
                    max_transposes(2, 3)
                if u == 8:
                    pe.wait_ge(v_ready, 1)
                    pe.wait_ge(lg_kept, 1)
                    value_bundle(0, 0, 0, 1)
            pe.wait_ge(m_ready, 3)
            pe.wait_ge(red_done[8], NG)
            pe.wait_ge(ones_ld[1], 16 * NG)

            g_bank, u_bank = bank[0:2], bank[2:4]
            xgT_bank, hidT_bank, y_bank = bank[4], bank[5:7], bank[7]

            def load_columns(step):
                clamped = "DVE clamps the expert before it multiplies"
                _, cols = nc.values_load_multi_w_load_instructions(
                    columns[0:1, bass.ds(step, 1), :].rearrange("o s c -> o (s c)"), engines=[mybir.EngineType.PE], min_val=0,
                    max_val=(NX - 1) * 2 * F, skip_runtime_bounds_check_because=clamped)
                return [c if k < 2 else nc.s_assert_within(c, 0, (NX - 1) * FC * E, skip_runtime_bounds_check_because=clamped)
                        for k, c in enumerate(cols)]

            def x_step(t, par):
                n = at(t, par)
                pe.wait_ge(xg_ld[par], 16 * (half(t, par, 0) + 1))
                for k in range(2):
                    ins = pe.transpose(xgT_bank[:, k * P:(k + 1) * P], xg[par][:, k, 0:E], ident[:])
                ins.then_inc(xg_tr, 1)

            def gate_up(par, cols, step):
                pe.wait_ge(xg_split, step)
                hi, lo = (w[:].rearrange("p x a f -> p (x a f)") for w in (egu_hi, egu_lo))
                for k in range(2):
                    g, u = g_bank[k][:, 0:F], u_bank[k][:, 0:F]
                    gate_cols, up_cols = bass.ds(cols[k], F), bass.ds(cols[k] + F, F)
                    pe.matmul(g, xgT_hi[par][:, k, :], hi[:, gate_cols], start=True, stop=False)
                    pe.matmul(g, xgT_hi[par][:, k, :], lo[:, gate_cols], start=False, stop=False)
                    pe.matmul(u, xgT_hi[par][:, k, :], hi[:, up_cols], start=True, stop=False)
                    pe.matmul(u, xgT_hi[par][:, k, :], lo[:, up_cols], start=False, stop=False)
                    pe.matmul(g, xgT_lo[par][:, k, :], hi[:, gate_cols], start=False, stop=True)
                    pe.matmul(u, xgT_lo[par][:, k, :], hi[:, up_cols], start=False, stop=True).then_inc(gu_done, 1)

            def down(par, cols, step):
                pe.wait_ge(hidT_done, step)
                pe.wait_ge(y_out, step)
                w = edn[:].rearrange("p x c e -> p (x c e)")
                for k in range(2):
                    for c in range(FC):
                        m = min(P, F - c * P)
                        ins = pe.matmul(y_bank[:, k * E:(k + 1) * E], hidT[par][0:m, c, k, :], w[0:m, bass.ds(cols[2 + k] + c * E, E)],
                                        start=(c == 0), stop=(c == FC - 1))
                ins.then_inc(y_done, 1)

            def hid_transposes(step):
                pe.wait_ge(hid_done, step)
                for k in range(2):
                    for c in range(FC):
                        m = min(P, F - c * P)
                        col = (c % 2 * 2 + k) * P
                        ins = pe.transpose(hidT_bank[c // 2][0:m, col:col + P], hid[:, k, c * P:c * P + m], ident[:])
                ins.then_inc(hid_tr, 1)

            def after_gate_up(t, par, has_next, has_t, has_1):
                n = at(t, par)
                step = held(pe, n + 2)
                if has_next or has_1:
                    cols = load_columns(n + 1)
                if has_next:
                    x_step(*shift(t, par, 1))
                if has_1:
                    down(1 - par, cols, step)
                if has_t:
                    hid_transposes(step)
                if has_next:
                    gate_up(1 - par, cols, step)

            def attention(b, par, more, more2):
                n = at(b, par)
                for k in range(NG):
                    g = (k + 1) % NG
                    spar = par if g else 1 - par
                    finished, scored = held(pe, n * NG + k + 1), held(pe, n * NG + k + 2)
                    before_max, with_max = held(pe, (n + 1) * NG + k), held(pe, (n + 1) * NG + k + 1)
                    for u in range(NU):
                        s = k * NU + u
                        if g or more:
                            if u == 0:
                                pe.wait_ge(m_ld[g], 16 * (n + 1 if g else n + 2))
                                if g == 0:
                                    pe.wait_ge(v_ready, n + 2)
                            if not more:
                                if s == 0:
                                    pe.wait_ge(red_done[NU - 1], B * NG)
                                if s < 4:
                                    pe.wait_ge(exp_done[NU - 1], finished)
                                else:
                                    pe.wait_ge(exp_done[(s - 4) % NU], n * NG + (s - 4) // NU + 2)
                                score_unit(spar, g, u, bank[s % 4])
                            else:
                                if u >= 3:
                                    pe.wait_ge(exp_done[u - 3], scored)
                                else:
                                    pe.wait_ge(exp_done[(9, 10, 8)[u]], finished)
                                score_unit(spar, g, u, st_bank[u % 3])
                        if more:
                            if s == 0:
                                pe.wait_ge(qk_ld[1 - par], 16 * 2 * HG * (half(b, par, 1) + 1))
                            if u >= 2:
                                pe.wait_ge(red_done[u - 2], with_max)
                            else:
                                pe.wait_ge(red_done[u + NU - 2], before_max)
                            max_unit(1 - par, k, u, mx_bank[s % 2])
                        if u < 3:
                            value_bundle(par, k, u + 1, finished)
                        if u == 3 and (more or k == 0):
                            if k == 0:
                                pe.wait_ge(aT_ready, n + PRIME_ATOUT)
                            else:
                                pe.wait_ge(a_done, finished)
                            max_transposes((k - 1) % NG, before_max)
                        if u == (6 if more or k == NG - 1 else 9):
                            pe.wait_ge(av_out, scored)
                            if more or k == 0:
                                pe.wait_ge(m_ready, before_max)
                            else:
                                pe.wait_ge(a_done, finished)
                            to_tokens(k)
                        if u == 7 and (g or more):
                            pe.wait_ge(av_out, scored)
                            value_bundle(spar, g, 0, scored)
                        if not more and k == NG - 1 and u == 0:
                            pe.wait_ge(columns_set, 2)
                            x_step(0, 0)
                        if not more and k == NG - 1 and u == 7:
                            pe.wait_ge(egu_split, NX)
                            gate_up(0, load_columns(0), 1)
                        if u == 9 and k == NG - 1:
                            pe.wait_ge(a_done, scored)
                            to_features()
                        if isinstance(n, int) and n == 0 and s == 34:
                            count_tokens()
                        if more and s == 4:
                            pe.wait_ge(qk_split, 2 * (n + 2))
                            if isinstance(n, int) and n == 1:
                                pe.wait_ge(counts_kept, 1)
                            project(n + 1, 2, v_proj)
                        if more and s == 8:
                            v_transposes(n + 1)
                        if more2 and s == 13:
                            pe.wait_ge(v_ready, n + 2)
                            project(n + 2, 0, qk_proj)
                        if more2 and s == 19:
                            pe.wait_ge(qk_split, 2 * (n + 2) + 1)
                            project(n + 2, 1, qk_proj)

            for b in range(2):
                attention(b, b, True, True)
            with pe.Fori(1, B // 2 - 1) as i:
                for par in range(2):
                    attention(("r", i), par, True, True)
            attention(B - 2, 0, True, False)
            attention(B - 1, 1, False, False)

            pe.wait_ge(aT_ready, B + PRIME_ATOUT)
            pe.wait_ge(edn_ld, 16 * FC)
            pe.wait_ge(w_late, 16 * 5)
            after_gate_up(0, 0, True, True, False)
            after_gate_up(1, 1, True, True, True)
            with pe.Fori(1, NPAIR // 2 - 1) as i:
                for par in range(2):
                    after_gate_up(("r", i), par, True, True, True)
            tok_bank = bank[7]

            def shared_up(t, par, chunks=range(FC)):
                n = at(t, par)
                for c in chunks:
                    m = min(P, F - c * P)
                    if not (isinstance(n, int) and n == 0):
                        pe.wait_ge(shid_done, FC * (n - 1) + c + 1)
                    tok = bass.ds(n * S, S)
                    for a in range(2):
                        dst, cols = bank[2 * c + a][0:m, :], slice(c * P, c * P + m)
                        pe.matmul(dst, sgu_hi[:, a, cols], xn_hi[:, tok], start=True, stop=False)
                        pe.matmul(dst, sgu_hi[:, a, cols], xn_lo[:, tok], start=False, stop=False)
                        ins = pe.matmul(dst, sgu_lo[:, a, cols], xn_hi[:, tok], start=False, stop=True)
                    ins.then_inc(sgu_done, 1)

            def shared_down(t, par):
                n = at(t, par)
                res_bank = res_bank_of(t)
                if not (isinstance(n, int) and n in (0, B - 1)):
                    pe.wait_ge(res_out, n)
                rows = [slice(0, min(P, F - c * P)) for c in range(FC)]
                for c, r in enumerate(rows):
                    pe.wait_ge(shid_high, FC * n + c + 1)
                    pe.matmul(res_bank[:], sdn_hi[r, c, :], s_hid_hi[par][r, c, :], start=(c == 0), stop=False)
                    pe.matmul(res_bank[:], sdn_lo[r, c, :], s_hid_hi[par][r, c, :], start=False, stop=False)
                pe.wait_ge(a_high, n + 1)
                pe.matmul(res_bank[:], wout_hi[:], a_hi[par][:], start=False, stop=False)
                pe.matmul(res_bank[:], wout_lo[:], a_hi[par][:], start=False, stop=False)
                for c, r in enumerate(rows):
                    pe.wait_ge(shid_split, FC * n + c + 1)
                    pe.matmul(res_bank[:], sdn_hi[r, c, :], s_hid_lo[par][r, c, :], start=False, stop=False)
                pe.wait_ge(a_split, n + 1)
                pe.matmul(res_bank[:], wout_hi[:], a_lo[par][:], start=False, stop=True).then_inc(res_done, 1)

            def back_to_tokens(t, par):
                n = at(t, par)
                pe.wait_ge(res_out, n + 1)
                if not (isinstance(n, int) and n == 0):
                    pe.wait_ge(o_sum, n)
                for k in range(NB):
                    ins = pe.transpose(tok_bank[:, k * P:(k + 1) * P], resT[:, k * P:(k + 1) * P], ident[:])
                ins.then_inc(o_tr, 1)

            for t in range(NPAIR - 2, NPAIR):
                after_gate_up(t, t % 2, t + 1 < NPAIR, True, True)
            pe.wait_ge(shared_split, B + 5)
            shared_up(0, 0, range(2))
            after_gate_up(NPAIR, NPAIR % 2, False, False, True)
            shared_up(0, 0, range(2, FC))
            shared_up(1, 1)
            shared_down(0, 0)
            with pe.Fori(1, B // 2) as i:
                for par in range(2):
                    shared_up(("r", i), par)
                    back_to_tokens(*shift(("r", i), par, -2))
                    shared_down(*shift(("r", i), par, -1))
            shared_down(B - 1, 1)
            back_to_tokens(B - 2, 0)
            back_to_tokens(B - 1, 1)

        @block.scalar
        def _(act):
            def split_high(n, c):
                dst, wr = ((q_hi, q_wr), (k_hi, k_wr))[c]
                act.wait_ge(qk_proj, 2 * n + c + 1)
                if not (isinstance(n, int) and n == 0):
                    act.wait_ge(wr, 48 * n)
                act.activation(dst[:], qkv_bank(n, c)[:], ACT.Identity, bias=bqkv[:, c:c + 1]).then_inc(qk_hi, 1)

            def first_std(i):
                act.wait_ge(stats, i + 1)
                q = slice(i * NT // 4, (i + 1) * NT // 4)
                act.activation(std[:, q], var[:, q], ACT.Sqrt).then_inc(std_done, 1)

            def xT_out(b):
                act.wait_ge(xT_done, b + 1)
                act.activation(xnT[:, b * S:(b + 1) * S], bank[b % 2][:], ACT.Copy).then_inc(xnT_done, 1)

            act.wait_ge(w_early, 48)
            first_std(0)
            xT_out(0)
            first_std(1)
            split_high(0, 0)
            split_high(0, 1)
            xT_out(1)
            first_std(2)
            for b in range(2, 5):
                xT_out(b)
            first_std(3)
            for b in range(5, 8):
                xT_out(b)
            split_high(1, 0)
            split_high(1, 1)
            def exp_unit(g, u, groups, groups_before, src):
                w = (S - ST_KB[u] * P) * len(ST_HEADS[u])
                act.wait_ge(st_done[u], groups)
                if u in (0, 4, 8, 10) and groups_before is not None:
                    act.wait_ge(av_done[(0, 4, 8, 10).index(u)], groups_before)
                act.activation(probs[:, u, 0:w], src[:, 0:w], ACT.Exp, scale=SCALE).then_inc(exp_done[u], 1)

            g_bank, xgT_bank, y_bank = bank[0:2], bank[4], bank[7]

            def x_out(t, par):
                n = at(t, par)
                act.wait_ge(xg_tr, n + 1)
                if not (isinstance(n, int) and n < 2):
                    act.wait_ge(gu_done, 2 * n - 2)
                act.activation(xgT_hi[par][:].rearrange("p k m -> p (k m)"), xgT_bank[:, 0:PR], ACT.Copy).then_inc(xgT_done, 1)

            def attention(b, par, more, more2):
                n = at(b, par)
                for k in range(NG):
                    g = (k + 1) % NG
                    finished, scored = held(act, n * NG + k + 1), held(act, n * NG + k + 2)
                    for u in range(NU):
                        if g or more:
                            exp_unit(g, u, scored, finished, st_bank[u % 3] if more else bank[(k * NU + u) % 4])
                        if not more and k == NG - 1 and u == 0:
                            x_out(0, 0)
                        if u == (4 if more else 3):
                            for kb in range(NB):
                                act.wait_ge(av_done[kb], finished)
                            act.wait_ge(t_done, finished)
                            act.activation(av_sb[k % 2][:], av_bank[:], ACT.Copy).then_inc(av_out, 1)
                        s = k * NU + u
                        if isinstance(n, int) and n == 0 and s == 7:
                            act.wait_ge(z_ready, 1)
                            act.activation(prob[:], logit[:], ACT.Exp).then_inc(e_ready, 1)
                        if isinstance(n, int) and n == 0 and s == 40:
                            act.wait_ge(count_done, 1)
                            act.activation(counts[:].rearrange("p a n x -> p (a n x)"), proj_bank[:], ACT.Copy).then_inc(counts_kept, 1)
                        if more2 and s == 14:
                            split_high(n + 2, 0)
                        if more2 and s == 20:
                            split_high(n + 2, 1)

            for u in range(NU):
                exp_unit(0, u, 1, None, st_bank[(u + 1) % 2])
                if u == 6:
                    act.wait_ge(lg_done, 1)
                    act.activation(lg[:].rearrange("p n x -> p (n x)"), bank[5][:, 0:NT * NX], ACT.Copy).then_inc(lg_kept, 1)
            for b in range(2):
                attention(b, b, True, True)
            with act.Fori(1, B // 2 - 1) as i:
                for par in range(2):
                    attention(("r", i), par, True, True)
            attention(B - 2, 0, True, False)
            attention(B - 1, 1, False, False)

            def sigmoid_part(t, par):
                n = at(t, par)
                for k in range(2):
                    act.wait_ge(gu_done, 2 * n + k + 1)
                    act.wait_ge(hid_done, n + PRIME_HID)
                    act.activation(sg[:, k, :], g_bank[k][:, 0:F], ACT.Silu).then_inc(sg_done, 1)

            def result(t, par):
                n = at(t, par)
                act.wait_ge(y_done, n + 1)
                if not (isinstance(n, int) and n < 2):
                    act.wait_ge(y_st[par], 16 * 2 * half(t, par, 0))
                act.activation(y_sb[par][:].rearrange("p k e -> p (k e)"), y_bank[:, 0:2 * E], ACT.Copy).then_inc(y_out, 1)

            def expert_step(t, par, has_t, has_next, has_1):
                if has_t:
                    sigmoid_part(t, par)
                if has_next:
                    x_out(*shift(t, par, 1))
                if has_1:
                    result(*shift(t, par, -1))

            expert_step(0, 0, True, True, False)
            expert_step(1, 1, True, True, True)
            with act.Fori(1, NPAIR // 2 - 1) as i:
                for par in range(2):
                    expert_step(("r", i), par, True, True, True)
            for t in range(NPAIR - 2, NPAIR + 1):
                expert_step(t, t % 2, t < NPAIR, t + 1 < NPAIR, True)

            def shared_sigmoid(n, c):
                m = min(P, F - c * P)
                act.wait_ge(sgu_done, FC * n + c + 1)
                if not (isinstance(n, int) and n == 0):
                    act.wait_ge(shid_done, FC * (n - 1) + c + 1)
                act.activation(s_sig[0:m, c, :], bank[2 * c][0:m, :], ACT.Silu).then_inc(ssig_done, 1)

            def hidden_high(n, par, c):
                m = min(P, F - c * P)
                act.wait_ge(shid_done, FC * n + c + 1)
                if c == 0 and not (isinstance(n, int) and n < 2):
                    act.wait_ge(res_done, n - 1)
                act.activation(s_hid_hi[par][0:m, c, :], s_hid[0:m, c, :], ACT.Copy).then_inc(shid_high, 1)

            def shared_step(t, par):
                n = at(t, par)
                shared_sigmoid(n, 0)
                for c in range(1, FC):
                    shared_sigmoid(n, c)
                    hidden_high(n, par, c - 1)
                hidden_high(n, par, FC - 1)
                act.wait_ge(a_ld[par], 16 * (half(t, par, 0) + 1))
                act.activation(a_hi[par][:], a_in[par][:], ACT.Copy).then_inc(a_high, 1)

            def result_out(t, par):
                n = at(t, par)
                act.wait_ge(res_done, n + 1)
                if not (isinstance(n, int) and n == 0):
                    act.wait_ge(o_tr, n)
                act.activation(resT[:], res_bank_of(t)[:], ACT.Identity, bias=bout[:, 0:1]).then_inc(res_out, 1)

            shared_step(0, 0)
            with act.Fori(0, B // 2 - 1) as i:
                for par in range(2):
                    shared_step(*shift(("r", i), par, 1))
                    result_out(("r", i), par)
            shared_step(B - 1, 1)
            result_out(B - 2, 0)
            result_out(B - 1, 1)

        @block.vector
        def _(dve):
            chain = [0]

            def link(ins):
                chain[0] += 1
                ins.then_inc(vec, 1)
                dve.wait_ge(vec, chain[0])

            dve.memset(one_row[:], 1.0).then_inc(ones_set, 1)
            link(dve.memset(columns[:], 0))
            for i, (s_, n_) in enumerate(((av_out, PRIME_AO), (t_done, PRIME_T), (f_done, PRIME_F), (aT_ready, PRIME_ATOUT), (aT_st, 16), (a_done, PRIME_A),
                                            (hid_done, PRIME_HID), (hidT_done, PRIME_HIDT), (y_out, PRIME_Y))):
                dve.memset(primed[:, i:i + 1], 0.0).then_inc(s_, n_)

            QT = NT // 4

            def block_stats(i):
                dve.wait_ge(x_ld[i], 16)
                for n in range(i * QT, (i + 1) * QT):
                    ins = dve.bn_stats(bn[:, n, :], x_all[:, n, :])
                ins.then_inc(stat1, 1)

            def variance(i):
                q = slice(i * QT, (i + 1) * QT)
                dve.wait_ge(stat1, i + 1)
                for n in range(i * QT, (i + 1) * QT):
                    ins = dve.bn_aggr(mv[:, n, :], bn[:, n, :])
                link(ins)
                dve.tensor_scalar(var[:, q], mv[:, q, 1], EPS, None, ALU.add).then_inc(stats, 1)

            def normal_scale(i):
                q = slice(i * QT, (i + 1) * QT)
                dve.wait_ge(std_done, i + 1)
                link(dve.reciprocal(rstd[:, q], std[:, q]))
                link(dve.scalar_tensor_tensor(out=newton[:, q], in0=rstd[:, q], scalar=-0.5, in1=rstd[:, q], op0=ALU.mult, op1=ALU.mult))
                link(dve.tensor_tensor(newton[:, q], newton[:, q], var[:, q], ALU.mult))
                link(dve.scalar_tensor_tensor(out=rstd[:, q], in0=newton[:, q], scalar=1.5, in1=rstd[:, q], op0=ALU.add, op1=ALU.mult))

            def normal_rows(b):
                for n in range(b * NB, (b + 1) * NB):
                    ins = dve.tensor_scalar(xn_rows[:, n, 0:E], x_all[:, n, :], mv[:, n, 0:1], rstd[:, n:n + 1], ALU.subtract, ALU.mult)
                ins.then_inc(xn_done, 1)

            def split_low(n, c):
                hi, lo, wr = ((q_hi, q_lo, q_wr), (k_hi, k_lo, k_wr))[c]
                dve.wait_ge(qk_hi, 2 * n + c + 1)
                if not (isinstance(n, int) and n == 0):
                    dve.wait_ge(wr, 48 * n)
                dve.scalar_tensor_tensor(out=lo[:], in0=qkv_bank(n, c)[:], scalar=bqkv[:, c:c + 1], in1=hi[:].bitcast(F32),
                                         op0=ALU.add, op1=ALU.subtract).then_inc(qk_split, 1)

            def value_bias(n):
                dve.wait_ge(v_proj, n + 1)
                if not (isinstance(n, int) and n == 0):
                    dve.wait_ge(v_tr, n)
                dve.tensor_scalar(vT[:], proj_bank[:], bqkv[:, 2:3], None, ALU.add).then_inc(v_biased, 1)

            def value_rows(n, par):
                dve.wait_ge(v_tr, n + 1)
                if not (isinstance(n, int) and n < 2):
                    dve.wait_ge(av_done[NB - 1], (n - 1) * NG)
                dve.tensor_copy(v32[par][:].rearrange("p n h c -> p (n h) c")[:, :, 0:D],
                                proj_bank[:].rearrange("p (n d) -> p n d", d=D)).then_inc(v_ready, 1)

            dve.wait_ge(w_early, 48)
            block_stats(0)
            variance(0)
            block_stats(1)
            normal_scale(0)
            normal_rows(0)
            normal_rows(1)
            variance(1)
            block_stats(2)
            normal_scale(1)
            normal_rows(2)
            split_low(0, 0)
            normal_rows(3)
            split_low(0, 1)
            variance(2)
            block_stats(3)
            normal_scale(2)
            normal_rows(4)
            normal_rows(5)
            variance(3)
            normal_scale(3)
            normal_rows(6)
            normal_rows(7)
            each = [P, NT, NX]

            def route_exponents():
                dve.wait_ge(lg_kept, 1)
                link(dve.tensor_reduce(pick[:], lg[:], AX.X, ALU.max))
                dve.tensor_tensor(logit[:], lg[:], pick[:, :, None].broadcast_to(each), ALU.subtract).then_inc(z_ready, 1)

            def route_probabilities():
                dve.wait_ge(e_ready, 1)
                link(dve.tensor_reduce(pick[:], prob[:], AX.X, ALU.add))
                link(dve.reciprocal(pick[:], pick[:]))
                link(dve.tensor_tensor(prob[:], prob[:], pick[:, :, None].broadcast_to(each), ALU.mult))

            def route_best(c):
                if c == 1:
                    link(dve.scalar_tensor_tensor(out=prob[:], in0=hot[0][:], scalar=-4.0, in1=prob[:], op0=ALU.mult, op1=ALU.add))
                link(dve.tensor_reduce(best[c][:], prob[:], AX.X, ALU.max))
                link(dve.tensor_tensor(cand[:], prob[:], best[c][:, :, None].broadcast_to(each), ALU.is_equal))

            def route_choice(c):
                dve.wait_ge(consts, 3)
                link(dve.scalar_tensor_tensor(out=cand[:], in0=cand[:], scalar=-float(NX * NX),
                                              in1=expert_no[:, None, :].broadcast_to(each), op0=ALU.mult, op1=ALU.add))
                link(dve.tensor_reduce(pick[:], cand[:], AX.X, ALU.min))
                link(dve.tensor_tensor(hot[c][:], cand[:], pick[:, :, None].broadcast_to(each), ALU.is_equal))

            def route_chosen():
                dve.tensor_tensor(hot_bf[:], hot[0][:], hot[1][:], ALU.add).then_inc(hot_ready, 1)

            def route_weights():
                link(dve.scalar_tensor_tensor(out=pick[:], in0=best[0][:], scalar=1e-20, in1=best[1][:], op0=ALU.add, op1=ALU.add))
                link(dve.reciprocal(pick[:], pick[:]))
                for c in range(2):
                    link(dve.tensor_tensor(topw[:, c, :], best[c][:], pick[:], ALU.mult))

            def route_blocks():
                dve.wait_ge(counts_kept, 1)
                for x in range(NX):
                    ins = dve.tensor_tensor_scan(upto[:, :, x], ones_f[:], counts[:, 1, :, x], 0.0, ALU.mult, ALU.add)
                link(ins)

            def route_rows():
                link(dve.tensor_scalar(rows_i[:], upto[:, NT - 1, :], float(P - 1), None, ALU.add))
                link(dve.tensor_scalar(rows_i[:], rows_i[:], -P, None, ALU.bitwise_and))
                link(dve.tensor_copy(rows_f[:], rows_i[:]))
                link(dve.tensor_tensor_scan(end_row[:], ones_f[:, 0:NX], rows_f[:], 0.0, ALU.mult, ALU.add))
                dve.tensor_tensor(base_row[:], end_row[:], rows_f[:], ALU.subtract).then_inc(base_ready, 1)

            def route_tiles():
                tiles = [1, NTILE, NX]
                link(dve.tensor_tensor(past[:], end_row[0:1, None, :].broadcast_to(tiles), tile_start[:, :, None].broadcast_to(tiles), ALU.is_le))
                link(dve.tensor_reduce(tile_f[:], past[:], AX.X, ALU.add))
                pairs = tile_f[:].rearrange("o (p k) -> o p k", k=2)
                dve.tensor_scalar(columns[:, 0:NPAIR, 0:2], pairs, float(NX - 1), float(2 * F), ALU.min, ALU.mult).then_inc(columns_set, 1)
                dve.tensor_scalar(columns[:, 2:NPAIR + 2, 2:4], pairs, float(NX - 1), float(FC * E), ALU.min, ALU.mult).then_inc(columns_set, 1)

            def reduce_unit(g, u, src, groups):
                qb, heads = MX_QB[u], MX_HEADS[u]
                w, nh = (qb + 1) * P, len(heads)
                dve.wait_ge(mx_done[u], groups)
                dve.tensor_reduce(neg_max[:, g, heads[0]:heads[0] + nh, qb],
                                  src[:, 0:nh * w].rearrange("p (h w) -> p h w", h=nh), AX.X, ALU.max,
                                  negate=True).then_inc(red_done[u], 1)

            def max_rows(n, g):
                dve.wait_ge(m_tr, n * NG + g + 1)
                if not (isinstance(n, int) and n == 0):
                    dve.wait_ge(m_ld[g], 16 * n)
                dve.tensor_copy(m_row[g][:], row_bank[0:HG * NB, 0:P]).then_inc(m_ready, 1)

            def normalise(n, g):
                dve.wait_ge(t_done, n * NG + g + 1 + PRIME_T)
                o = row_bank[:].rearrange("p (n c) -> p n c", c=32)
                dve.reciprocal(inv_sum[:], o[:, :, D]).then_inc(inv_done, 1)
                dve.wait_ge(inv_done, n * NG + g + 1)
                if g == 0:
                    dve.wait_ge(f_done, n + PRIME_F)
                dve.tensor_tensor(a_tok[:, :, g * HG * D:(g + 1) * HG * D].rearrange("p n (h d) -> p n h d", d=D),
                                  row_bank[:].rearrange("p (n h c) -> p n h c", h=HG, c=32)[:, :, :, 0:D],
                                  inv_sum[:].rearrange("p (n h) -> p n h", h=HG)[:, :, :, None].broadcast_to([P, NB, HG, D]),
                                  ALU.mult).then_inc(a_done, 1)

            for u in range(UB):
                reduce_unit(u // NU, u % NU, first_mx_bank[u % 3], u // NU + 1)
                if u == NU - 1:
                    max_rows(0, 0)
                if u == AHEAD - 1:
                    split_low(1, 0)
                if u == AHEAD + 2:
                    split_low(1, 1)
                if u == AHEAD + 12:
                    max_rows(0, 1)
                    value_bias(0)
                if u == AHEAD + 18:
                    value_rows(0, 0)
            max_rows(0, 2)

            def x_low(t, par):
                n = at(t, par)
                dve.wait_ge(xgT_done, n + 1)
                dve.tensor_tensor(xgT_lo[par][:].rearrange("p k m -> p (k m)"), bank[4][:, 0:PR],
                                  xgT_hi[par][:].bitcast(F32).rearrange("p k m -> p (k m)"), ALU.subtract).then_inc(xg_split, 1)

            def result_rows(t, par):
                n = at(t, par)
                dve.wait_ge(xg_ld[par], 16 * (half(t, par, 0) + 1))
                dve.tensor_tensor(y_rows[:, bass.ds(n, 1), :].rearrange("p o k -> p (o k)"), xg[par][:, :, E], nowhere[:, par], ALU.max).then_inc(y_rows_kept, 1)

            def split_weights(x):
                if x % (NX // 2) == 0:
                    dve.wait_ge(egu_ld[x // (NX // 2)], 16)
                dve.tensor_copy(egu_hi[:, x], egu_lo[:, x].bitcast(F32)).then_inc(egu_high, 1)
                dve.wait_ge(egu_high, x + 1)
                dve.tensor_tensor(egu_lo[:, x], egu_lo[:, x].bitcast(F32), egu_hi[:, x].bitcast(F32), ALU.subtract).then_inc(egu_split, 1)

            def attention(b, par, more, more2):
                n = at(b, par)
                for k in range(NG):
                    with_max = held(dve, (n + 1) * NG + k + 1)
                    for u in range(NU):
                        s = k * NU + u
                        if more:
                            reduce_unit(k, u, mx_bank[s % 2], with_max)
                        if u == 4 and k == 0:
                            max_rows(n, NG - 1)
                        if u == 4 and k and more:
                            max_rows(n + 1, k - 1)
                        if u == 0 and not more and k == NG - 1:
                            x_low(0, 0)
                            result_rows(0, 0)
                        if u == 7:
                            normalise(n, k)
                        if u == 7 and not more and k < NG - 1:
                            for x in range(3 * k, min(3 * k + 3, NX)):
                                split_weights(x)
                        if isinstance(n, int) and n == 0:
                            if s == 2:
                                route_exponents()
                            if s == 10:
                                route_probabilities()
                            if s in (12, 20):
                                route_best(s // 20)
                            if s in (17, 23):
                                route_choice(s // 20)
                            if s == 27:
                                route_chosen()
                            if s == 31:
                                route_weights()
                        if isinstance(n, int) and n == 1:
                            if s == 2:
                                route_blocks()
                            if s == 10:
                                route_rows()
                            if s == 17:
                                route_tiles()
                        if more and s == 5:
                            value_bias(n + 1)
                        if more and s == 9:
                            value_rows(n + 1, 1 - par)
                        if more2 and s == 15:
                            split_low(n + 2, 0)
                        if more2 and s == 21:
                            split_low(n + 2, 1)
                        if u == 10 and k == NG - 1:
                            dve.wait_ge(f_done, n + 1 + PRIME_F)
                            dve.wait_ge(aT_st, 16 * (n + 1))
                            dve.tensor_copy(a_T[:], row_bank[:]).then_inc(aT_ready, 1)

            for b in range(2):
                attention(b, b, True, True)
            with dve.Fori(1, B // 2 - 1) as i:
                for par in range(2):
                    attention(("r", i), par, True, True)
            attention(B - 2, 0, True, False)
            attention(B - 1, 1, False, False)

            u_bank, hidT_bank = bank[2:4], bank[5:7]

            def hidden(t, par):
                n = at(t, par)
                if not (isinstance(n, int) and n < 1):
                    dve.wait_ge(hid_tr, n)
                for k in range(2):
                    dve.wait_ge(sg_done, 2 * n + k + 1)
                    ins = dve.tensor_tensor(hid[:, k, :], sg[:, k, :], u_bank[k][:, 0:F], ALU.mult)
                ins.then_inc(hid_done, 1)

            def hiddenT_out(t, par):
                n = at(t, par)
                dve.wait_ge(hid_tr, n + 1)
                if not (isinstance(n, int) and n < 2):
                    dve.wait_ge(y_done, n - 1)
                dve.tensor_copy(hidT[par][:, 0:2].rearrange("p c k m -> p (c k m)"), hidT_bank[0][:])
                dve.tensor_copy(hidT[par][0:FR, 2].rearrange("p k m -> p (k m)"), hidT_bank[1][0:FR, 0:PR]).then_inc(hidT_done, 1)

            def expert_step(t, par, has_next):
                hidden(t, par)
                if has_next:
                    x_low(*shift(t, par, 1))
                hiddenT_out(t, par)
                if has_next:
                    result_rows(*shift(t, par, 1))

            for t in range(2):
                expert_step(t, t, True)
            with dve.Fori(1, NPAIR // 2 - 1) as i:
                for par in range(2):
                    expert_step(("r", i), par, True)
            for t in range(NPAIR - 2, NPAIR):
                expert_step(t, t % 2, t + 1 < NPAIR)

            def shared_hidden(t, par):
                n = at(t, par)
                for c in range(FC):
                    m = min(P, F - c * P)
                    dve.wait_ge(ssig_done, FC * n + c + 1)
                    if not (isinstance(n, int) and n == 0):
                        dve.wait_ge(shid_split, FC * (n - 1) + c + 1)
                    dve.tensor_tensor(s_hid[0:m, c, :], s_sig[0:m, c, :], bank[2 * c + 1][0:m, :], ALU.mult).then_inc(shid_done, 1)

            def add_choices(t, par):
                n = at(t, par)
                dve.wait_ge(r_ld[par], 16 * (half(t, par, 0) + 1))
                dve.wait_ge(got[par], 16 * 2 * (half(t, par, 0) + 1))
                if not (isinstance(n, int) and n in (0, 1, B - 1)):
                    dve.wait_ge(o_st[par], 16 * half(t, par, 0))
                for c in range(2):
                    if c == 1:
                        dve.wait_ge(o_half, 2 * n + 1)
                    for k in range(NB):
                        o, x = sums_of(t, par)[:, k, :], x_in[par][:, k, :]
                        ins = dve.scalar_tensor_tensor(out=o, in0=picked[par][:, c, k, :], scalar=topw[:, c, bass.ds(n * NB + k, 1)],
                                                       in1=o if c else x, op0=ALU.mult, op1=ALU.add)
                    ins.then_inc(o_half, 1)

            def add_rest(t, par):
                n = at(t, par)
                dve.wait_ge(o_half, 2 * n + 2)
                dve.wait_ge(o_tr, n + 1)
                dve.tensor_tensor(sums_of(t, par)[:], sums_of(t, par)[:], bank[7][:].rearrange("p (n e) -> p n e", e=E), ALU.add).then_inc(o_sum, 1)

            shared_hidden(0, 0)
            shared_hidden(1, 1)
            add_choices(0, 0)
            with dve.Fori(1, B // 2) as i:
                for par in range(2):
                    shared_hidden(("r", i), par)
                    add_choices(*shift(("r", i), par, -1))
                    add_rest(*shift(("r", i), par, -2))
            add_choices(B - 1, 1)
            add_rest(B - 2, 0)
            add_rest(B - 1, 1)


_OUTS = [((B, S, E), "float32")]


def kernel(L0_attn_x, L0_attn_W1, L0_attn_b1, L0_attn_Wp, L0_attn_bp, L0_ffn_gate_w, L0_ffn_expert_gate,
           L0_ffn_expert_up, L0_ffn_expert_down, L0_ffn_shared_gate, L0_ffn_shared_up, L0_ffn_shared_down):
    import numpy as np
    import concourse.bacc as bacc
    from concourse.bass_utils import run_bass_kernel_spmd

    w1 = np.asarray(L0_attn_W1).reshape(E, H, 3, D).transpose(0, 2, 1, 3).reshape(E, 3, E)
    b1 = np.asarray(L0_attn_b1).reshape(H, 3, D).transpose(0, 2, 1).reshape(E, 3)
    e_gu = np.stack([np.asarray(L0_ffn_expert_gate), np.asarray(L0_ffn_expert_up)], axis=1).transpose(3, 0, 1, 2)
    s_gu = np.stack([np.asarray(L0_ffn_shared_gate), np.asarray(L0_ffn_shared_up)], axis=0).transpose(2, 0, 1)
    laid_out = {
        "x": np.asarray(L0_attn_x), "w_qkv": w1, "b_qkv": b1, "w_out": np.asarray(L0_attn_Wp),
        "b_out": np.asarray(L0_attn_bp).reshape(E, 1), "gate_w": np.asarray(L0_ffn_gate_w).transpose(1, 0),
        "e_gu": e_gu, "e_down": np.asarray(L0_ffn_expert_down).transpose(0, 2, 1),
        "s_gu": s_gu, "s_down": np.asarray(L0_ffn_shared_down).transpose(1, 0),
    }
    nc = bacc.Bacc("TRN2", target_bir_lowering=False, num_devices=1)
    arrays, args = {}, {}
    for name, a in laid_out.items():
        a = np.ascontiguousarray(a)
        arrays[f"in_{name}"] = a
        args[name] = nc.dram_tensor(f"in_{name}", a.shape, mybir.dt.from_np(a.dtype), kind="ExternalInput").ap()
    (shape, dtype), = _OUTS
    out = nc.dram_tensor("out_0", shape, mybir.dt.from_np(np.dtype(dtype)), kind="ExternalOutput").ap()
    nc.disable_value_cache = True
    attention_moe_kernel(nc, **args, out=out)
    return run_bass_kernel_spmd(nc, [arrays], core_ids=[0]).results[0]["out_0"]
```
